# Optimizing a Trainium2 kernel written in Bass

```python
import numpy as np
import jax
import jax.numpy as jnp

def _softmax(x, axis=-1):
    return jax.nn.softmax(x, axis=axis)

def _gelu(x):
    return jax.nn.gelu(x, approximate=True)

def _silu(x):
    return jax.nn.silu(x)

def _sigmoid(x):
    return jax.nn.sigmoid(x)

def _layernorm(x, axis=-1, eps=1e-05):
    m = jnp.mean(x, axis=axis, keepdims=True)
    v = jnp.var(x, axis=axis, keepdims=True)
    return (x - m) / jnp.sqrt(v + eps)

def _scatter_add(tgt, idx, src, axis=0):
    return tgt.at[idx].add(src)

def _segment_sum(src, seg, n):
    return jax.ops.segment_sum(src, seg, n)
kernel_name = 'mk_xattn_ffn_d2_seqx_r4_d5cd06'

def setup_inputs(seed: int=0):
    np.random.seed(seed)
    _w = jnp.asarray

    def _rec_inputs():
        import jax
        import jax.numpy as jnp
        _rk = jax.random.key(seed)
        x = 7.22e-05 + 1 * jax.random.normal(jax.random.fold_in(_rk, 1), (2, 1024, 256), jnp.float32)
        _lenS = 1024 - jax.random.randint(jax.random.fold_in(_rk, 7), (2,), 0, max(1, 1024 // 4) + 1, jnp.int32)
        _lenS2 = 77 - jax.random.randint(jax.random.fold_in(_rk, 8), (2,), 0, max(1, 77 // 4) + 1, jnp.int32)
        _ctx_768P = jax.random.normal(jax.random.fold_in(_rk, 11), (2, 16, 192), jnp.float32)
        _ctx_768c = jax.random.dirichlet(jax.random.fold_in(_rk, 511), 0.3 * jnp.ones((16,), jnp.float32), (2, 77))
        _ctx_768t = jnp.einsum('bsk,bkd->bsd', _ctx_768c, _ctx_768P)
        _ctx_768t = _ctx_768t * jax.lax.rsqrt(jnp.mean(jnp.square(_ctx_768t)) + 1e-12) * 0.953939
        ctx_768 = -0.000191848 + 0.999787 * (_ctx_768t + 0.3 * jax.random.normal(jax.random.fold_in(_rk, 611), (2, 77, 192), jnp.float32))
        return (x, ctx_768)
    x, ctx_768 = _rec_inputs()

    def _L0_xattn_setup():
        import jax, jax.numpy as jnp
        import numpy as np
        HEADS = 8
        DIM_HEAD = 64
        SCALE = DIM_HEAD ** (-0.5)
        key = jax.random.key(seed)
        ks = jax.random.split(key, 7)
        B, Nq, Nc = (4, 512, 512)
        Dq, Dc = (256, 192)
        inner = HEADS * DIM_HEAD
        x = jax.random.normal(ks[0], (B, Nq, Dq), dtype=jnp.float32)
        context = jax.random.normal(ks[1], (B, Nc, Dc), dtype=jnp.float32)
        Wq = jax.random.normal(ks[2], (Dq, inner), dtype=jnp.float32) * Dq ** (-0.5)
        Wk = jax.random.normal(ks[3], (Dc, inner), dtype=jnp.float32) * Dc ** (-0.5)
        Wv = jax.random.normal(ks[4], (Dc, inner), dtype=jnp.float32) * Dc ** (-0.5)
        Wo = jax.random.normal(ks[5], (inner, Dq), dtype=jnp.float32) * inner ** (-0.5)
        bo = jax.random.normal(ks[6], (Dq,), dtype=jnp.float32) * 0.01
        return {'x': x, 'context': context, 'Wq': Wq, 'Wk': Wk, 'Wv': Wv, 'Wo': Wo, 'bo': bo}
    _L0_xattn_all = _L0_xattn_setup()
    _L0_xattn_in = {k: v for k, v in _L0_xattn_all.items() if k in ('Wq', 'Wk', 'Wv', 'Wo', 'bo')}
    del _L0_xattn_all

    def _L0_ffn_setup():
        import jax, jax.numpy as jnp
        import numpy as np
        import math
        D = 256
        H = 16
        E = 8
        TOPK = 2
        LAT = D // 2
        KPH = LAT // H
        HD = D // H

        def _forward(hs, q_w, q_b, k_w, k_b, v_w, v_b, o_w, o_b, router_w, router_b, w1, b1, w2, b2):
            B, S, _ = hs.shape
            Q = (hs @ q_w + q_b).reshape(B, S, H, HD).transpose(0, 2, 1, 3)
            K = (hs @ k_w + k_b).reshape(B, S, H, KPH).transpose(0, 2, 1, 3)
            V = (hs @ v_w + v_b).reshape(B, S, H, KPH).transpose(0, 2, 1, 3)
            scores = jnp.einsum('bhsk,bhtk->bhst', Q[..., :KPH], K) / math.sqrt(KPH)
            attn = jax.nn.softmax(scores, axis=-1)
            ao = jnp.einsum('bhst,bhtv->bhsv', attn, V)
            ao = ao.transpose(0, 2, 1, 3).reshape(B, S, H * KPH)
            ao = jnp.concatenate([ao, jnp.zeros((B, S, D - LAT), ao.dtype)], axis=-1)
            mla_out = ao @ o_w + o_b
            probs = jax.nn.softmax(mla_out @ router_w + router_b, axis=-1)
            topw, topi = jax.lax.top_k(probs, TOPK)
            topw = topw / (topw.sum(-1, keepdims=True) + 1e-08)
            combine = jnp.sum(jax.nn.one_hot(topi, E, dtype=probs.dtype) * topw[..., None], axis=-2)
            h1 = jnp.einsum('bsd,edf->ebsf', mla_out, w1) + b1[:, None, None, :]
            h1 = jax.nn.gelu(h1, approximate=False)
            h2 = jnp.einsum('ebsf,efd->ebsd', h1, w2) + b2[:, None, None, :]
            moe_out = jnp.einsum('bse,ebsd->bsd', combine, h2)
            return hs + 0.3 * moe_out
        key = jax.random.key(seed)
        ks = jax.random.split(key, 16)
        s = 0.02
        inp = {'hidden_states': jax.random.normal(ks[0], (2, 512, D), jnp.float32), 'q_w': jax.random.normal(ks[1], (D, D), jnp.float32) * s, 'q_b': jnp.zeros((D,), jnp.float32), 'k_w': jax.random.normal(ks[2], (D, LAT), jnp.float32) * s, 'k_b': jnp.zeros((LAT,), jnp.float32), 'v_w': jax.random.normal(ks[3], (D, LAT), jnp.float32) * s, 'v_b': jnp.zeros((LAT,), jnp.float32), 'o_w': jax.random.normal(ks[4], (D, D), jnp.float32) * s, 'o_b': jnp.zeros((D,), jnp.float32), 'router_w': jax.random.normal(ks[5], (D, E), jnp.float32) * s, 'router_b': jnp.zeros((E,), jnp.float32), 'w1': jax.random.normal(ks[6], (E, D, 2 * D), jnp.float32) * s, 'b1': jnp.zeros((E, 2 * D), jnp.float32), 'w2': jax.random.normal(ks[7], (E, 2 * D, D), jnp.float32) * s, 'b2': jnp.zeros((E, D), jnp.float32)}
        return inp
    _L0_ffn_all = _L0_ffn_setup()
    _L0_ffn_in = {k: v for k, v in _L0_ffn_all.items() if k in ('q_w', 'q_b', 'k_w', 'k_b', 'v_w', 'v_b', 'o_w', 'o_b', 'router_w', 'router_b', 'w1', 'b1', 'w2', 'b2')}
    del _L0_ffn_all

    def _L1_xattn_setup():
        import jax, jax.numpy as jnp
        import numpy as np
        N_HEADS = 16
        key = jax.random.key(seed)
        ks = jax.random.split(key, 8)
        b, l, m = (8, 256, 256)
        d_embed, d_cross = (256, 192)
        s_q = 1.0 / np.sqrt(d_embed)
        s_kv = 1.0 / np.sqrt(d_cross)
        return {'x': jax.random.normal(ks[0], (b, l, d_embed), jnp.float32), 'y': jax.random.normal(ks[1], (b, m, d_cross), jnp.float32), 'Wq': jax.random.normal(ks[2], (d_embed, d_embed), jnp.float32) * s_q, 'bq': jax.random.normal(ks[3], (d_embed,), jnp.float32) * 0.01, 'Wkv': jax.random.normal(ks[4], (2 * d_embed, d_cross), jnp.float32) * s_kv, 'bkv': jax.random.normal(ks[5], (2 * d_embed,), jnp.float32) * 0.01, 'Wo': jax.random.normal(ks[6], (d_embed, d_embed), jnp.float32) * s_q, 'bo': jax.random.normal(ks[7], (d_embed,), jnp.float32) * 0.01}
    _L1_xattn_all = _L1_xattn_setup()
    _L1_xattn_in = {k: v for k, v in _L1_xattn_all.items() if k in ('Wq', 'bq', 'Wkv', 'bkv', 'Wo', 'bo')}
    del _L1_xattn_all

    def _L1_ffn_setup():
        import jax, jax.numpy as jnp
        import numpy as np
        LN_EPS = 1e-05

        def layernorm(x, g, b):
            mu = jnp.mean(x, axis=-1, keepdims=True)
            var = jnp.mean((x - mu) ** 2, axis=-1, keepdims=True)
            return (x - mu) * jax.lax.rsqrt(var + LN_EPS) * g + b

        def act_quant_fake(x):
            scale = 127.0 / jnp.clip(jnp.max(jnp.abs(x), axis=-1, keepdims=True), 1e-05)
            return jnp.clip(jnp.round(x * scale), -128.0, 127.0) / scale

        def weight_quant_fake(w):
            scale = 1.0 / jnp.clip(jnp.mean(jnp.abs(w)), 1e-05)
            return jnp.clip(jnp.round(w * scale), -1.0, 1.0) / scale

        def bitlinear(x, w, b):
            dqx = act_quant_fake(x)
            dqw = weight_quant_fake(w)
            return jnp.einsum('btd,hd->bth', dqx, dqw) + b
        key = jax.random.key(seed)
        ks = jax.random.split(key, 5)
        B, T, D, H = (8, 1024, 256, 1024)
        return {'x': jax.random.normal(ks[0], (B, T, D), dtype=jnp.float32), 'ln1_g': jnp.ones((D,), jnp.float32), 'ln1_b': jnp.zeros((D,), jnp.float32), 'w1': jax.random.normal(ks[1], (H, D), dtype=jnp.float32) * (1.0 / np.sqrt(D)), 'b1': jax.random.normal(ks[2], (H,), dtype=jnp.float32) * 0.02, 'ln2_g': jnp.ones((H,), jnp.float32), 'ln2_b': jnp.zeros((H,), jnp.float32), 'w2': jax.random.normal(ks[3], (D, H), dtype=jnp.float32) * (1.0 / np.sqrt(H)), 'b2': jax.random.normal(ks[4], (D,), jnp.float32) * 0.02}
    _L1_ffn_all = _L1_ffn_setup()
    _L1_ffn_in = {k: v for k, v in _L1_ffn_all.items() if k in ('ln1_g', 'ln1_b', 'w1', 'b1', 'ln2_g', 'ln2_b', 'w2', 'b2')}
    del _L1_ffn_all
    return {'x': x, 'ctx_768': ctx_768, 'L0_xattn_Wq': _L0_xattn_in['Wq'], 'L0_xattn_Wk': _L0_xattn_in['Wk'], 'L0_xattn_Wv': _L0_xattn_in['Wv'], 'L0_xattn_Wo': _L0_xattn_in['Wo'], 'L0_xattn_bo': _L0_xattn_in['bo'], 'L0_ffn_q_w': _L0_ffn_in['q_w'], 'L0_ffn_q_b': _L0_ffn_in['q_b'], 'L0_ffn_k_w': _L0_ffn_in['k_w'], 'L0_ffn_k_b': _L0_ffn_in['k_b'], 'L0_ffn_v_w': _L0_ffn_in['v_w'], 'L0_ffn_v_b': _L0_ffn_in['v_b'], 'L0_ffn_o_w': _L0_ffn_in['o_w'], 'L0_ffn_o_b': _L0_ffn_in['o_b'], 'L0_ffn_router_w': _L0_ffn_in['router_w'], 'L0_ffn_router_b': _L0_ffn_in['router_b'], 'L0_ffn_w1': _L0_ffn_in['w1'], 'L0_ffn_b1': _L0_ffn_in['b1'], 'L0_ffn_w2': _L0_ffn_in['w2'], 'L0_ffn_b2': _L0_ffn_in['b2'], 'L1_xattn_Wq': _L1_xattn_in['Wq'], 'L1_xattn_bq': _L1_xattn_in['bq'], 'L1_xattn_Wkv': _L1_xattn_in['Wkv'], 'L1_xattn_bkv': _L1_xattn_in['bkv'], 'L1_xattn_Wo': _L1_xattn_in['Wo'], 'L1_xattn_bo': _L1_xattn_in['bo'], 'L1_ffn_ln1_g': _L1_ffn_in['ln1_g'], 'L1_ffn_ln1_b': _L1_ffn_in['ln1_b'], 'L1_ffn_w1': _L1_ffn_in['w1'], 'L1_ffn_b1': _L1_ffn_in['b1'], 'L1_ffn_ln2_g': _L1_ffn_in['ln2_g'], 'L1_ffn_ln2_b': _L1_ffn_in['ln2_b'], 'L1_ffn_w2': _L1_ffn_in['w2'], 'L1_ffn_b2': _L1_ffn_in['b2']}

def reference(x, ctx_768, L0_xattn_Wq, L0_xattn_Wk, L0_xattn_Wv, L0_xattn_Wo, L0_xattn_bo, L0_ffn_q_w, L0_ffn_q_b, L0_ffn_k_w, L0_ffn_k_b, L0_ffn_v_w, L0_ffn_v_b, L0_ffn_o_w, L0_ffn_o_b, L0_ffn_router_w, L0_ffn_router_b, L0_ffn_w1, L0_ffn_b1, L0_ffn_w2, L0_ffn_b2, L1_xattn_Wq, L1_xattn_bq, L1_xattn_Wkv, L1_xattn_bkv, L1_xattn_Wo, L1_xattn_bo, L1_ffn_ln1_g, L1_ffn_ln1_b, L1_ffn_w1, L1_ffn_b1, L1_ffn_ln2_g, L1_ffn_ln2_b, L1_ffn_w2, L1_ffn_b2):
    import jax
    import jax.numpy as jnp

    def _L0_xattn_ref(x, context, Wq, Wk, Wv, Wo, bo):
        import jax, jax.numpy as jnp
        import numpy as np
        HEADS = 8
        DIM_HEAD = 64
        SCALE = DIM_HEAD ** (-0.5)
        B, Nq, _ = x.shape
        q = (x @ Wq).reshape(B, Nq, HEADS, DIM_HEAD)
        k = (context @ Wk).reshape(B, context.shape[1], HEADS, DIM_HEAD)
        v = (context @ Wv).reshape(B, context.shape[1], HEADS, DIM_HEAD)
        sim = jnp.einsum('bihd,bjhd->bhij', q, k) * SCALE
        attn = jax.nn.softmax(sim, axis=-1)
        out = jnp.einsum('bhij,bjhd->bihd', attn, v)
        out = out.reshape(B, Nq, HEADS * DIM_HEAD)
        return out @ Wo + bo

    def _L0_ffn_ref(hidden_states, q_w, q_b, k_w, k_b, v_w, v_b, o_w, o_b, router_w, router_b, w1, b1, w2, b2):
        import jax, jax.numpy as jnp
        import numpy as np
        import math
        D = 256
        H = 16
        E = 8
        TOPK = 2
        LAT = D // 2
        KPH = LAT // H
        HD = D // H

        def _forward(hs, q_w, q_b, k_w, k_b, v_w, v_b, o_w, o_b, router_w, router_b, w1, b1, w2, b2):
            B, S, _ = hs.shape
            Q = (hs @ q_w + q_b).reshape(B, S, H, HD).transpose(0, 2, 1, 3)
            K = (hs @ k_w + k_b).reshape(B, S, H, KPH).transpose(0, 2, 1, 3)
            V = (hs @ v_w + v_b).reshape(B, S, H, KPH).transpose(0, 2, 1, 3)
            scores = jnp.einsum('bhsk,bhtk->bhst', Q[..., :KPH], K) / math.sqrt(KPH)
            attn = jax.nn.softmax(scores, axis=-1)
            ao = jnp.einsum('bhst,bhtv->bhsv', attn, V)
            ao = ao.transpose(0, 2, 1, 3).reshape(B, S, H * KPH)
            ao = jnp.concatenate([ao, jnp.zeros((B, S, D - LAT), ao.dtype)], axis=-1)
            mla_out = ao @ o_w + o_b
            probs = jax.nn.softmax(mla_out @ router_w + router_b, axis=-1)
            topw, topi = jax.lax.top_k(probs, TOPK)
            topw = topw / (topw.sum(-1, keepdims=True) + 1e-08)
            combine = jnp.sum(jax.nn.one_hot(topi, E, dtype=probs.dtype) * topw[..., None], axis=-2)
            h1 = jnp.einsum('bsd,edf->ebsf', mla_out, w1) + b1[:, None, None, :]
            h1 = jax.nn.gelu(h1, approximate=False)
            h2 = jnp.einsum('ebsf,efd->ebsd', h1, w2) + b2[:, None, None, :]
            moe_out = jnp.einsum('bse,ebsd->bsd', combine, h2)
            return hs + 0.3 * moe_out
        return _forward(hidden_states, q_w, q_b, k_w, k_b, v_w, v_b, o_w, o_b, router_w, router_b, w1, b1, w2, b2)

    def _L1_xattn_ref(x, y, Wq, bq, Wkv, bkv, Wo, bo):
        import jax, jax.numpy as jnp
        import numpy as np
        N_HEADS = 16
        b, l, d = x.shape
        m = y.shape[1]
        h = N_HEADS
        dh = d // h
        q = (jnp.einsum('bld,ed->ble', x, Wq) + bq).reshape(b, l, h, dh)
        kv = (jnp.einsum('bmc,ec->bme', y, Wkv) + bkv).reshape(b, m, h, 2 * dh)
        k, v = (kv[..., :dh], kv[..., dh:])
        scale = 1.0 / jnp.sqrt(jnp.asarray(dh, x.dtype))
        att = jax.nn.softmax(jnp.einsum('blhd,bmhd->blmh', q, k) * scale, axis=2)
        out = jnp.einsum('blmh,bmhd->blhd', att, v).reshape(b, l, d)
        return jnp.einsum('bld,ed->ble', out, Wo) + bo

    def _L1_ffn_ref(x, ln1_g, ln1_b, w1, b1, ln2_g, ln2_b, w2, b2):
        import jax, jax.numpy as jnp
        import numpy as np
        LN_EPS = 1e-05

        def layernorm(x, g, b):
            mu = jnp.mean(x, axis=-1, keepdims=True)
            var = jnp.mean((x - mu) ** 2, axis=-1, keepdims=True)
            return (x - mu) * jax.lax.rsqrt(var + LN_EPS) * g + b

        def act_quant_fake(x):
            scale = 127.0 / jnp.clip(jnp.max(jnp.abs(x), axis=-1, keepdims=True), 1e-05)
            return jnp.clip(jnp.round(x * scale), -128.0, 127.0) / scale

        def weight_quant_fake(w):
            scale = 1.0 / jnp.clip(jnp.mean(jnp.abs(w)), 1e-05)
            return jnp.clip(jnp.round(w * scale), -1.0, 1.0) / scale

        def bitlinear(x, w, b):
            dqx = act_quant_fake(x)
            dqw = weight_quant_fake(w)
            return jnp.einsum('btd,hd->bth', dqx, dqw) + b
        h = layernorm(x, ln1_g, ln1_b)
        h = bitlinear(h, w1, b1)
        h = jax.nn.gelu(h, approximate=False)
        h = layernorm(h, ln2_g, ln2_b)
        h = bitlinear(h, w2, b2)
        return h
    x = x + _L0_xattn_ref(_layernorm(x, axis=-1), ctx_768, L0_xattn_Wq, L0_xattn_Wk, L0_xattn_Wv, L0_xattn_Wo, L0_xattn_bo)
    x = x + _L0_ffn_ref(_layernorm(x, axis=-1), L0_ffn_q_w, L0_ffn_q_b, L0_ffn_k_w, L0_ffn_k_b, L0_ffn_v_w, L0_ffn_v_b, L0_ffn_o_w, L0_ffn_o_b, L0_ffn_router_w, L0_ffn_router_b, L0_ffn_w1, L0_ffn_b1, L0_ffn_w2, L0_ffn_b2)
    x = x + _L1_xattn_ref(_layernorm(x, axis=-1), ctx_768, L1_xattn_Wq, L1_xattn_bq, L1_xattn_Wkv, L1_xattn_bkv, L1_xattn_Wo, L1_xattn_bo)
    x = x + _L1_ffn_ref(_layernorm(x, axis=-1), L1_ffn_ln1_g, L1_ffn_ln1_b, L1_ffn_w1, L1_ffn_b1, L1_ffn_ln2_g, L1_ffn_ln2_b, L1_ffn_w2, L1_ffn_b2)
    return x

_drawn_inputs = setup_inputs


def setup_inputs(seed=0):
    import zlib

    import numpy as np

    out = dict(_drawn_inputs(seed))
    spreads = {'L0_ffn_q_b': (0.0, 0.8),
     'L0_ffn_k_b': (0.0, 2.0),
     'L0_ffn_v_b': (0.0, 0.8),
     'L0_ffn_o_b': (0.0, 0.635),
     'L0_ffn_router_b': (0.0, 0.603),
     'L0_ffn_b1': (0.0, 0.8),
     'L0_ffn_b2': (0.0, 2.0),
     'L1_ffn_ln1_g': (1.0, 0.6),
     'L1_ffn_ln1_b': (0.0, 0.881),
     'L1_ffn_ln2_g': (1.0, 0.6),
     'L1_ffn_ln2_b': (0.0, 0.8)}
    factors = {'L0_xattn_bo': 5.235,
     'L0_ffn_q_w': 8.0,
     'L0_ffn_k_w': 8.0,
     'L0_ffn_v_w': 8.0,
     'L0_ffn_o_w': 8.0,
     'L0_ffn_router_w': 6.281,
     'L0_ffn_w1': 8.0,
     'L0_ffn_w2': 8.0,
     'L1_xattn_bq': 177.049,
     'L1_xattn_bkv': 42.559,
     'L1_xattn_bo': 39.521,
     'L1_ffn_b1': 18.901,
     'L1_ffn_b2': 20.938}
    for name, (base, spread) in spreads.items():
        noise = np.random.default_rng([zlib.crc32(name.encode()), seed]).standard_normal(out[name].shape)
        drawn = base * np.exp(spread * noise) if base else spread * noise
        out[name] = jnp.asarray(drawn.astype(out[name].dtype))
    for name, factor in factors.items():
        out[name] = (out[name] * factor).astype(out[name].dtype)
    return out
```

```python
from contextlib import ExitStack

import concourse.bass as bass
from concourse import mybir

F32 = mybir.dt.float32
F32R = mybir.dt.float32r
BF16 = mybir.dt.bfloat16
U32 = mybir.dt.uint32
ALU = mybir.AluOpType
ACT = mybir.ActivationFunctionType
AX = mybir.AxisListType

P = 128
BATCH, SEQ, DIM = 2, 1024, 256
TILES = BATCH * SEQ // P
PAIRS = TILES // 2
TILES_PER_BATCH = SEQ // P
KD = DIM // P
CTX, CDIM = 77, 192
C2 = CDIM - P
EPS = 1e-5

GH = 8
HJ = GH * CTX
HALF = HJ // 2
HJT = (HJ + P - 1) // P
HJR = HJ - (HJT - 1) * P


class Scope:

    def __init__(self, nc, ctx, tag):
        self.nc, self.ctx, self.tag, self.sems = nc, ctx, tag, []
        ctx.callback(self.clear)

    def sb(self, name, shape, dt=F32):
        return self.ctx.enter_context(self.nc.sbuf_tensor(f"{self.tag}_{name}", shape, dt))

    def ps(self, name, shape, dt=F32):
        return self.ctx.enter_context(self.nc.psum_tensor(f"{self.tag}_{name}", shape, dt))

    def sem(self, name):
        self.sems.append(self.nc.alloc_semaphore(f"{self.tag}_{name}"))
        return self.sems[-1]

    def clear(self):
        self.nc.clear_and_free_semaphores(self.sems)
        self.nc.all_engine_barrier()


LEAD = 2


def has(t):
    return t + 1 + LEAD


def two_ago(t):
    return t - 1 + LEAD


def one_ago(t):
    return t + LEAD


def live(t):
    return not isinstance(t, int) or 0 <= t < TILES


def tile_of(t, parity):
    return parity * TILES_PER_BATCH + t // 2


def turns(eng, lag, turn):
    head = (lag + 1) // 2
    for i in range(2 * head):
        turn(i, i % 2)
    with eng.Fori(head, PAIRS) as pair:
        turn(pair * 2, 0)
        turn(pair * 2 + 1, 1)
    for i in range(TILES, TILES + lag):
        turn(i, i % 2)


def norm_stats(dve, act_done, X, stats, mv, root, rstd, s_stats, s_var, s_rstd):
    for t in range(TILES):
        dve.bn_stats(stats[:, t, :], X[:, t, :]).then_inc(s_stats, 1)
    dve.wait_ge(s_stats, TILES)
    for t in range(TILES):
        dve.bn_aggr(mv[:, t, :], stats[:, t, :]).then_inc(s_stats, 1)
    dve.wait_ge(s_stats, 2 * TILES)
    dve.tensor_scalar(root[:, :], mv[:, :, 1], EPS, None, ALU.add).then_inc(s_var, 1)
    dve.wait_ge(act_done, 1)
    dve.reciprocal(rstd[:, :], root[:, :]).then_inc(s_rstd, 1)
    dve.wait_ge(s_rstd, 1)


def phase_xattn0(nc, X, ident, x_loaded, x, ctxT, WqT, Wk, Wv, Wo, bo, mask2, identd):
    with ExitStack() as ctx:
        m = Scope(nc, ctx, "xa0")
        R = 4
        pair = 2 * CTX
        ctx_sb = m.sb("ctx", [P, 2, BATCH * CTX])
        wqT = m.sb("wqT", [P, R, DIM])
        wk = m.sb("wk", [P, 2, 512])
        wv = m.sb("wv", [P, 2, 512])
        wo = m.sb("wo", [P, R, DIM])
        bo_sb = m.sb("bo", [P, DIM])
        mask = m.sb("mask", [P, 2])
        kblk = m.sb("kblk", [P, BATCH, R, pair])
        vblk = m.sb("vblk", [P, BATCH, R, HJ])
        G = m.sb("G", [P, BATCH, KD, HJ])
        U = m.sb("U", [P, BATCH, HJT, DIM])
        stats = m.sb("stats", [P, TILES, 6])
        mv = m.sb("mv", [P, TILES, 2])
        root = m.sb("root", [P, TILES])
        rstd = m.sb("rstd", [P, TILES])
        xn = m.sb("xn", [P, 2, DIM])
        xT = m.sb("xT", [P, 2, KD, P])
        mx = m.sb("mx", [P, 2, GH])
        sm = m.sb("sm", [P, 2, GH])
        rc = m.sb("rc", [P, 2, GH])
        pr = m.sb("pr", [P, 2, HJ])
        pT = m.sb("pT", [P, 2, HJT, P])
        ps_x = m.ps("ps_x", [P, 512])
        ps_s = m.ps("ps_s", [P, 2, 2, 512])
        ps_p = m.ps("ps_p", [P, 2, 512])
        ps_o = m.ps("ps_o", [P, 512])

        w_in, zeroed = m.sem("w_in"), m.sem("zeroed")
        prep_pe, prep_dve, prep_act = m.sem("prep_pe"), m.sem("prep_dve"), m.sem("prep_act")
        s_stats, s_var, s_root, s_rstd = m.sem("s_stats"), m.sem("s_var"), m.sem("s_root"), m.sem("s_rstd")
        normed, turned, xT_in = m.sem("normed"), m.sem("turned"), m.sem("xT_in")
        scored, maxed, shifted = m.sem("scored"), m.sem("maxed"), m.sem("shifted")
        exped, summed, inverted, weighted = m.sem("exped"), m.sem("summed"), m.sem("inverted"), m.sem("weighted")
        pturned, pT_in, projected = m.sem("pturned"), m.sem("pT_in"), m.sem("projected")
        biased, added = m.sem("biased"), m.sem("added")

        LOADS = 12
        LAG = 4

        def U_rows(i):
            return P if i < HJT - 1 else HJR

        block = ctx.enter_context(nc.Block())

        @block.sync
        def _(sp):
            sp.dma_start(X[:, :, :], x.rearrange("(t p) d -> p t d", p=P)).then_inc(x_loaded, 16)
            sp.dma_start(ident[:, :], identd).then_inc(w_in, 16)
            sp.dma_start(mask[:, :], mask2).then_inc(w_in, 16)
            for k, (at, rows) in enumerate(((0, P), (P, C2))):
                sp.dma_start(ctx_sb[0:rows, k, :], ctxT[at:at + rows, :]).then_inc(w_in, 16)
                sp.dma_start(wk[0:rows, k, :], Wk[at:at + rows, :]).then_inc(w_in, 16)
                sp.dma_start(wv[0:rows, k, :], Wv[at:at + rows, :]).then_inc(w_in, 16)
            sp.dma_start(wqT[:, :, :], WqT.rearrange("(r p) c -> p r c", p=P)).then_inc(w_in, 16)
            sp.dma_start(wo[:, :, :], Wo.rearrange("(r p) c -> p r c", p=P)).then_inc(w_in, 16)
            sp.dma_start(bo_sb[0:64, :], bo.partition_broadcast(64)).then_inc(w_in, 16)
            sp.dma_start(bo_sb[64:P, :], bo.partition_broadcast(64)).then_inc(w_in, 16)

        @block.tensor
        def _(pe):
            pe.wait_ge(w_in, 16 * LOADS)
            for w, bank0 in ((wk, 0), (wv, 1)):
                for r in range(R):
                    for k, rows in enumerate((P, C2)):
                        mm = pe.matmul(ps_s[:, bank0, r // 2, (r % 2) * pair:(r % 2 + 1) * pair],
                                       w[0:rows, k, r * P:(r + 1) * P], ctx_sb[0:rows, k, :],
                                       start=k == 0, stop=k == 1)
                mm.then_inc(prep_pe, 1)
            for b in range(BATCH):
                for k in range(KD):
                    n = b * KD + k
                    pe.wait_ge(prep_dve, 1)
                    pe.wait_ge(prep_dve, 2)
                    if n >= 2:
                        pe.wait_ge(prep_act, n - 1)
                    for r in range(R):
                        mm = pe.matmul(ps_s[:, n % 2, r // 2, (r % 2) * pair:(r % 2 + 1) * pair],
                                       wqT[:, r, k * P:(k + 1) * P], kblk[:, b, r, :],
                                       start=True, stop=True)
                    mm.then_inc(prep_pe, 1)
            for b in range(BATCH):
                for i in range(HJT):
                    n = b * HJT + i
                    if n >= 1:
                        pe.wait_ge(prep_act, 4 + n)
                    rows = U_rows(i)
                    over = [r for r in range(R) if r * pair < i * P + rows and (r + 1) * pair > i * P]
                    for r in over:
                        mm = pe.matmul(ps_o[0:rows, 0:DIM], vblk[:, b, r, i * P:i * P + rows], wo[:, r, :],
                                       start=r == over[0], stop=r == over[-1])
                    mm.then_inc(prep_pe, 1)

            for s in (turned, scored, pturned, projected):
                pe.sem_inc(s, LEAD)
            pe.wait_ge(prep_act, 4 + 2 * HJT)

            def turn(i, par):
                if live(i):
                    t = i
                    pe.wait_ge(normed, has(t))
                    pe.wait_ge(xT_in, one_ago(t))
                    for k in range(KD):
                        mm = pe.transpose(ps_x[:, k * P:(k + 1) * P], xn[:, par, k * P:(k + 1) * P], ident[:, :])
                    mm.then_inc(turned, 1)
                if live(i - 3):
                    t, s = i - 3, 1 - par
                    pe.wait_ge(weighted, has(t))
                    pe.wait_ge(pT_in, one_ago(t))
                    for j in range(HJT):
                        rows = U_rows(j)
                        mm = pe.transpose(ps_p[0:rows, j // 4, (j % 4) * P:(j % 4 + 1) * P],
                                          pr[:, s, j * P:j * P + rows], ident[:, :])
                    mm.then_inc(pturned, 1)
                if live(i - 4):
                    t, s = i - 4, par
                    pe.wait_ge(pT_in, has(t))
                    pe.wait_ge(added, one_ago(t))
                    for j in range(HJT):
                        rows = U_rows(j)
                        mm = pe.matmul(ps_o[:, 0:DIM], pT[0:rows, s, j, :], U[0:rows, s, j, :],
                                       start=j == 0, stop=j == HJT - 1)
                    mm.then_inc(projected, 1)
                if live(i - 1):
                    t, s = i - 1, 1 - par
                    pe.wait_ge(xT_in, has(t))
                    pe.wait_ge(shifted, two_ago(t))
                    for half in range(2):
                        for k in range(KD):
                            mm = pe.matmul(ps_s[:, s, half, 0:HALF], xT[:, s, k, :],
                                           G[:, s, k, half * HALF:(half + 1) * HALF],
                                           start=k == 0, stop=k == KD - 1)
                    mm.then_inc(scored, 1)

            turns(pe, LAG, turn)

        @block.vector
        def _(dve):
            dve.memset(vblk[:, :, :, :], 0.0).then_inc(zeroed, 1)
            dve.wait_ge(x_loaded, 16)
            dve.wait_ge(w_in, 16 * LOADS)
            dve.wait_ge(prep_pe, 1)
            for b in range(BATCH):
                for r in range(R):
                    src = ps_s[:, 0, r // 2, (r % 2) * pair + b * CTX:(r % 2) * pair + (b + 1) * CTX]
                    ins = dve.tensor_tensor(kblk[:, b, r, :].rearrange("p (h j) -> p h j", h=2),
                                            src.unsqueeze(1).to_broadcast([P, 2, CTX]),
                                            mask[:, :].unsqueeze(2).to_broadcast([P, 2, CTX]), ALU.mult)
            ins.then_inc(prep_dve, 1)
            dve.wait_ge(prep_pe, 2)
            dve.wait_ge(zeroed, 1)
            for b in range(BATCH):
                for r in range(R):
                    src = ps_s[:, 1, r // 2, (r % 2) * pair + b * CTX:(r % 2) * pair + (b + 1) * CTX]
                    ins = dve.tensor_tensor(vblk[:, b, r, r * pair:(r + 1) * pair].rearrange("p (h j) -> p h j", h=2),
                                            src.unsqueeze(1).to_broadcast([P, 2, CTX]),
                                            mask[:, :].unsqueeze(2).to_broadcast([P, 2, CTX]), ALU.mult)
            ins.then_inc(prep_dve, 1)

            norm_stats(dve, s_root, X, stats, mv, root, rstd, s_stats, s_var, s_rstd)
            for s in (normed, maxed, shifted, summed, inverted, added):
                dve.sem_inc(s, LEAD)

            def turn(i, par):
                if live(i):
                    t = i
                    dve.wait_ge(turned, two_ago(t))
                    x = tile_of(t, par)
                    dve.tensor_scalar(xn[:, par, :], X[:, x, :], mv[:, x, 0:1], rstd[:, bass.ds(x, 1)],
                                      ALU.subtract, ALU.mult).then_inc(normed, 1)
                if live(i - 1):
                    t, s = i - 1, 1 - par
                    dve.wait_ge(scored, has(t))
                    src = ps_s[:, s, :, 0:HALF].rearrange("p a (h j) -> p a h j", j=CTX)
                    dve.tensor_reduce(mx[:, s, :].rearrange("p (a h) -> p a h", a=2), src, AX.X,
                                      ALU.max).then_inc(maxed, 1)
                    dve.wait_ge(maxed, has(t))
                    dve.wait_ge(pturned, two_ago(t))
                    dve.tensor_tensor(pr[:, s, :].rearrange("p (a h j) -> p a h j", a=2, j=CTX), src,
                                      mx[:, s, :].rearrange("p (a h) -> p a h", a=2).unsqueeze(3)
                                      .to_broadcast([P, 2, GH // 2, CTX]), ALU.subtract).then_inc(shifted, 1)
                if live(i - 2):
                    t, s = i - 2, par
                    dve.wait_ge(exped, has(t))
                    dve.wait_ge(weighted, two_ago(t))
                    dve.tensor_reduce(sm[:, s, :], pr[:, s, :].rearrange("p (h j) -> p h j", j=CTX), AX.X,
                                      ALU.add).then_inc(summed, 1)
                    dve.wait_ge(summed, has(t))
                    dve.reciprocal(rc[:, s, :], sm[:, s, :]).then_inc(inverted, 1)
                if live(i - 4):
                    t, x = i - 4, tile_of(i - 4, par)
                    dve.wait_ge(projected, has(t))
                    dve.wait_ge(biased, has(t))
                    dve.tensor_tensor(X[:, x, :], ps_o[:, 0:DIM], X[:, x, :], ALU.add).then_inc(added, 1)

            turns(dve, LAG, turn)

        @block.gpsimd
        def _(pool):
            for s in (weighted, biased):
                pool.sem_inc(s, LEAD)
            pool.wait_ge(w_in, 16 * LOADS)

            def turn(i, par):
                if live(i - 1):
                    t, x = i - 1, tile_of(i - 1, 1 - par)
                    pool.wait_ge(normed, has(t))
                    pool.tensor_tensor(X[:, x, :], X[:, x, :], bo_sb[:, :], ALU.add).then_inc(biased, 1)
                if live(i - 2):
                    t, s = i - 2, par
                    pool.wait_ge(inverted, has(t))
                    v = pr[:, s, :].rearrange("p (h j) -> p h j", j=CTX)
                    pool.tensor_tensor(v, v, rc[:, s, :].unsqueeze(2).to_broadcast([P, GH, CTX]),
                                       ALU.mult).then_inc(weighted, 1)

            turns(pool, LAG, turn)

        @block.scalar
        def _(act):
            for n in range(BATCH * KD):
                act.wait_ge(prep_pe, 3 + n)
                act.activation(G[:, n // KD, n % KD, :].rearrange("p (a c) -> p a c", a=2),
                               ps_s[:, n % 2, :, 0:HALF], ACT.Copy).then_inc(prep_act, 1)
            for n in range(BATCH * HJT):
                act.wait_ge(prep_pe, 3 + BATCH * KD + n)
                rows = U_rows(n % HJT)
                act.activation(U[0:rows, n // HJT, n % HJT, :], ps_o[0:rows, 0:DIM], ACT.Copy).then_inc(prep_act, 1)
            act.wait_ge(s_var, 1)
            act.activation(root[:, :], root[:, :], ACT.Sqrt).then_inc(s_root, 1)
            for s in (xT_in, exped, pT_in):
                act.sem_inc(s, LEAD)

            def turn(i, par):
                if live(i):
                    t = i
                    act.wait_ge(turned, has(t))
                    act.wait_ge(scored, two_ago(t))
                    act.activation(xT[:, par, :, :].rearrange("p k n -> p (k n)"), ps_x[:, 0:DIM],
                                   ACT.Copy).then_inc(xT_in, 1)
                if live(i - 3):
                    t, s = i - 3, 1 - par
                    act.wait_ge(pturned, has(t))
                    act.wait_ge(projected, two_ago(t))
                    act.activation(pT[:, s, 0:4, :].rearrange("p k n -> p (k n)"), ps_p[:, 0, :], ACT.Copy)
                    act.activation(pT[0:HJR, s, 4, :], ps_p[0:HJR, 1, 0:P], ACT.Copy).then_inc(pT_in, 1)
                if live(i - 1):
                    t, s = i - 1, 1 - par
                    act.wait_ge(shifted, has(t))
                    act.activation(pr[:, s, :], pr[:, s, :], ACT.Exp, scale=0.125).then_inc(exped, 1)

            turns(act, LAG, turn)


HEADS, HD = 16, 8
GROUP = 4
GROUPS = BATCH * HEADS // GROUP
GROWS = GROUP * HD
PARTS = 3
TERMS = PARTS * PARTS * HD
MAXROW = 96
KT = SEQ // P
CHUNK = 512
CHUNKS = BATCH * SEQ // CHUNK


def phase_qkv(nc, X, ident, V, qkd, Wq, Wk, Wv, qb, kb, vb):
    with ExitStack() as ctx:
        m = Scope(nc, ctx, "qkv")
        w = m.sb("w", [P, 3, KD, P])
        qb_sb, kb_sb = m.sb("qb", [P, 1]), m.sb("kb", [P, 1])
        vb_sb = m.sb("vb", [P, P])
        stats, mv = m.sb("stats", [P, TILES, 6]), m.sb("mv", [P, TILES, 2])
        root, rstd = m.sb("root", [P, TILES]), m.sb("rstd", [P, TILES])
        xn = m.sb("xn", [P, 2, 4, DIM])
        xT = m.sb("xT", [P, 2, KD, CHUNK])
        full = m.sb("full", [P, 2, 2, CHUNK])
        part = m.sb("part", [P, 2, 2, PARTS, CHUNK], BF16)
        ps_x = m.ps("ps_x", [P, KD, CHUNK])
        ps_qk = m.ps("ps_qk", [P, 2, 2, CHUNK])
        ps_v = m.ps("ps_v", [P, 4, P])
        w_in = m.sem("w_in")
        s_stats, s_var, s_root, s_rstd = m.sem("s_stats"), m.sem("s_var"), m.sem("s_root"), m.sem("s_rstd")
        normed, turned, xT_in = m.sem("normed"), m.sem("turned"), m.sem("xT_in")
        qk_made, v_made, qk_full, v_in = m.sem("qk_made"), m.sem("v_made"), m.sem("qk_full"), m.sem("v_in")
        split_hi, rest1, split_mid, split_lo = m.sem("split_hi"), m.sem("rest1"), m.sem("split_mid"), m.sem("split_lo")
        residual, stored = m.sem("residual"), [m.sem(f"stored{n}") for n in range(2)]
        LOADS = 7
        STORES = 2
        scale = float(HD) ** -0.5

        block = ctx.enter_context(nc.Block())

        @block.sync
        def _(sp):
            for n, src in enumerate((Wq, Wk, Wv)):
                sp.dma_start(w[:, n, :, :], src.rearrange("(k p) n -> p k n", p=P)).then_inc(w_in, 16)
            sp.dma_start(qb_sb[:, :], qb).then_inc(w_in, 16)
            sp.dma_start(kb_sb[:, :], kb).then_inc(w_in, 16)
            sp.dma_start(vb_sb[0:64, :], vb.partition_broadcast(64)).then_inc(w_in, 16)
            sp.dma_start(vb_sb[64:P, :], vb.partition_broadcast(64)).then_inc(w_in, 16)
            for c in range(CHUNKS):
                s, b, at = c % 2, c // 2, (c % 2) * CHUNK
                sp.wait_ge(split_lo, 2 * c + 2)
                for n in range(2):
                    sp.dma_start(qkd[n, :, b * P:(b + 1) * P, at:at + CHUNK].rearrange("a p n -> p a n"),
                                 part[:, s, n, :, :]).then_inc(stored[s], 16)
            for s in range(2):
                sp.wait_ge(stored[s], 16 * STORES * CHUNKS // 2)

        @block.tensor
        def _(pe):
            pe.wait_ge(w_in, 16 * LOADS)
            for c in range(CHUNKS):
                s = c % 2
                pe.wait_ge(normed, c + 1)
                if c >= 1:
                    pe.wait_ge(xT_in, c)
                for t in range(4):
                    for k in range(KD):
                        mm = pe.transpose(ps_x[:, k, t * P:(t + 1) * P], xn[:, s, t, k * P:(k + 1) * P], ident[:, :])
                mm.then_inc(turned, 1)
                pe.wait_ge(xT_in, c + 1)
                if c >= 2:
                    pe.wait_ge(qk_full, 2 * (c - 1))
                for n in range(2):
                    for k in range(KD):
                        mm = pe.matmul(ps_qk[:, s, n, :], w[:, n, k, :], xT[:, s, k, :], start=k == 0, stop=k == KD - 1)
                mm.then_inc(qk_made, 1)
                if c >= 1:
                    pe.wait_ge(v_in, c)
                for t in range(4):
                    for k in range(KD):
                        mm = pe.matmul(ps_v[:, t, :], xT[:, s, k, t * P:(t + 1) * P], w[:, 2, k, :],
                                       start=k == 0, stop=k == KD - 1)
                mm.then_inc(v_made, 1)

        @block.vector
        def _(dve):
            norm_stats(dve, s_root, X, stats, mv, root, rstd, s_stats, s_var, s_rstd)

            def norm(c):
                if c >= 2:
                    dve.wait_ge(turned, c - 1)
                    dve.wait_ge(residual, c - 1)
                for t in range(4):
                    n = 4 * c + t
                    ins = dve.tensor_scalar(xn[:, c % 2, t, :], X[:, n, :], mv[:, n, 0:1], rstd[:, n:n + 1],
                                            ALU.subtract, ALU.mult)
                ins.then_inc(normed, 1)

            dve.wait_ge(w_in, 16 * LOADS)
            norm(0)
            for c in range(CHUNKS):
                s = c % 2
                if c + 1 < CHUNKS:
                    norm(c + 1)
                dve.wait_ge(qk_made, c + 1)
                if c >= 2:
                    dve.wait_ge(split_lo, 2 * (c - 1))
                dve.tensor_scalar(full[:, s, 0, :], ps_qk[:, s, 0, :], qb_sb[:, :], scale, ALU.add,
                                  ALU.mult).then_inc(qk_full, 1)
                dve.tensor_scalar(full[:, s, 1, :], ps_qk[:, s, 1, :], kb_sb[:, :], None, ALU.add).then_inc(qk_full, 1)
                dve.wait_ge(v_made, c + 1)
                b = c // 2
                for t in range(4):
                    kt = (c % 2) * 4 + t
                    ins = dve.tensor_tensor(V[:, b * GROUP:(b + 1) * GROUP, kt, :],
                                            ps_v[:, t, :].rearrange("p (g n) -> p g n", g=GROUP),
                                            vb_sb[:, :].rearrange("p (g n) -> p g n", g=GROUP), ALU.add)
                ins.then_inc(v_in, 1)
                dve.wait_ge(split_hi, c + 1)
                dve.tensor_tensor(full[:, s, :, :], full[:, s, :, :], part[:, s, :, 0, :], ALU.subtract).then_inc(rest1, 1)
                dve.wait_ge(split_mid, c + 1)
                for n in range(2):
                    dve.tensor_tensor(part[:, s, n, 2, :], full[:, s, n, :], part[:, s, n, 1, :],
                                      ALU.subtract).then_inc(split_lo, 1)

        @block.gpsimd
        def _(pool):
            for c in range(CHUNKS):
                pool.wait_ge(normed, c + 1)
                for t in range(4):
                    n = 4 * c + t
                    ins = pool.tensor_tensor(X[:, n, :], X[:, n, :], xn[:, c % 2, t, :], ALU.add)
                ins.then_inc(residual, 1)

        @block.scalar
        def _(act):
            act.wait_ge(s_var, 1)
            act.activation(root[:, :], root[:, :], ACT.Sqrt).then_inc(s_root, 1)
            for c in range(CHUNKS):
                s = c % 2
                act.wait_ge(turned, c + 1)
                if c >= 2:
                    act.wait_ge(v_made, c - 1)
                act.activation(xT[:, s, :, :], ps_x[:, :, :], ACT.Copy).then_inc(xT_in, 1)
                act.wait_ge(qk_full, 2 * c + 2)
                if c >= 2:
                    act.wait_ge(stored[s], 16 * STORES * (c // 2))
                act.activation(part[:, s, :, 0, :], full[:, s, :, :], ACT.Copy).then_inc(split_hi, 1)
                act.wait_ge(rest1, c + 1)
                act.activation(part[:, s, :, 1, :], full[:, s, :, :], ACT.Copy).then_inc(split_mid, 1)


SLOTS = 3
STEPS = KT * GROUP


def first_pass():
    items = []
    for j in range(GROUP):
        for n in range(2 * KT):
            if j and n == 8:
                items.append(("turn", j - 1, 0, 0))
            items.append(("score", j, n // 2, n % 2))
    return items + [("turn", GROUP - 1, 0, 0)]


ITEMS = first_pass()


def turned_at(j):
    return ITEMS.index(("turn", j, 0, 0)) + 1


def scored_at(j):
    return ITEMS.index(("score", j, KT - 1, 1)) + 1


def phase_attention(nc, ident, identb, V, qkd, aon, aod):
    with ExitStack() as ctx:
        m = Scope(nc, ctx, "att")
        q = m.sb("q", [P, SLOTS, GROUP, SEQ], BF16)
        k = m.sb("k", [P, SLOTS, GROUP, SEQ], BF16)
        v = m.sb("v", [P, SLOTS, KT, GROUP, 32])
        e = m.sb("e", [P, 2, GROUP, SEQ])
        o = m.sb("o", [P, SLOTS, SEQ])
        mh = m.sb("mh", [P, 2, 2 * KT])
        mf = m.sb("mf", [P, 2, KT])
        mr = m.sb("mr", [P, 2, KT])
        mp = m.sb("mp", [P, 2, PARTS, KT], BF16)
        mT = m.sb("mT", [PARTS * KT, 2, P], BF16)
        ps_s = m.ps("ps_s", [P, 2, 2, 512])
        ps_o = m.ps("ps_o", [P, 2, 512])
        ps_m = [m.ps(f"ps_m{n}", [P, 512]) for n in range(2)]

        ready = m.sem("ready")
        qk_in, m_in = [m.sem(f"qk_in{n}") for n in range(SLOTS)], [m.sem(f"m_in{n}") for n in range(2)]
        zeroed, v_in = m.sem("zeroed"), m.sem("v_in")
        item_made, item_read = m.sem("item_made"), m.sem("item_read")
        m_hi, m_mid, m_parts = m.sem("m_hi"), m.sem("m_mid"), m.sem("m_parts")
        step_made, step_exp, summed, sums_out, stored = (m.sem("step_made"), m.sem("step_exp"), m.sem("summed"),
                                                         m.sem("sums_out"), m.sem("stored"))
        NI = len(ITEMS)
        QKL = 2 * PARTS * GROUP
        OST = GROUP + 1
        PV_LEAD = 4

        def groups(eng, run):
            run(0, 0)
            with eng.Fori(0, (GROUPS - 2) // SLOTS) as i:
                for s in range(SLOTS):
                    run(i * SLOTS + s + 1, (s + 1) % SLOTS)
            run(GROUPS - 1, (GROUPS - 1) % SLOTS)

        def first_group(g):
            return isinstance(g, int) and g == 0

        def last_group(g):
            return isinstance(g, int) and g == GROUPS - 1

        block = ctx.enter_context(nc.Block())

        @block.sync
        def _(sp):
            def load(g, slot):
                for j in range(GROUP):
                    rows = bass.ds(g * GROWS + j * HD, HD)
                    for a in range(PARTS):
                        sp.dma_start(q[24 * a:24 * (a + 1), slot, j, :], qkd[0, :, rows, :]).then_inc(qk_in[slot], 16)
                        sp.dma_start(k[24 * a:24 * (a + 1), slot, j, :],
                                     qkd[1, a, rows, :].unsqueeze(0).to_broadcast([PARTS, HD, SEQ])
                                     ).then_inc(qk_in[slot], 16)

            def maxima(g, slot):
                for j in range(GROUP):
                    sp.wait_ge(item_read, g * NI + turned_at(j) + LEAD)
                    sp.dma_start(q[MAXROW:MAXROW + PARTS, slot, j, :], mT[:, j % 2, :]).then_inc(m_in[j % 2], 16)

            def store(g, slot):
                sp.wait_ge(sums_out, g + 1)
                sp.dma_start(aod[bass.ds(g * GROUP, GROUP), :], o[HD:P:32, slot, :]).then_inc(stored, 16)
                for j in range(GROUP):
                    sp.dma_start(aon[bass.ds(g * GROWS + j * HD, HD), :], o[32 * j:32 * j + HD, slot, :]).then_inc(stored, 16)

            sp.wait_ge(ready, 2)
            load(0, 0)
            load(1, 1)
            maxima(0, 0)
            with sp.Fori(0, (GROUPS - 2) // SLOTS) as i:
                for s in range(SLOTS):
                    g = i * SLOTS + s
                    sp.wait_ge(step_exp, g * STEPS + LEAD)
                    load(g + 2, (s + 2) % SLOTS)
                    maxima(g + 1, (s + 1) % SLOTS)
                    store(g, s)
            maxima(GROUPS - 1, (GROUPS - 1) % SLOTS)
            for g in (GROUPS - 2, GROUPS - 1):
                store(g, g % SLOTS)
            sp.wait_ge(stored, 16 * OST * GROUPS + LEAD)

        @block.tensor
        def _(pe):
            pe.sem_inc(summed, PV_LEAD)

            def first(g, slot, items):
                for n in items:
                    what, j, t, half = ITEMS[n]
                    pe.wait_ge(item_read, g * NI + n - 1 + LEAD)
                    bank = ps_m[n % 2]
                    if what == "score":
                        mm = pe.matmul(bank[:, :], q[0:MAXROW, slot, j, t * P:(t + 1) * P],
                                       k[0:MAXROW, slot, j, half * 512:(half + 1) * 512], start=True, stop=True)
                    else:
                        pe.wait_ge(m_parts, g * GROUP + j + 1)
                        mm = pe.transpose(bank[0:PARTS * KT, 0:P // 2].bitcast(BF16),
                                          mp[:, j % 2, :, :].rearrange("p a t -> p (a t)"), identb[:, :])
                    mm.then_inc(item_made, 1)

            def sums(g, slot, kt, half):
                for j in range(GROUP):
                    mm = pe.matmul(ps_o[32 * j:32 * (j + 1), half, :], v[:, slot, kt, j, :],
                                   e[:, kt % 2, j, half * 512:(half + 1) * 512], start=kt == 0, stop=kt == KT - 1)
                mm.then_inc(summed, 1)

            def load_wait(g, slot):
                pe.wait_ge(qk_in[slot], 16 * QKL * ((g - slot) // SLOTS + 1))

            pe.wait_ge(ready, 2)
            load_wait(0, 0)
            first(0, 0, range(NI))

            def run(g, slot):
                more = not last_group(g)
                if more:
                    load_wait(g + 1, (slot + 1) % SLOTS)
                for n in range(2):
                    pe.wait_ge(m_in[n], 16 * (GROUP // 2) * (g + 1))
                done = 0
                for s in range(STEPS):
                    kt, j = s // GROUP, s % GROUP
                    pe.wait_ge(step_exp, g * STEPS + s - 1 + LEAD)
                    for half in range(2):
                        mm = pe.matmul(ps_s[:, s % 2, half, :], k[:, slot, j, kt * P:(kt + 1) * P],
                                       q[:, slot, j, half * 512:(half + 1) * 512], start=True, stop=True)
                    mm.then_inc(step_made, 1)
                    if more:
                        upto = min(NI, (s + 1) * NI // (STEPS - 4))
                        first(g + 1, (slot + 1) % SLOTS, range(done, upto))
                        done = upto
                    if s % 2 == 1:
                        half = j // 2
                        if kt:
                            if j == 1:
                                pe.wait_ge(step_exp, g * STEPS + kt * GROUP + LEAD)
                            if kt == 1 and j == 1:
                                pe.wait_ge(sums_out, g)
                                pe.wait_ge(v_in, g + 1)
                            sums(g, slot, kt - 1, half)
                        elif not first_group(g):
                            if j == 1:
                                pe.wait_ge(step_exp, g * STEPS + LEAD)
                            sums(g - 1, (slot - 1) % SLOTS, KT - 1, half)

            groups(pe, run)
            pe.wait_ge(step_exp, GROUPS * STEPS + LEAD)
            for half in range(2):
                sums(GROUPS - 1, (GROUPS - 1) % SLOTS, KT - 1, half)

        @block.vector
        def _(dve):
            dve.tensor_copy(identb[:, :], ident[:, :])
            dve.memset(q[64:P, :, :, :], 0.0)
            dve.memset(k[64:MAXROW, :, :, :], 0.0)
            dve.memset(k[MAXROW:P, :, :, :], -1.0).then_inc(ready, 1)
            dve.sem_inc(item_read, LEAD)

            def first(g):
                for n, (what, j, t, half) in enumerate(ITEMS):
                    dve.wait_ge(item_made, g * NI + n + 1)
                    if what == "score" and t == half == 0 and not (first_group(g) and j < 2):
                        dve.wait_ge(m_parts, g * GROUP + j - 1)
                    if what == "score":
                        dve.tensor_reduce(mh[:, j % 2, 2 * t + half:2 * t + half + 1], ps_m[n % 2][:, :], AX.X,
                                          ALU.max).then_inc(item_read, 1)
                        if n + 1 == scored_at(j):
                            dve.wait_ge(item_read, g * NI + n + 1 + LEAD)
                            a, b = (mh[:, j % 2, h:2 * KT:2] for h in range(2))
                            for dst in (mp[:, j % 2, 0, :], mf[:, j % 2, :]):
                                dve.tensor_tensor(dst, a, b, ALU.max).then_inc(m_hi, 1)
                    else:
                        if not (first_group(g) and j < 2):
                            dve.wait_ge(m_in[j % 2], 16 * (g * (GROUP // 2) + j // 2))
                        dve.tensor_copy(mT[:, j % 2, :], ps_m[n % 2][0:PARTS * KT, 0:P // 2].bitcast(BF16)
                                        ).then_inc(item_read, 1)

            first(0)
            with dve.Fori(1, GROUPS) as g:
                first(g)

        @block.gpsimd
        def _(pool):
            pool.memset(v[:, :, :, :, :], 0.0).then_inc(zeroed, 1)
            pool.wait_ge(zeroed, 1)
            pool.memset(v[:, :, :, :, HD:HD + 1], 1.0).then_inc(ready, 1)
            pool.wait_ge(ready, 1)

            def first(g):
                for j in range(GROUP):
                    n = g * GROUP + j
                    s = j % 2
                    pool.wait_ge(m_hi, 2 * n + 2)
                    pool.tensor_tensor(mp[:, s, 1, :], mf[:, s, :], mp[:, s, 0, :], ALU.subtract).then_inc(m_mid, 1)
                    pool.tensor_tensor(mr[:, s, :], mf[:, s, :], mp[:, s, 0, :], ALU.subtract).then_inc(m_mid, 1)
                    pool.wait_ge(m_mid, 2 * n + 2)
                    pool.tensor_tensor(mp[:, s, 2, :], mr[:, s, :], mp[:, s, 1, :], ALU.subtract).then_inc(m_parts, 1)

            def values(g, slot):
                pool.tensor_copy(v[:, slot, :, :, 0:HD], V[:, g, :, :].rearrange("p t (j d) -> p t j d", d=HD)
                                 ).then_inc(v_in, 1)

            first(0)

            def run(g, slot):
                values(g, slot)
                if not last_group(g):
                    first(g + 1)

            groups(pool, run)

        @block.scalar
        def _(act):
            for s in (step_exp, stored):
                act.sem_inc(s, LEAD)

            def out(g, slot):
                act.wait_ge(summed, (g + 1) * 2 * KT + PV_LEAD)
                act.wait_ge(stored, 16 * OST * g + LEAD)
                act.activation(o[:, slot, :].rearrange("p (a n) -> p a n", a=2), ps_o[:, :, :], ACT.Copy).then_inc(sums_out, 1)

            def run(g, slot):
                for s in range(STEPS):
                    kt, j = s // GROUP, s % GROUP
                    act.wait_ge(step_made, g * STEPS + s + 1)
                    if j == 0:
                        act.wait_ge(summed, g * 2 * KT + 2 * (kt - 1) + PV_LEAD)
                    act.activation(e[:, kt % 2, j, :].rearrange("p (a n) -> p a n", a=2), ps_s[:, s % 2, :, :],
                                   ACT.Exp).then_inc(step_exp, 1)
                    if s == GROUP and not first_group(g):
                        out(g - 1, (slot - 1) % SLOTS)

            groups(act, run)
            out(GROUPS - 1, (GROUPS - 1) % SLOTS)


EXPERTS, FF = 8, 512
FT = FF // P
CT = CHUNK // P


def f32(ap):
    return ap.bitcast(F32)


def phase_router(nc, ident, mla_hi, mla_lo, combine, acc, aon, aod, ow, ob, rw, rb, b2, iota):
    with ExitStack() as ctx:
        m = Scope(nc, ctx, "rt")
        ow_sb, ob_sb = m.sb("ow", [P, DIM]), m.sb("ob", [P, KD])
        rw_sb, rb_sb = m.sb("rw", [P, KD, EXPERTS]), m.sb("rb", [P, EXPERTS])
        b2_sb, iota_sb = m.sb("b2", [EXPERTS, DIM]), m.sb("iota", [P, EXPERTS])
        num, den = m.sb("num", [P, 2, CHUNK]), m.sb("den", [P, 2, CHUNK])
        ao = m.sb("ao", [P, 2, CHUNK])
        full = m.sb("full", [P, 2, KD, CHUNK])
        logit = m.sb("logit", [P, TILES, EXPERTS])
        top = m.sb("top", [P, TILES, 8])
        index = m.sb("index", [P, TILES, 8], U32)
        indexf = m.sb("indexf", [P, TILES, 2])
        big = m.sb("big", [P, TILES])
        pair = m.sb("pair", [P, TILES, 2])
        first = m.sb("first", [P, TILES, EXPERTS])
        cT = m.sb("cT", [EXPERTS, TILES, P])
        ps_m = m.ps("ps_m", [P, 2, KD, CHUNK])
        ps_r = m.ps("ps_r", [P, 2, 512])
        ps_a = m.ps("ps_a", [P, 2, 512])

        w_in, sums_in = m.sem("w_in"), [m.sem(f"sums_in{n}") for n in range(2)]
        inverted, divided, mla_made, mla_full, hi_made, lo_made = (m.sem("inverted"), m.sem("divided"), m.sem("mla_made"),
                                                                   m.sem("mla_full"), m.sem("hi_made"), m.sem("lo_made"))
        routed, logits, chain, exped = m.sem("routed"), m.sem("logits"), m.sem("chain"), m.sem("exped")
        c_turned, c_out, acc_made, acc_out = m.sem("c_turned"), m.sem("c_out"), m.sem("acc_made"), m.sem("acc_out")
        LOADS = 9
        CHAIN = 13 + 2 * TILES

        block = ctx.enter_context(nc.Block())

        @block.sync
        def _(sp):
            for dst, src in ((ow_sb, ow), (ob_sb, ob), (b2_sb, b2), (iota_sb, iota)):
                sp.dma_start(dst[:, :], src).then_inc(w_in, 16)
            sp.dma_start(rw_sb[:, :, :], rw.rearrange("(k p) e -> p k e", p=P)).then_inc(w_in, 16)
            for n in range(4):
                sp.dma_start(rb_sb[32 * n:32 * (n + 1), :], rb.partition_broadcast(32)).then_inc(w_in, 16)
            for c in range(CHUNKS):
                s, b, at = c % 2, c // 2, (c % 2) * CHUNK
                if c >= 2:
                    sp.wait_ge(divided, c - 1)
                sp.dma_start(num[:, s, :], aon[b * P:(b + 1) * P, at:at + CHUNK]).then_inc(sums_in[s], 16)
                sp.dma_start(den[:, s, :], aod[b * HEADS:(b + 1) * HEADS, at:at + CHUNK].unsqueeze(1)
                             .to_broadcast([HEADS, HD, CHUNK])).then_inc(sums_in[s], 16)

        @block.tensor
        def _(pe):
            pe.wait_ge(w_in, 16 * LOADS)
            for c in range(CHUNKS):
                s = c % 2
                pe.wait_ge(divided, c + 1)
                if c >= 2:
                    pe.wait_ge(mla_full, c - 1)
                for k in range(KD):
                    mm = pe.matmul(ps_m[:, s, k, :], ow_sb[:, k * P:(k + 1) * P], ao[:, s, :], start=True, stop=True)
                mm.then_inc(mla_made, 1)
                pe.wait_ge(mla_full, c + 1)
                if c >= 2:
                    pe.wait_ge(logits, c - 1)
                for t in range(CT):
                    for k in range(KD):
                        mm = pe.matmul(ps_r[:, s, t * EXPERTS:(t + 1) * EXPERTS], full[:, s, k, t * P:(t + 1) * P],
                                       rw_sb[:, k, :], start=k == 0, stop=k == KD - 1)
                mm.then_inc(routed, 1)
            pe.wait_ge(chain, CHAIN)
            for t in range(TILES):
                if t >= 1:
                    pe.wait_ge(c_out, t)
                pe.transpose(ps_r[0:EXPERTS, 0, 0:P], combine[:, t, :], ident[:, :]).then_inc(c_turned, 1)
                pe.wait_ge(c_out, t + 1)
                if t >= 2:
                    pe.wait_ge(acc_out, t - 1)
                pe.matmul(ps_a[:, t % 2, 0:DIM], cT[:, t, :], b2_sb[:, :], start=True, stop=True).then_inc(acc_made, 1)

        @block.vector
        def _(dve):
            dve.wait_ge(w_in, 16 * LOADS)
            for c in range(CHUNKS):
                s = c % 2
                at = c * CHUNK
                dve.wait_ge(sums_in[s], 32 * (c // 2 + 1))
                dve.reciprocal(den[:, s, :], den[:, s, :]).then_inc(inverted, 1)
                dve.wait_ge(inverted, c + 1)
                if c >= 2:
                    dve.wait_ge(mla_made, c - 1)
                dve.tensor_tensor(ao[:, s, :], num[:, s, :], den[:, s, :], ALU.mult).then_inc(divided, 1)
                dve.wait_ge(mla_full, c + 1)
                dve.tensor_copy(mla_hi[:, :, at:at + CHUNK], full[:, s, :, :]).then_inc(hi_made, 1)
                dve.wait_ge(hi_made, c + 1)
                dve.tensor_tensor(mla_lo[:, :, at:at + CHUNK], full[:, s, :, :], f32(mla_hi[:, :, at:at + CHUNK]),
                                  ALU.subtract).then_inc(lo_made, 1)
                dve.wait_ge(routed, c + 1)
                dve.tensor_tensor(logit[:, c * CT:(c + 1) * CT, :],
                                  ps_r[:, s, 0:CT * EXPERTS].rearrange("p (t e) -> p t e", e=EXPERTS),
                                  rb_sb[:, :].unsqueeze(1).to_broadcast([P, CT, EXPERTS]), ALU.add).then_inc(logits, 1)

            made = [0]

            def linked(ins):
                made[0] += 1
                ins.then_inc(chain, 1)
                dve.wait_ge(chain, made[0])

            wide = [P, TILES, EXPERTS]
            dve.wait_ge(logits, CHUNKS)
            linked(dve.tensor_reduce(big[:, :], logit[:, :, :], AX.X, ALU.max))
            linked(dve.tensor_tensor(logit[:, :, :], logit[:, :, :], big[:, :].unsqueeze(2).to_broadcast(wide),
                                     ALU.subtract))
            dve.wait_ge(exped, 1)
            linked(dve.tensor_reduce(big[:, :], logit[:, :, :], AX.X, ALU.add))
            linked(dve.reciprocal(big[:, :], big[:, :]))
            linked(dve.tensor_tensor(logit[:, :, :], logit[:, :, :], big[:, :].unsqueeze(2).to_broadcast(wide), ALU.mult))
            for t in range(TILES):
                dve.max(top[:, t, :], logit[:, t, :]).then_inc(chain, 1)
            made[0] += TILES
            dve.wait_ge(chain, made[0])
            for t in range(TILES):
                dve.max_index(index[:, t, :], top[:, t, :], logit[:, t, :]).then_inc(chain, 1)
            made[0] += TILES
            dve.wait_ge(chain, made[0])
            linked(dve.tensor_copy(indexf[:, :, :], index[:, :, 0:2]))
            linked(dve.tensor_tensor(big[:, :], top[:, :, 0], top[:, :, 1], ALU.add))
            linked(dve.tensor_scalar(big[:, :], big[:, :], 1e-8, None, ALU.add))
            linked(dve.reciprocal(big[:, :], big[:, :]))
            linked(dve.tensor_tensor(pair[:, :, :], top[:, :, 0:2], big[:, :].unsqueeze(2).to_broadcast([P, TILES, 2]),
                                     ALU.mult))
            for n, dst in ((0, first), (1, combine)):
                dve.tensor_tensor(dst[:, :, :], iota_sb[:, :].unsqueeze(1).to_broadcast(wide),
                                  indexf[:, :, n].unsqueeze(2).to_broadcast(wide), ALU.is_equal).then_inc(hi_made, 1)
                dve.wait_ge(hi_made, CHUNKS + n + 1)
                linked(dve.tensor_tensor(dst[:, :, :], dst[:, :, :], pair[:, :, n].unsqueeze(2).to_broadcast(wide),
                                         ALU.mult))
            linked(dve.tensor_tensor(combine[:, :, :], combine[:, :, :], first[:, :, :], ALU.add))
            assert made[0] == CHAIN, made[0]
            for t in range(TILES):
                dve.wait_ge(c_turned, t + 1)
                dve.tensor_copy(cT[:, t, :], ps_r[0:EXPERTS, 0, 0:P]).then_inc(c_out, 1)

        @block.scalar
        def _(act):
            act.wait_ge(w_in, 16 * LOADS)
            for c in range(CHUNKS):
                s = c % 2
                act.wait_ge(mla_made, c + 1)
                if c >= 2:
                    act.wait_ge(lo_made, c - 1)
                    act.wait_ge(routed, c - 1)
                act.activation(full[:, s, 0, :], ps_m[:, s, 0, :], ACT.Identity, bias=ob_sb[:, 0:1])
                act.activation(full[:, s, 1, :], ps_m[:, s, 1, :], ACT.Identity, bias=ob_sb[:, 1:2]).then_inc(mla_full, 1)
            act.wait_ge(chain, 2)
            act.activation(logit[:, :, :], logit[:, :, :], ACT.Exp).then_inc(exped, 1)
            for t in range(TILES):
                act.wait_ge(acc_made, t + 1)
                act.activation(acc[:, t, :], ps_a[:, t % 2, 0:DIM], ACT.Copy).then_inc(acc_out, 1)


def phase_experts(nc, X, mla_hi, mla_lo, combine, acc, w1, b1, w2):
    with ExitStack() as ctx:
        m = Scope(nc, ctx, "moe")
        raw1, raw2, rawb = m.sb("raw1", [P, 2, KD, FF]), m.sb("raw2", [P, 2, FT, DIM]), m.sb("rawb", [P, 2, FT])
        w1_hi, w1_lo = m.sb("w1_hi", [P, 2, KD, FF], F32R), m.sb("w1_lo", [P, 2, KD, FF], F32R)
        w2_hi, w2_lo = m.sb("w2_hi", [P, 2, FT, DIM], F32R), m.sb("w2_lo", [P, 2, FT, DIM], F32R)
        b1_sb = m.sb("b1", [P, 2, FT])
        one = m.sb("one", [P, KD])
        g = m.sb("g", [P, 2, FT, CHUNK])
        g_hi, g_lo = m.sb("g_hi", [P, 2, FT, CHUNK], F32R), m.sb("g_lo", [P, 2, FT, CHUNK], F32R)
        ps_h = [m.ps(f"ps_h{n}", [P, CHUNK]) for n in range(FT)]
        ps_o = [m.ps(f"ps_o{n}", [P, 512]) for n in range(CT)]
        raw_in = [m.sem(f"raw_in{n}") for n in range(2)]
        w_ready, hid_made, hid_out, lo_made, out_made, out_added = (m.sem("w_ready"), m.sem("hid_made"), m.sem("hid_out"),
                                                                    m.sem("lo_made"), m.sem("out_made"), m.sem("out_added"))
        scaled, one_set = m.sem("scaled"), m.sem("one_set")
        SPLITS = 5
        W_LEAD, HID_LEAD, OUT_LEAD, ADD_LEAD = 2 * SPLITS, 2 * FT, CHUNKS * CT + 1, CT
        EPAIRS = EXPERTS // 2

        block = ctx.enter_context(nc.Block())

        def expert_pairs(eng, run):
            with eng.Fori(0, EPAIRS - 1) as i:
                run(i * 2, True)
            run(EXPERTS - 2, False)

        @block.sync
        def _(sp):
            with sp.Fori(0, EPAIRS) as i:
                for s in range(2):
                    e = i * 2 + s
                    sp.wait_ge(w_ready, W_LEAD + (e - 1) * SPLITS)
                    sp.dma_start(raw1[:, s, :, :], w1[e].rearrange("(k p) f -> p k f", p=P)).then_inc(raw_in[s], 16)
                    sp.dma_start(raw2[:, s, :, :], w2[e].rearrange("(k p) f -> p k f", p=P)).then_inc(raw_in[s], 16)
                    sp.dma_start(rawb[:, s, :], b1[e]).then_inc(raw_in[s], 16)

        @block.gpsimd
        def _(pool):
            pool.sem_inc(w_ready, W_LEAD)
            pool.memset(one[:, :], 1.0).then_inc(one_set, 1)
            pool.wait_ge(one_set, 1)
            with pool.Fori(0, EPAIRS) as i:
                for s in range(2):
                    e = i * 2 + s
                    pool.wait_ge(raw_in[s], 48 * (i + 1))
                    pool.wait_ge(out_made, OUT_LEAD + (e - 1) * CHUNKS * CT)
                    pool.tensor_tensor(w1_hi[:, s, :, :], raw1[:, s, :, :],
                                       one[:, :].unsqueeze(2).to_broadcast([P, KD, FF]), ALU.mult).then_inc(w_ready, 1)
                    pool.tensor_copy(w2_hi[:, s, :, :], raw2[:, s, :, :]).then_inc(w_ready, 1)
                    pool.tensor_copy(b1_sb[:, s, :], rawb[:, s, :]).then_inc(w_ready, 1)
                    pool.wait_ge(w_ready, W_LEAD + e * SPLITS + 2)
                    pool.tensor_tensor(w1_lo[:, s, :, :], raw1[:, s, :, :], f32(w1_hi[:, s, :, :]),
                                       ALU.subtract).then_inc(w_ready, 1)
                    pool.tensor_tensor(w2_lo[:, s, :, :], raw2[:, s, :, :], f32(w2_hi[:, s, :, :]),
                                       ALU.subtract).then_inc(w_ready, 1)

        @block.tensor
        def _(pe):
            pe.sem_inc(out_made, OUT_LEAD)

            def hidden(n, s, c, sg):
                for f in range(FT):
                    pe.wait_ge(hid_out, n * 2 * FT + 2 * (f + 1))
                    at = slice(c * CHUNK, (c + 1) * CHUNK)
                    for i, (w, x) in enumerate(((w1_hi, mla_hi), (w1_lo, mla_hi), (w1_hi, mla_lo))):
                        for k in range(KD):
                            mm = pe.matmul(ps_h[f][:, :], w[:, s, k, f * P:(f + 1) * P], x[:, k, at],
                                           start=i == 0 and k == 0, stop=i == 2 and k == KD - 1)
                    mm.then_inc(hid_made, 1)

            def output(n, s, sg):
                pe.wait_ge(lo_made, (n + 1) * FT)
                for t in range(CT):
                    pe.wait_ge(out_added, n * CT + t + 1)
                    for i, (x, w) in enumerate(((g_hi, w2_hi), (g_lo, w2_hi), (g_hi, w2_lo))):
                        for f in range(FT):
                            mm = pe.matmul(ps_o[t][:, 0:DIM], x[:, sg, f, t * P:(t + 1) * P], w[:, s, f, :],
                                           start=i == 0 and f == 0, stop=i == 2 and f == FT - 1)
                    mm.then_inc(out_made, 1)

            pe.wait_ge(w_ready, W_LEAD + SPLITS)
            hidden(0, 0, 0, 0)

            def run(e0, more):
                for j in range(2 * CHUNKS):
                    n = e0 * CHUNKS + j
                    if more or j + 1 < 2 * CHUNKS:
                        if (j + 1) % CHUNKS == 0:
                            pe.wait_ge(w_ready, W_LEAD + (e0 + (j + 1) // CHUNKS + 1) * SPLITS)
                        hidden(n + 1, (j + 1) // CHUNKS % 2, (j + 1) % CHUNKS, (j + 1) % 2)
                    output(n, j // CHUNKS, j % 2)

            expert_pairs(pe, run)

        @block.scalar
        def _(act):
            act.sem_inc(hid_out, HID_LEAD)
            with act.Fori(0, EPAIRS) as i:
                for j in range(2 * CHUNKS):
                    n, s, sg = i * (2 * CHUNKS) + j, j // CHUNKS, j % 2
                    act.wait_ge(out_made, OUT_LEAD + (n - 1) * CT)
                    for f in range(FT):
                        act.wait_ge(hid_made, n * FT + f + 1)
                        for dst in (g, g_hi):
                            act.activation(dst[:, sg, f, :], ps_h[f][:, :], ACT.Gelu, bias=b1_sb[:, s, f:f + 1]).then_inc(hid_out, 1)

        @block.vector
        def _(dve):
            dve.sem_inc(out_added, ADD_LEAD)

            def low(n, sg):
                for f in range(FT):
                    dve.wait_ge(hid_out, HID_LEAD + n * 2 * FT + 2 * (f + 1))
                    dve.tensor_tensor(g_lo[:, sg, f, :], g[:, sg, f, :], f32(g_hi[:, sg, f, :]), ALU.subtract).then_inc(lo_made, 1)

            def add(n, e, c):
                for t in range(CT):
                    dve.wait_ge(out_made, OUT_LEAD + n * CT + t + 1)
                    tile = c * CT + t
                    dve.scalar_tensor_tensor(out=acc[:, tile, :], in0=ps_o[t][:, 0:DIM], scalar=combine[:, tile, bass.ds(e, 1)],
                                             in1=acc[:, tile, :], op0=ALU.mult, op1=ALU.add).then_inc(out_added, 1)

            low(0, 0)

            def run(e0, more):
                for j in range(2 * CHUNKS):
                    n = e0 * CHUNKS + j
                    if more or j + 1 < 2 * CHUNKS:
                        low(n + 1, (j + 1) % 2)
                    add(n, e0 + j // CHUNKS, j % CHUNKS)

            expert_pairs(dve, run)
            dve.wait_ge(out_added, ADD_LEAD + EXPERTS * TILES)
            for t in range(TILES):
                dve.scalar_tensor_tensor(out=X[:, t, :], in0=acc[:, t, :], scalar=0.3, in1=X[:, t, :],
                                         op0=ALU.mult, op1=ALU.add).then_inc(scaled, 1)


GROUPS1 = 2


def phase_xattn1(nc, X, ident, ctxT, Wq, Wk, Wv, Wo, bq, bk, bv, bo, mask8):
    with ExitStack() as ctx:
        m = Scope(nc, ctx, "xa1")
        ctx_sb = m.sb("ctx", [P, 2, BATCH * CTX])
        wq, wk, wv, wo = (m.sb(n, [P, 2, DIM]) for n in ("wq", "wk", "wv", "wo"))
        bq_sb, bk_sb, bv_sb = (m.sb(n, [P, GROUPS1]) for n in ("bq", "bk", "bv"))
        bo_sb = m.sb("bo", [P, DIM])
        mask = m.sb("mask", [P, GH])
        kblk = m.sb("kblk", [P, BATCH, GROUPS1, HJ])
        vT = m.sb("vT", [P, BATCH, GROUPS1, HJ])
        vblk = m.sb("vblk", [P, BATCH, GROUPS1, HJT, P])
        stats, mv = m.sb("stats", [P, TILES, 6]), m.sb("mv", [P, TILES, 2])
        root, rstd = m.sb("root", [P, TILES]), m.sb("rstd", [P, TILES])
        xn = m.sb("xn", [P, 2, DIM])
        xT = m.sb("xT", [P, 2, KD, P])
        qT = m.sb("qT", [P, 2, GROUPS1, P])
        mx, sm, rc = (m.sb(n, [P, 2, GROUPS1, GH]) for n in ("mx", "sm", "rc"))
        pr = m.sb("pr", [P, 2, GROUPS1, HJ])
        pT = m.sb("pT", [P, 2, GROUPS1, HJT, P])
        aT = m.sb("aT", [P, 2, GROUPS1, P])
        ps_x = m.ps("ps_x", [P, 512])
        ps_s = m.ps("ps_s", [P, GROUPS1, 2, 512])
        ps_p = m.ps("ps_p", [P, 2, 512])
        ps_o = m.ps("ps_o", [P, 512])

        w_in = m.sem("w_in")
        prep_pe, prep_dve, prep_act = m.sem("prep_pe"), m.sem("prep_dve"), m.sem("prep_act")
        s_stats, s_var, s_root, s_rstd = m.sem("s_stats"), m.sem("s_var"), m.sem("s_root"), m.sem("s_rstd")
        normed, turned, xT_in, queried, qT_in = (m.sem("normed"), m.sem("turned"), m.sem("xT_in"), m.sem("queried"),
                                                 m.sem("qT_in"))
        pairs = ("scored", "maxed", "shifted", "exped", "summed", "inverted", "weighted", "pturned", "pT_in")
        scored, maxed, shifted, exped, summed, inverted, weighted, pturned, pT_in = (
            [m.sem(f"{n}{g}") for g in range(GROUPS1)] for n in pairs)
        attended, aT_in, projected, biased, added = (m.sem("attended"), m.sem("aT_in"), m.sem("projected"),
                                                     m.sem("biased"), m.sem("added"))
        LOADS = 14
        LAG = 4

        def rows_of(i):
            return P if i < HJT - 1 else HJR

        block = ctx.enter_context(nc.Block())

        @block.sync
        def _(sp):
            sp.dma_start(mask[:, :], mask8).then_inc(w_in, 16)
            for k, (at, rows) in enumerate(((0, P), (P, C2))):
                sp.dma_start(ctx_sb[0:rows, k, :], ctxT[at:at + rows, :]).then_inc(w_in, 16)
                sp.dma_start(wk[0:rows, k, :], Wk[at:at + rows, :]).then_inc(w_in, 16)
                sp.dma_start(wv[0:rows, k, :], Wv[at:at + rows, :]).then_inc(w_in, 16)
            for dst, src in ((bq_sb, bq), (bk_sb, bk), (bv_sb, bv)):
                sp.dma_start(dst[:, :], src).then_inc(w_in, 16)
            for dst, src in ((wq, Wq), (wo, Wo)):
                sp.dma_start(dst[:, :, :], src.rearrange("(k p) n -> p k n", p=P)).then_inc(w_in, 16)
            for n in range(2):
                sp.dma_start(bo_sb[64 * n:64 * (n + 1), :], bo.partition_broadcast(64)).then_inc(w_in, 16)

        @block.tensor
        def _(pe):
            pe.wait_ge(w_in, 16 * LOADS)
            for n, w in enumerate((wk, wv)):
                for g in range(GROUPS1):
                    for k, rows in enumerate((P, C2)):
                        mm = pe.matmul(ps_s[:, n, g, 0:BATCH * CTX], w[0:rows, k, g * P:(g + 1) * P],
                                       ctx_sb[0:rows, k, :], start=k == 0, stop=k == 1)
                    mm.then_inc(prep_pe, 1)
            pe.wait_ge(prep_dve, 2 * BATCH * GROUPS1)
            n = 0
            for b in range(BATCH):
                for g in range(GROUPS1):
                    if n:
                        pe.wait_ge(prep_act, n)
                    for i in range(HJT):
                        rows = rows_of(i)
                        mm = pe.transpose(ps_p[0:rows, i // 4, (i % 4) * P:(i % 4 + 1) * P],
                                          vT[:, b, g, i * P:i * P + rows], ident[:, :])
                    mm.then_inc(prep_pe, 1)
                    n += 1
            pe.wait_ge(prep_act, n)
            for s in (turned, queried, *scored, *pturned, attended, projected):
                pe.sem_inc(s, LEAD)

            def turn_p(t, s, g):
                pe.wait_ge(weighted[g], has(t))
                pe.wait_ge(pT_in[1 - g], one_ago(t) if g == 0 else has(t))
                for j in range(HJT):
                    rows = rows_of(j)
                    mm = pe.transpose(ps_p[0:rows, j // 4, (j % 4) * P:(j % 4 + 1) * P],
                                      pr[:, s, g, j * P:j * P + rows], ident[:, :])
                mm.then_inc(pturned[g], 1)

            def turn(i, par):
                if live(i):
                    t = i
                    pe.wait_ge(normed, has(t))
                    pe.wait_ge(qT_in, one_ago(t))
                    for k in range(KD):
                        mm = pe.transpose(ps_x[:, k * P:(k + 1) * P], xn[:, par, k * P:(k + 1) * P], ident[:, :])
                    mm.then_inc(turned, 1)
                if live(i - 3):
                    turn_p(i - 3, 1 - par, 0)
                if live(i - 4):
                    t, s = i - 4, par
                    pe.wait_ge(pT_in[1], has(t))
                    pe.wait_ge(added, one_ago(t))
                    for g in range(GROUPS1):
                        for j in range(HJT):
                            rows = rows_of(j)
                            mm = pe.matmul(ps_o[:, g * P:(g + 1) * P], vblk[0:rows, s, g, j, :],
                                           pT[0:rows, s, g, j, :], start=j == 0, stop=j == HJT - 1)
                    mm.then_inc(attended, 1)
                if live(i - 1):
                    t, s = i - 1, 1 - par
                    pe.wait_ge(qT_in, has(t))
                    for g in range(GROUPS1):
                        pe.wait_ge(shifted[g], one_ago(t))
                        for half in range(2):
                            mm = pe.matmul(ps_s[:, g, half, 0:HALF], qT[:, s, g, :],
                                           kblk[:, s, g, half * HALF:(half + 1) * HALF], start=True, stop=True)
                        mm.then_inc(scored[g], 1)
                if live(i):
                    t = i
                    pe.wait_ge(xT_in, has(t))
                    for g in range(GROUPS1):
                        for k in range(KD):
                            mm = pe.matmul(ps_x[:, g * P:(g + 1) * P], wq[:, k, g * P:(g + 1) * P], xT[:, par, k, :],
                                           start=k == 0, stop=k == KD - 1)
                    mm.then_inc(queried, 1)
                if live(i - 3):
                    turn_p(i - 3, 1 - par, 1)
                if live(i - 4):
                    t, s = i - 4, par
                    pe.wait_ge(aT_in, has(t))
                    for g in range(GROUPS1):
                        mm = pe.matmul(ps_o[:, DIM:2 * DIM], aT[:, s, g, :], wo[:, g, :], start=g == 0,
                                       stop=g == GROUPS1 - 1)
                    mm.then_inc(projected, 1)

            turns(pe, LAG, turn)

        @block.vector
        def _(dve):
            dve.wait_ge(w_in, 16 * LOADS)
            for n, (dst, bias) in enumerate(((kblk, bk_sb), (vT, bv_sb))):
                dve.wait_ge(prep_pe, 2 * (n + 1))
                for b in range(BATCH):
                    for g in range(GROUPS1):
                        dve.scalar_tensor_tensor(
                            out=dst[:, b, g, :].rearrange("p (h j) -> p h j", h=GH),
                            in0=ps_s[:, n, g, b * CTX:(b + 1) * CTX].unsqueeze(1).to_broadcast([P, GH, CTX]),
                            scalar=bias[:, g:g + 1], in1=mask[:, :].unsqueeze(2).to_broadcast([P, GH, CTX]),
                            op0=ALU.add, op1=ALU.mult).then_inc(prep_dve, 1)
            norm_stats(dve, s_root, X, stats, mv, root, rstd, s_stats, s_var, s_rstd)
            for s in (normed, *maxed, *shifted, *summed, *inverted, added):
                dve.sem_inc(s, LEAD)

            def turn(i, par):
                if live(i):
                    t = i
                    dve.wait_ge(turned, two_ago(t))
                    x = tile_of(t, par)
                    dve.tensor_scalar(xn[:, par, :], X[:, x, :], mv[:, x, 0:1], rstd[:, bass.ds(x, 1)],
                                      ALU.subtract, ALU.mult).then_inc(normed, 1)
                if live(i - 2):
                    t, s = i - 2, par
                    for g in range(GROUPS1):
                        dve.wait_ge(exped[g], has(t))
                        dve.wait_ge(weighted[g], two_ago(t))
                        dve.tensor_reduce(sm[:, s, g, :], pr[:, s, g, :].rearrange("p (h j) -> p h j", j=CTX), AX.X,
                                          ALU.add).then_inc(summed[g], 1)
                        dve.wait_ge(summed[g], has(t))
                        dve.reciprocal(rc[:, s, g, :], sm[:, s, g, :]).then_inc(inverted[g], 1)
                if live(i - 1):
                    t, s = i - 1, 1 - par
                    for g in range(GROUPS1):
                        dve.wait_ge(scored[g], has(t))
                        src = ps_s[:, g, :, 0:HALF].rearrange("p a (h j) -> p a h j", j=CTX)
                        dve.tensor_reduce(mx[:, s, g, :].rearrange("p (a h) -> p a h", a=2), src, AX.X,
                                          ALU.max).then_inc(maxed[g], 1)
                        dve.wait_ge(maxed[g], has(t))
                        dve.wait_ge(pturned[g], two_ago(t))
                        dve.tensor_tensor(pr[:, s, g, :].rearrange("p (a h j) -> p a h j", a=2, j=CTX), src,
                                          mx[:, s, g, :].rearrange("p (a h) -> p a h", a=2).unsqueeze(3)
                                          .to_broadcast([P, 2, GH // 2, CTX]), ALU.subtract).then_inc(shifted[g], 1)
                if live(i - 4):
                    t = i - 4
                    dve.wait_ge(projected, has(t))
                    dve.wait_ge(biased, has(t))
                    x = tile_of(t, par)
                    dve.tensor_tensor(X[:, x, :], ps_o[:, DIM:2 * DIM], X[:, x, :], ALU.add).then_inc(added, 1)

            turns(dve, LAG, turn)

        @block.gpsimd
        def _(pool):
            for s in (*weighted, biased):
                pool.sem_inc(s, LEAD)
            pool.wait_ge(w_in, 16 * LOADS)

            def turn(i, par):
                if live(i - 2):
                    t, s = i - 2, par
                    for g in range(GROUPS1):
                        pool.wait_ge(inverted[g], has(t))
                        v = pr[:, s, g, :].rearrange("p (h j) -> p h j", j=CTX)
                        pool.tensor_tensor(v, v, rc[:, s, g, :].unsqueeze(2).to_broadcast([P, GH, CTX]),
                                           ALU.mult).then_inc(weighted[g], 1)
                if live(i - 1):
                    t = i - 1
                    pool.wait_ge(normed, has(t))
                    x = tile_of(t, 1 - par)
                    pool.tensor_tensor(X[:, x, :], X[:, x, :], bo_sb[:, :], ALU.add).then_inc(biased, 1)

            turns(pool, LAG, turn)

        @block.scalar
        def _(act):
            n = 0
            for b in range(BATCH):
                for g in range(GROUPS1):
                    act.wait_ge(prep_pe, 5 + n)
                    act.activation(vblk[:, b, g, 0:4, :].rearrange("p k n -> p (k n)"), ps_p[:, 0, :], ACT.Copy)
                    act.activation(vblk[0:HJR, b, g, 4, :], ps_p[0:HJR, 1, 0:P], ACT.Copy).then_inc(prep_act, 1)
                    n += 1
            act.wait_ge(s_var, 1)
            act.activation(root[:, :], root[:, :], ACT.Sqrt).then_inc(s_root, 1)
            for s in (xT_in, qT_in, *exped, *pT_in, aT_in):
                act.sem_inc(s, LEAD)

            def copy_p(t, s, g):
                act.wait_ge(pturned[g], has(t))
                act.wait_ge(attended, two_ago(t))
                act.activation(pT[:, s, g, 0:4, :].rearrange("p k n -> p (k n)"), ps_p[:, 0, :], ACT.Copy)
                act.activation(pT[0:HJR, s, g, 4, :], ps_p[0:HJR, 1, 0:P], ACT.Copy).then_inc(pT_in[g], 1)

            def exps(t, s, g):
                act.wait_ge(shifted[g], has(t))
                act.activation(pr[:, s, g, :], pr[:, s, g, :], ACT.Exp, scale=0.25).then_inc(exped[g], 1)

            def turn(i, par):
                if live(i):
                    t = i
                    act.wait_ge(turned, has(t))
                    act.wait_ge(queried, two_ago(t))
                    act.activation(xT[:, par, :, :].rearrange("p k n -> p (k n)"), ps_x[:, 0:DIM],
                                   ACT.Copy).then_inc(xT_in, 1)
                if live(i - 3):
                    copy_p(i - 3, 1 - par, 0)
                if live(i - 4):
                    t, s = i - 4, par
                    act.wait_ge(attended, has(t))
                    act.wait_ge(projected, two_ago(t))
                    act.activation(aT[:, s, :, :].rearrange("p k n -> p (k n)"), ps_o[:, 0:DIM], ACT.Copy).then_inc(aT_in, 1)
                if live(i - 1):
                    exps(i - 1, 1 - par, 0)
                if live(i):
                    t = i
                    act.wait_ge(queried, has(t))
                    act.wait_ge(scored[1], two_ago(t))
                    act.activation(qT[:, par, 0, :], ps_x[:, 0:P], ACT.Identity, bias=bq_sb[:, 0:1])
                    act.activation(qT[:, par, 1, :], ps_x[:, P:2 * P], ACT.Identity, bias=bq_sb[:, 1:2]).then_inc(qT_in, 1)
                if live(i - 1):
                    exps(i - 1, 1 - par, 1)
                if live(i - 3):
                    copy_p(i - 3, 1 - par, 1)

            turns(act, LAG, turn)


HID = 1024
KH = HID // P
ROUND = 12582912.0


def phase_ffn(nc, X, ident, identb, out, w1T, w2T, b1, b2, g1, n1, g2, n2):
    with ExitStack() as ctx:
        m = Scope(nc, ctx, "ffn")
        raw = m.sb("raw", [P, 2, 2048])
        wq = m.sb("wq", [P, 2, 2048], BF16)
        w1q = wq[:, 0, :].rearrange("p (k n) -> p k n", k=KD)
        w2q = wq[:, 1, :].rearrange("p (k n) -> p k n", k=KH)
        ones = m.sb("ones", [P, P])
        wsum, wmean, winv, wfac = m.sb("wsum", [P, 2]), m.sb("wmean", [P, 2]), m.sb("winv", [P, 2]), m.sb("wfac", [P, 2])
        b1_sb, g2_sb, n2_sb = m.sb("b1", [P, HID]), m.sb("g2", [P, HID]), m.sb("n2", [P, HID])
        b2_sb, g1_sb, n1_sb = m.sb("b2", [P, DIM]), m.sb("g1", [P, DIM]), m.sb("n1", [P, DIM])
        stats, mv = m.sb("stats", [P, TILES, 6]), m.sb("mv", [P, TILES, 2])
        root, rstd = m.sb("root", [P, TILES]), m.sb("rstd", [P, TILES])
        stats2, mv2 = m.sb("stats2", [P, TILES, 12]), m.sb("mv2", [P, TILES, 2])
        root2, rstd2 = m.sb("root2", [P, TILES]), m.sb("rstd2", [P, TILES])
        G = m.sb("G", [P, TILES, HID])
        h = m.sb("h", [P, 2, HID])
        q = m.sb("q", [P, 2, HID], BF16)
        qT = m.sb("qT", [P, 2, HID], BF16)
        y = m.sb("y", [P, 2, HID])
        amax, ainv, fac = m.sb("amax", [P, TILES]), m.sb("ainv", [P, TILES]), m.sb("fac", [P, TILES])
        ps_t = m.ps("ps_t", [P, 2, 1024], BF16)
        ps_y = m.ps("ps_y", [P, 2, HID])
        ps_w = m.ps("ps_w", [P, 512])

        w_in, v_in = m.sem("w_in"), m.sem("v_in")
        w_abs, w_sum, w_chain, w_rounded = m.sem("w_abs"), m.sem("w_sum"), m.sem("w_chain"), m.sem("w_rounded")
        s_stats, s_var, s_root, s_rstd = m.sem("s_stats"), m.sem("s_var"), m.sem("s_root"), m.sem("s_rstd")
        s_stats2, s_var2, s_root2, s_rstd2 = m.sem("s_stats2"), m.sem("s_var2"), m.sem("s_root2"), m.sem("s_rstd2")
        names = ("quant", "scaled", "rounded", "turned", "qT_in", "made", "used")
        first = {n: m.sem(f"first_{n}") for n in names + ("gelued",)}
        second = {n: m.sem(f"second_{n}") for n in names}
        biased, stored = m.sem("biased"), m.sem("stored")
        LAG = 4
        VLOADS = 12

        block = ctx.enter_context(nc.Block())

        @block.sync
        def _(sp):
            sp.dma_start(raw[:, 0, :].rearrange("p (k n) -> p k n", k=KD), w1T.rearrange("(k p) n -> p k n", p=P)).then_inc(w_in, 16)
            sp.dma_start(raw[:, 1, :].rearrange("p (k n) -> p k n", k=KH), w2T.rearrange("(k p) n -> p k n", p=P)).then_inc(w_in, 16)
            for dst, src in ((g1_sb, g1), (n1_sb, n1), (b1_sb, b1), (g2_sb, g2), (n2_sb, n2), (b2_sb, b2)):
                for n in range(2):
                    sp.dma_start(dst[64 * n:64 * (n + 1), :], src.partition_broadcast(64)).then_inc(v_in, 16)
            for t in range(0, TILES, 4):
                sp.wait_ge(second["used"], LEAD + t + 4)
                sp.dma_start(out[t * P:(t + 4) * P, :].rearrange("(t p) d -> p t d", p=P), X[:, t:t + 4, :]).then_inc(stored, 16)
            sp.wait_ge(stored, 16 * TILES // 4)

        @block.gpsimd
        def _(pool):
            pool.memset(ones[:, :], 1.0).then_inc(w_abs, 1)
            pool.wait_ge(v_in, 16 * VLOADS)
            pool.wait_ge(first["quant"], LEAD + 2 * TILES)
            for t in range(TILES):
                pool.tensor_tensor(X[:, t, :], X[:, t, :], b2_sb[:, :], ALU.add).then_inc(biased, 1)

        @block.tensor
        def _(pe):
            pe.wait_ge(w_abs, 3)
            pe.matmul(ps_w[:, 0:2], ones[:, :], wsum[:, :], start=True, stop=True).then_inc(w_sum, 1)
            for sems in (first, second):
                for n in ("turned", "made"):
                    pe.sem_inc(sems[n], LEAD)
            pe.wait_ge(w_rounded, 2)

            def layer(sems, kin, width, w):
                def turn(i, par):
                    if live(i - 1):
                        t, s = i - 1, 1 - par
                        pe.wait_ge(sems["rounded"], has(t))
                        pe.wait_ge(sems["qT_in"], two_ago(t))
                        for k in range(kin):
                            mm = pe.transpose(ps_t[:, s, k * P:(k + 1) * P], q[:, s, k * P:(k + 1) * P], identb[:, :])
                        mm.then_inc(sems["turned"], 1)
                    if live(i - 2):
                        t, s = i - 2, par
                        pe.wait_ge(sems["qT_in"], has(t))
                        pe.wait_ge(sems["used"], two_ago(t))
                        for half in range((width + 511) // 512):
                            n = min(512, width)
                            for k in range(kin):
                                mm = pe.matmul(ps_y[:, s, half * n:(half + 1) * n], qT[:, s, k * P:(k + 1) * P],
                                               w[:, k, half * n:(half + 1) * n], start=k == 0, stop=k == kin - 1)
                        mm.then_inc(sems["made"], 1)

                turns(pe, LAG, turn)

            layer(first, KD, HID, w1q)
            layer(second, KH, DIM, w2q)

        @block.vector
        def _(dve):
            dve.wait_ge(w_sum, 1)
            dve.tensor_scalar(wmean[:, :], ps_w[:, 0:2], 1.0 / (DIM * HID), 1e-5, ALU.mult, ALU.max).then_inc(w_chain, 1)
            dve.wait_ge(w_chain, 1)
            dve.reciprocal(winv[:, :], wmean[:, :]).then_inc(w_chain, 1)
            dve.tensor_scalar(wfac[:, :], wmean[:, :], 1.0 / 127.0, None, ALU.mult).then_inc(w_chain, 1)
            dve.wait_ge(w_chain, 3)
            for n in range(2):
                dve.tensor_scalar(raw[:, n, :], raw[:, n, :], winv[:, n:n + 1], ROUND, ALU.mult, ALU.add).then_inc(w_chain, 1)
                dve.wait_ge(w_chain, 4 + 2 * n)
                dve.tensor_scalar(raw[:, n, :], raw[:, n, :], ROUND, 1.0, ALU.subtract, ALU.min).then_inc(w_chain, 1)
                dve.wait_ge(w_chain, 5 + 2 * n)
                dve.tensor_scalar(wq[:, n, :], raw[:, n, :], -1.0, None, ALU.max).then_inc(w_rounded, 1)
            norm_stats(dve, s_root, X, stats, mv, root, rstd, s_stats, s_var, s_rstd)
            for sems in (first, second):
                for n in ("quant", "scaled", "used"):
                    dve.sem_inc(sems[n], LEAD)
            dve.wait_ge(v_in, 16 * VLOADS)

            def quantise(sems, t, s, x, width, mean, rst, gain, shift, wn):
                col = bass.ds(t, 1)
                dve.wait_ge(sems["rounded"], two_ago(t))
                hs = h[:, s, 0:width]
                dve.scalar_tensor_tensor(out=hs, in0=x, scalar=mean[:, t, 0:1], in1=gain[:, 0:width],
                                         op0=ALU.subtract, op1=ALU.mult).then_inc(sems["quant"], 1)
                dve.wait_ge(sems["quant"], LEAD + 2 * t + 1)
                dve.scalar_tensor_tensor(out=hs, in0=hs, scalar=rst[:, col], in1=shift[:, 0:width],
                                         op0=ALU.mult, op1=ALU.add).then_inc(sems["quant"], 1)
                dve.wait_ge(sems["quant"], LEAD + 2 * t + 2)
                dve.tensor_reduce(amax[:, col], hs, AX.X, ALU.max, apply_absolute_value=True).then_inc(sems["scaled"], 1)
                dve.wait_ge(sems["scaled"], LEAD + 6 * t + 1)
                dve.tensor_scalar(amax[:, col], amax[:, col], 1e-5, None, ALU.max).then_inc(sems["scaled"], 1)
                dve.wait_ge(sems["scaled"], LEAD + 6 * t + 2)
                dve.reciprocal(ainv[:, col], amax[:, col]).then_inc(sems["scaled"], 1)
                dve.tensor_scalar(fac[:, col], amax[:, col], wfac[:, wn:wn + 1], None, ALU.mult).then_inc(sems["scaled"], 1)
                dve.wait_ge(sems["scaled"], LEAD + 6 * t + 4)
                dve.tensor_scalar(hs, hs, ainv[:, col], 127.0, ALU.mult, ALU.mult).then_inc(sems["scaled"], 1)
                dve.wait_ge(sems["scaled"], LEAD + 6 * t + 5)
                dve.tensor_scalar(hs, hs, 127.0, ROUND, ALU.min, ALU.add).then_inc(sems["scaled"], 1)

            def turn1(i, par):
                if live(i):
                    quantise(first, i, par, X[:, i, :], DIM, mv, rstd, g1_sb, n1_sb, 0)
                if live(i - 3):
                    t, s = i - 3, 1 - par
                    dve.wait_ge(first["made"], has(t))
                    dve.wait_ge(first["gelued"], two_ago(t))
                    dve.scalar_tensor_tensor(out=y[:, s, :], in0=ps_y[:, s, :], scalar=fac[:, bass.ds(t, 1)],
                                             in1=b1_sb[:, :], op0=ALU.mult, op1=ALU.add).then_inc(first["used"], 1)
                if live(i - 4):
                    t = i - 4
                    dve.wait_ge(first["gelued"], has(t))
                    for n in range(2):
                        dve.bn_stats(stats2[:, t, 6 * n:6 * n + 6], G[:, t, n * 512:(n + 1) * 512]).then_inc(s_stats2, 1)

            turns(dve, LAG, turn1)
            dve.wait_ge(s_stats2, 2 * TILES)
            for t in range(TILES):
                dve.bn_aggr(mv2[:, t, :], stats2[:, t, :]).then_inc(s_stats2, 1)
            dve.wait_ge(s_stats2, 3 * TILES)
            dve.tensor_scalar(root2[:, :], mv2[:, :, 1], EPS, None, ALU.add).then_inc(s_var2, 1)
            dve.wait_ge(s_root2, 1)
            dve.reciprocal(rstd2[:, :], root2[:, :]).then_inc(s_rstd2, 1)
            dve.wait_ge(s_rstd2, 1)

            def turn2(i, par):
                if live(i):
                    quantise(second, i, par, G[:, i, :], HID, mv2, rstd2, g2_sb, n2_sb, 1)
                if live(i - 3):
                    t, s = i - 3, 1 - par
                    dve.wait_ge(second["made"], has(t))
                    dve.wait_ge(biased, TILES)
                    dve.scalar_tensor_tensor(out=X[:, t, :], in0=ps_y[:, s, 0:DIM], scalar=fac[:, bass.ds(t, 1)],
                                             in1=X[:, t, :], op0=ALU.mult, op1=ALU.add).then_inc(second["used"], 1)

            turns(dve, LAG, turn2)

        @block.scalar
        def _(act):
            act.wait_ge(w_in, 32)
            for n in range(2):
                act.activation(G[:, 2 * n:2 * n + 2, :].rearrange("p t n -> p (t n)"), raw[:, n, :], ACT.Abs, accum_out=wsum[:, n:n + 1]).then_inc(w_abs, 1)
            act.wait_ge(s_var, 1)
            act.activation(root[:, :], root[:, :], ACT.Sqrt).then_inc(s_root, 1)
            for sems in (first, second):
                for n in ("rounded", "qT_in"):
                    act.sem_inc(sems[n], LEAD)
            act.sem_inc(first["gelued"], LEAD)

            def layer(sems, width, gelu):
                def turn(i, par):
                    if live(i):
                        t, s = i, par
                        act.wait_ge(sems["scaled"], LEAD + 6 * t + 6)
                        act.wait_ge(sems["turned"], two_ago(t))
                        act.activation(q[:, s, 0:width], h[:, s, 0:width], ACT.Copy, bias=-ROUND).then_inc(sems["rounded"], 1)
                    if live(i - 1):
                        t, s = i - 1, 1 - par
                        act.wait_ge(sems["turned"], has(t))
                        act.wait_ge(sems["made"], two_ago(t))
                        act.activation(qT[:, s, 0:width], ps_t[:, s, 0:width], ACT.Copy).then_inc(sems["qT_in"], 1)
                    if gelu and live(i - 3):
                        t, s = i - 3, 1 - par
                        act.wait_ge(sems["used"], has(t))
                        act.activation(G[:, t, :], y[:, s, :], ACT.Gelu).then_inc(sems["gelued"], 1)

                turns(act, LAG, turn)

            layer(first, DIM, True)
            act.wait_ge(s_var2, 1)
            act.activation(root2[:, :], root2[:, :], ACT.Sqrt).then_inc(s_root2, 1)
            layer(second, HID, False)


def program(nc, a, out):
    with ExitStack() as ctx:
        X = ctx.enter_context(nc.sbuf_tensor("X", [P, TILES, DIM], F32))
        ident = ctx.enter_context(nc.sbuf_tensor("ident", [P, P], F32))
        identb = ctx.enter_context(nc.sbuf_tensor("identb", [P, P], BF16))
        x_loaded = ctx.enter_context(nc.semaphore("x_loaded"))
        phase_xattn0(nc, X, ident, x_loaded, a["x"], a["ctxT"], a["WqT0"], a["Wk0"], a["Wv0"], a["Wo0"], a["bo0"],
                     a["mask2"], a["ident"])
        qkd = nc.dram_tensor("qk_parts", (2, PARTS, BATCH * P, SEQ), BF16).ap()
        aon = nc.dram_tensor("attn_sums", (BATCH * P, SEQ), F32).ap()
        aod = nc.dram_tensor("attn_weights", (BATCH * HEADS, SEQ), F32).ap()
        with ExitStack() as attn:
            V = attn.enter_context(nc.sbuf_tensor("V", [P, GROUPS, KT, GROWS], F32))
            phase_qkv(nc, X, ident, V, qkd, a["Wq"], a["Wk"], a["Wv"], a["qb"], a["kb"], a["vb"])
            phase_attention(nc, ident, identb, V, qkd, aon, aod)
        with ExitStack() as moe:
            mla_hi = moe.enter_context(nc.sbuf_tensor("mla_hi", [P, KD, BATCH * SEQ], F32R))
            mla_lo = moe.enter_context(nc.sbuf_tensor("mla_lo", [P, KD, BATCH * SEQ], F32R))
            combine = moe.enter_context(nc.sbuf_tensor("combine", [P, TILES, EXPERTS], F32))
            acc = moe.enter_context(nc.sbuf_tensor("acc", [P, TILES, DIM], F32))
            phase_router(nc, ident, mla_hi, mla_lo, combine, acc, aon, aod, a["ow"], a["ob"], a["rw"], a["rb"],
                         a["b2"], a["iota"])
            phase_experts(nc, X, mla_hi, mla_lo, combine, acc, a["w1"], a["b1"], a["w2"])
        phase_xattn1(nc, X, ident, a["ctxT"], a["Wq1"], a["Wk1"], a["Wv1"], a["Wo1"], a["bq1"], a["bk1"], a["bv1"],
                     a["bo1"], a["mask8"])
        phase_ffn(nc, X, ident, identb, out, a["f1T"], a["f2T"], a["fb1"], a["fb2"], a["g1"], a["n1"], a["g2"], a["n2"])


def layout(inputs):
    import numpy as np

    g = {k: np.asarray(v) for k, v in inputs.items()}
    c = np.ascontiguousarray
    kv1 = g["L1_xattn_Wkv"].reshape(16, 2, 16, CDIM)
    bkv1 = g["L1_xattn_bkv"].reshape(16, 2, 16)
    a = {
        "x": c(g["x"].reshape(-1, DIM)),
        "ctxT": c(g["ctx_768"].reshape(-1, CDIM).T),
        "WqT0": c(g["L0_xattn_Wq"].T), "Wk0": g["L0_xattn_Wk"], "Wv0": g["L0_xattn_Wv"],
        "Wo0": g["L0_xattn_Wo"], "bo0": g["L0_xattn_bo"],
        "ident": np.eye(P, dtype=np.float32),
        "Wq": g["L0_ffn_q_w"].reshape(DIM, HEADS, 2 * HD)[:, :, :HD].reshape(DIM, P),
        "qb": g["L0_ffn_q_b"].reshape(HEADS, 2 * HD)[:, :HD].reshape(P, 1),
        "Wk": g["L0_ffn_k_w"], "kb": g["L0_ffn_k_b"].reshape(P, 1),
        "Wv": g["L0_ffn_v_w"], "vb": g["L0_ffn_v_b"],
        "ow": g["L0_ffn_o_w"][:P], "ob": g["L0_ffn_o_b"].reshape(KD, P).T,
        "rw": g["L0_ffn_router_w"], "rb": g["L0_ffn_router_b"], "b2": g["L0_ffn_b2"],
        "iota": np.tile(np.arange(EXPERTS, dtype=np.float32), (P, 1)),
        "w1": g["L0_ffn_w1"], "w2": g["L0_ffn_w2"], "b1": g["L0_ffn_b1"].reshape(EXPERTS, FT, P).transpose(0, 2, 1),
        "Wq1": g["L1_xattn_Wq"].T, "Wo1": g["L1_xattn_Wo"].T,
        "Wk1": kv1[:, 0].reshape(DIM, CDIM).T, "Wv1": kv1[:, 1].reshape(DIM, CDIM).T,
        "bq1": g["L1_xattn_bq"].reshape(GROUPS1, P).T, "bo1": g["L1_xattn_bo"],
        "bk1": bkv1[:, 0].reshape(GROUPS1, P).T, "bv1": bkv1[:, 1].reshape(GROUPS1, P).T,
        "f1T": g["L1_ffn_w1"].T, "f2T": g["L1_ffn_w2"].T, "fb1": g["L1_ffn_b1"], "fb2": g["L1_ffn_b2"],
        "g1": g["L1_ffn_ln1_g"], "n1": g["L1_ffn_ln1_b"], "g2": g["L1_ffn_ln2_g"], "n2": g["L1_ffn_ln2_b"],
        "mask8": np.repeat(np.eye(GH, dtype=np.float32), P // GH, axis=0),
        "mask2": np.repeat(np.eye(2, dtype=np.float32), 64, axis=0),
    }
    return {k: c(v) for k, v in a.items()}


def kernel(**inputs):
    import concourse.bacc as bacc
    from concourse.bass_utils import run_bass_kernel_spmd

    nc = bacc.Bacc("TRN2", target_bir_lowering=False, num_devices=1)
    arrays = layout(inputs)
    a = {k: nc.dram_tensor(k + "_dram", v.shape, mybir.dt.from_np(v.dtype), kind="ExternalInput").ap()
         for k, v in arrays.items()}
    out = nc.dram_tensor("out_dram", (BATCH * SEQ, DIM), F32, kind="ExternalOutput").ap()
    program(nc, a, out)
    r = run_bass_kernel_spmd(nc, [{k + "_dram": v for k, v in arrays.items()}], core_ids=[0])
    return r.results[0]["out_dram"].reshape(BATCH, SEQ, DIM)
```

```python
from contextlib import ExitStack

import concourse.bass as bass
from concourse import mybir

F32 = mybir.dt.float32
F32R = mybir.dt.float32r
BF16 = mybir.dt.bfloat16
U32 = mybir.dt.uint32
ALU = mybir.AluOpType
ACT = mybir.ActivationFunctionType
AX = mybir.AxisListType

P = 128
BATCH, SEQ, DIM = 2, 1024, 256
TILES = BATCH * SEQ // P
PAIRS = TILES // 2
TILES_PER_BATCH = SEQ // P
KD = DIM // P
CTX, CDIM = 77, 192
C2 = CDIM - P
EPS = 1e-5

GH = 8
HJ = GH * CTX
HALF = HJ // 2
HJT = (HJ + P - 1) // P
HJR = HJ - (HJT - 1) * P


class Scope:

    def __init__(self, nc, ctx, tag):
        self.nc, self.ctx, self.tag, self.sems = nc, ctx, tag, []
        ctx.callback(self.clear)

    def sb(self, name, shape, dt=F32):
        return self.ctx.enter_context(self.nc.sbuf_tensor(f"{self.tag}_{name}", shape, dt))

    def ps(self, name, shape, dt=F32):
        return self.ctx.enter_context(self.nc.psum_tensor(f"{self.tag}_{name}", shape, dt))

    def sem(self, name):
        self.sems.append(self.nc.alloc_semaphore(f"{self.tag}_{name}"))
        return self.sems[-1]

    def clear(self):
        self.nc.clear_and_free_semaphores(self.sems)
        self.nc.all_engine_barrier()


LEAD = 3


def has(t):
    return t + 1 + LEAD


def two_ago(t):
    return t - 1 + LEAD


def one_ago(t):
    return t + LEAD


def live(t):
    return not isinstance(t, int) or 0 <= t < TILES


def tile_of(t, parity):
    return parity * TILES_PER_BATCH + t // 2


def turns(eng, lag, turn):
    head = (lag + 1) // 2
    for i in range(2 * head):
        turn(i, i % 2)
    with eng.Fori(head, PAIRS) as pair:
        turn(pair * 2, 0)
        turn(pair * 2 + 1, 1)
    for i in range(TILES, TILES + lag):
        turn(i, i % 2)


def norm_stats(dve, act_done, X, stats, mv, root, rstd, s_stats, s_var, s_rstd):
    for t in range(TILES):
        dve.bn_stats(stats[:, t, :], X[:, t, :]).then_inc(s_stats, 1)
    dve.wait_ge(s_stats, TILES)
    for t in range(TILES):
        dve.bn_aggr(mv[:, t, :], stats[:, t, :]).then_inc(s_stats, 1)
    dve.wait_ge(s_stats, 2 * TILES)
    dve.tensor_scalar(root[:, :], mv[:, :, 1], EPS, None, ALU.add).then_inc(s_var, 1)
    dve.wait_ge(act_done, 1)
    dve.reciprocal(rstd[:, :], root[:, :]).then_inc(s_rstd, 1)
    dve.wait_ge(s_rstd, 1)


def phase_xattn0(nc, X, ident, x_loaded, x, ctxT, WqT, Wk, Wv, Wo, bo, mask2, identd):
    with ExitStack() as ctx:
        m = Scope(nc, ctx, "xa0")
        R = 4
        pair = 2 * CTX
        ctx_sb = m.sb("ctx", [P, 2, BATCH * CTX])
        wqT = m.sb("wqT", [P, R, DIM])
        wk = m.sb("wk", [P, 2, 512])
        wv = m.sb("wv", [P, 2, 512])
        wo = m.sb("wo", [P, R, DIM])
        bo_sb = m.sb("bo", [P, DIM])
        mask = m.sb("mask", [P, 2])
        kblk = m.sb("kblk", [P, BATCH, R, pair])
        vblk = m.sb("vblk", [P, BATCH, R, HJ])
        G = m.sb("G", [P, BATCH, KD, HJ])
        U = m.sb("U", [P, BATCH, HJT, DIM])
        stats = m.sb("stats", [P, TILES, 6])
        mv = m.sb("mv", [P, TILES, 2])
        root = m.sb("root", [P, TILES])
        rstd = m.sb("rstd", [P, TILES])
        xn = m.sb("xn", [P, 2, DIM])
        xT = m.sb("xT", [P, 2, KD, P])
        mx = m.sb("mx", [P, 2, GH])
        sm = m.sb("sm", [P, 2, GH])
        rc = m.sb("rc", [P, 2, GH])
        pr = m.sb("pr", [P, 2, HJ])
        pT = m.sb("pT", [P, 2, HJT, P])
        ps_x = m.ps("ps_x", [P, 512])
        ps_s = m.ps("ps_s", [P, 2, 2, 512])
        ps_p = m.ps("ps_p", [P, 2, 512])
        ps_o = m.ps("ps_o", [P, 512])

        w_in, zeroed = m.sem("w_in"), m.sem("zeroed")
        prep_pe, prep_dve, prep_act = m.sem("prep_pe"), m.sem("prep_dve"), m.sem("prep_act")
        s_stats, s_var, s_root, s_rstd = m.sem("s_stats"), m.sem("s_var"), m.sem("s_root"), m.sem("s_rstd")
        normed, turned, xT_in = m.sem("normed"), m.sem("turned"), m.sem("xT_in")
        scored, maxed, shifted = m.sem("scored"), m.sem("maxed"), m.sem("shifted")
        exped, summed, inverted, weighted = m.sem("exped"), m.sem("summed"), m.sem("inverted"), m.sem("weighted")
        pturned, pT_in, projected = m.sem("pturned"), m.sem("pT_in"), m.sem("projected")
        biased, added = m.sem("biased"), m.sem("added")

        LOADS = 12
        LAG = 4

        def U_rows(i):
            return P if i < HJT - 1 else HJR

        block = ctx.enter_context(nc.Block())

        @block.sync
        def _(sp):
            sp.dma_start(X[:, :, :], x.rearrange("(t p) d -> p t d", p=P)).then_inc(x_loaded, 16)
            sp.dma_start(ident[:, :], identd).then_inc(w_in, 16)
            sp.dma_start(mask[:, :], mask2).then_inc(w_in, 16)
            for k, (at, rows) in enumerate(((0, P), (P, C2))):
                sp.dma_start(ctx_sb[0:rows, k, :], ctxT[at:at + rows, :]).then_inc(w_in, 16)
                sp.dma_start(wk[0:rows, k, :], Wk[at:at + rows, :]).then_inc(w_in, 16)
                sp.dma_start(wv[0:rows, k, :], Wv[at:at + rows, :]).then_inc(w_in, 16)
            sp.dma_start(wqT[:, :, :], WqT.rearrange("(r p) c -> p r c", p=P)).then_inc(w_in, 16)
            sp.dma_start(wo[:, :, :], Wo.rearrange("(r p) c -> p r c", p=P)).then_inc(w_in, 16)
            sp.dma_start(bo_sb[0:64, :], bo.partition_broadcast(64)).then_inc(w_in, 16)
            sp.dma_start(bo_sb[64:P, :], bo.partition_broadcast(64)).then_inc(w_in, 16)

        @block.tensor
        def _(pe):
            pe.wait_ge(w_in, 16 * LOADS)
            for w, bank0 in ((wk, 0), (wv, 1)):
                for r in range(R):
                    for k, rows in enumerate((P, C2)):
                        mm = pe.matmul(ps_s[:, bank0, r // 2, (r % 2) * pair:(r % 2 + 1) * pair],
                                       w[0:rows, k, r * P:(r + 1) * P], ctx_sb[0:rows, k, :],
                                       start=k == 0, stop=k == 1)
                mm.then_inc(prep_pe, 1)
            for b in range(BATCH):
                for k in range(KD):
                    n = b * KD + k
                    pe.wait_ge(prep_dve, 1)
                    pe.wait_ge(prep_dve, 2)
                    if n >= 2:
                        pe.wait_ge(prep_act, n - 1)
                    for r in range(R):
                        mm = pe.matmul(ps_s[:, n % 2, r // 2, (r % 2) * pair:(r % 2 + 1) * pair],
                                       wqT[:, r, k * P:(k + 1) * P], kblk[:, b, r, :],
                                       start=True, stop=True)
                    mm.then_inc(prep_pe, 1)
            for b in range(BATCH):
                for i in range(HJT):
                    n = b * HJT + i
                    if n >= 1:
                        pe.wait_ge(prep_act, 4 + n)
                    rows = U_rows(i)
                    over = [r for r in range(R) if r * pair < i * P + rows and (r + 1) * pair > i * P]
                    for r in over:
                        mm = pe.matmul(ps_o[0:rows, 0:DIM], vblk[:, b, r, i * P:i * P + rows], wo[:, r, :],
                                       start=r == over[0], stop=r == over[-1])
                    mm.then_inc(prep_pe, 1)

            for s in (turned, scored, pturned, projected):
                pe.sem_inc(s, LEAD)
            pe.wait_ge(prep_act, 4 + 2 * HJT)

            def turn(i, par):
                if live(i - 1):
                    t, s = i - 1, 1 - par
                    pe.wait_ge(xT_in, has(t))
                    pe.wait_ge(shifted, two_ago(t))
                    for half in range(2):
                        for k in range(KD):
                            mm = pe.matmul(ps_s[:, s, half, 0:HALF], xT[:, s, k, :],
                                           G[:, s, k, half * HALF:(half + 1) * HALF],
                                           start=k == 0, stop=k == KD - 1)
                    mm.then_inc(scored, 1)
                if live(i):
                    t = i
                    pe.wait_ge(normed, has(t))
                    pe.wait_ge(xT_in, one_ago(t))
                    for k in range(KD):
                        mm = pe.transpose(ps_x[:, k * P:(k + 1) * P], xn[:, par, k * P:(k + 1) * P], ident[:, :])
                    mm.then_inc(turned, 1)
                if live(i - 3):
                    t, s = i - 3, 1 - par
                    pe.wait_ge(weighted, has(t))
                    pe.wait_ge(pT_in, one_ago(t))
                    for j in range(HJT):
                        rows = U_rows(j)
                        mm = pe.transpose(ps_p[0:rows, j // 4, (j % 4) * P:(j % 4 + 1) * P],
                                          pr[:, s, j * P:j * P + rows], ident[:, :])
                    mm.then_inc(pturned, 1)
                if live(i - 4):
                    t, s = i - 4, par
                    pe.wait_ge(pT_in, has(t))
                    pe.wait_ge(added, one_ago(t))
                    for j in range(HJT):
                        rows = U_rows(j)
                        mm = pe.matmul(ps_o[:, 0:DIM], pT[0:rows, s, j, :], U[0:rows, s, j, :],
                                       start=j == 0, stop=j == HJT - 1)
                    mm.then_inc(projected, 1)

            turns(pe, LAG, turn)

        @block.vector
        def _(dve):
            dve.memset(vblk[:, :, :, :], 0.0).then_inc(zeroed, 1)
            dve.wait_ge(x_loaded, 16)
            norm_stats(dve, s_root, X, stats, mv, root, rstd, s_stats, s_var, s_rstd)
            dve.wait_ge(w_in, 16 * LOADS)
            dve.wait_ge(prep_pe, 1)
            for b in range(BATCH):
                for r in range(R):
                    src = ps_s[:, 0, r // 2, (r % 2) * pair + b * CTX:(r % 2) * pair + (b + 1) * CTX]
                    ins = dve.tensor_tensor(kblk[:, b, r, :].rearrange("p (h j) -> p h j", h=2),
                                            src.unsqueeze(1).to_broadcast([P, 2, CTX]),
                                            mask[:, :].unsqueeze(2).to_broadcast([P, 2, CTX]), ALU.mult)
            ins.then_inc(prep_dve, 1)
            dve.wait_ge(prep_pe, 2)
            dve.wait_ge(zeroed, 1)
            for b in range(BATCH):
                for r in range(R):
                    src = ps_s[:, 1, r // 2, (r % 2) * pair + b * CTX:(r % 2) * pair + (b + 1) * CTX]
                    ins = dve.tensor_tensor(vblk[:, b, r, r * pair:(r + 1) * pair].rearrange("p (h j) -> p h j", h=2),
                                            src.unsqueeze(1).to_broadcast([P, 2, CTX]),
                                            mask[:, :].unsqueeze(2).to_broadcast([P, 2, CTX]), ALU.mult)
            ins.then_inc(prep_dve, 1)

            for s in (normed, maxed, shifted, summed, inverted, added):
                dve.sem_inc(s, LEAD)

            def turn(i, par):
                if live(i):
                    t = i
                    dve.wait_ge(turned, two_ago(t))
                    x = tile_of(t, par)
                    dve.tensor_scalar(xn[:, par, :], X[:, x, :], mv[:, x, 0:1], rstd[:, bass.ds(x, 1)],
                                      ALU.subtract, ALU.mult).then_inc(normed, 1)
                if live(i - 5):
                    t, x = i - 5, tile_of(i - 5, 1 - par)
                    dve.wait_ge(projected, has(t))
                    dve.wait_ge(biased, has(t))
                    dve.tensor_tensor(X[:, x, :], ps_o[:, 0:DIM], X[:, x, :], ALU.add).then_inc(added, 1)
                if live(i - 1):
                    t, s = i - 1, 1 - par
                    dve.wait_ge(scored, has(t))
                    src = ps_s[:, s, :, 0:HALF].rearrange("p a (h j) -> p a h j", j=CTX)
                    dve.tensor_reduce(mx[:, s, :].rearrange("p (a h) -> p a h", a=2), src, AX.X,
                                      ALU.max).then_inc(maxed, 1)
                    dve.wait_ge(maxed, has(t))
                    dve.wait_ge(pturned, two_ago(t))
                    dve.tensor_tensor(pr[:, s, :].rearrange("p (a h j) -> p a h j", a=2, j=CTX), src,
                                      mx[:, s, :].rearrange("p (a h) -> p a h", a=2).unsqueeze(3)
                                      .to_broadcast([P, 2, GH // 2, CTX]), ALU.subtract).then_inc(shifted, 1)
                if live(i - 2):
                    t, s = i - 2, par
                    dve.wait_ge(exped, has(t))
                    dve.wait_ge(weighted, two_ago(t))
                    dve.tensor_reduce(sm[:, s, :], pr[:, s, :].rearrange("p (h j) -> p h j", j=CTX), AX.X,
                                      ALU.add).then_inc(summed, 1)
                    dve.wait_ge(summed, has(t))
                    dve.reciprocal(rc[:, s, :], sm[:, s, :]).then_inc(inverted, 1)

            turns(dve, LAG + 1, turn)

        @block.gpsimd
        def _(pool):
            for s in (weighted, biased):
                pool.sem_inc(s, LEAD)
            pool.wait_ge(w_in, 16 * LOADS)

            def turn(i, par):
                if live(i - 1):
                    t, x = i - 1, tile_of(i - 1, 1 - par)
                    pool.wait_ge(normed, has(t))
                    pool.tensor_tensor(X[:, x, :], X[:, x, :], bo_sb[:, :], ALU.add).then_inc(biased, 1)
                if live(i - 2):
                    t, s = i - 2, par
                    pool.wait_ge(inverted, has(t))
                    v = pr[:, s, :].rearrange("p (h j) -> p h j", j=CTX)
                    pool.tensor_tensor(v, v, rc[:, s, :].unsqueeze(2).to_broadcast([P, GH, CTX]),
                                       ALU.mult).then_inc(weighted, 1)

            turns(pool, LAG, turn)

        @block.scalar
        def _(act):
            act.wait_ge(s_var, 1)
            act.activation(root[:, :], root[:, :], ACT.Sqrt).then_inc(s_root, 1)
            for n in range(BATCH * KD):
                act.wait_ge(prep_pe, 3 + n)
                act.activation(G[:, n // KD, n % KD, :].rearrange("p (a c) -> p a c", a=2),
                               ps_s[:, n % 2, :, 0:HALF], ACT.Copy).then_inc(prep_act, 1)
            for n in range(BATCH * HJT):
                act.wait_ge(prep_pe, 3 + BATCH * KD + n)
                rows = U_rows(n % HJT)
                act.activation(U[0:rows, n // HJT, n % HJT, :], ps_o[0:rows, 0:DIM], ACT.Copy).then_inc(prep_act, 1)
            for s in (xT_in, exped, pT_in):
                act.sem_inc(s, LEAD)

            def turn(i, par):
                if live(i):
                    t = i
                    act.wait_ge(turned, has(t))
                    act.wait_ge(scored, two_ago(t))
                    act.activation(xT[:, par, :, :].rearrange("p k n -> p (k n)"), ps_x[:, 0:DIM],
                                   ACT.Copy).then_inc(xT_in, 1)
                if live(i - 3):
                    t, s = i - 3, 1 - par
                    act.wait_ge(pturned, has(t))
                    act.wait_ge(projected, two_ago(t))
                    act.activation(pT[:, s, 0:4, :].rearrange("p k n -> p (k n)"), ps_p[:, 0, :], ACT.Copy)
                    act.activation(pT[0:HJR, s, 4, :], ps_p[0:HJR, 1, 0:P], ACT.Copy).then_inc(pT_in, 1)
                if live(i - 1):
                    t, s = i - 1, 1 - par
                    act.wait_ge(shifted, has(t))
                    act.activation(pr[:, s, :], pr[:, s, :], ACT.Exp, scale=0.125).then_inc(exped, 1)

            turns(act, LAG, turn)


HEADS, HD = 16, 8
GROUP = 4
GROUPS = BATCH * HEADS // GROUP
GROWS = GROUP * HD
PARTS = 3
TERMS = PARTS * PARTS * HD
MAXROW = 96
KT = SEQ // P
CHUNK = 512
CHUNKS = BATCH * SEQ // CHUNK


SLOTS = 3


class AttentionBuffers:

    def __init__(self, m):
        self.V = m.sb("V", [P, GROUPS, KT, GROWS])
        self.q = m.sb("q", [P, SLOTS, GROUP, SEQ], BF16)
        self.k = m.sb("k", [P, SLOTS, GROUP, SEQ], BF16)
        self.v = m.sb("v", [P, SLOTS, KT, GROUP, 32])
        self.qk_in = [m.sem(f"qk_in{n}") for n in range(SLOTS)]

    def load(self, sp, qkd, g, slot):
        rows = bass.ds(g * GROWS, GROWS)
        for a in range(PARTS):
            at = slice(a * PARTS * HD, (a + 1) * PARTS * HD)
            sp.dma_start(self.q[at, slot, :, :], qkd[0, :, rows, :].rearrange("b (d j) n -> b d (j n)", d=HD)
                         ).then_inc(self.qk_in[slot], 16)
            sp.dma_start(self.k[at, slot, :, :], qkd[1, a, rows, :].rearrange("(d j) n -> d (j n)", d=HD).unsqueeze(0)
                         .to_broadcast([PARTS, HD, GROUP * SEQ])).then_inc(self.qk_in[slot], 16)


def phase_qkv(nc, X, ident, identb, B, qkd, Wq, Wk, Wv, qb, kb, vb):
    with ExitStack() as ctx:
        m = Scope(nc, ctx, "qkv")
        V = B.V
        w = m.sb("w", [P, 3, KD, P])
        qb_sb, kb_sb = m.sb("qb", [P, 1]), m.sb("kb", [P, 1])
        vb_sb = m.sb("vb", [P, P])
        stats, mv = m.sb("stats", [P, TILES, 6]), m.sb("mv", [P, TILES, 2])
        root, rstd = m.sb("root", [P, TILES]), m.sb("rstd", [P, TILES])
        xn = m.sb("xn", [P, 2, 4, DIM])
        xT = m.sb("xT", [P, 2, KD, CHUNK])
        full = m.sb("full", [P, 2, 2, CHUNK])
        part = m.sb("part", [P, 2, 2, PARTS, CHUNK], BF16)
        ps_x = m.ps("ps_x", [P, KD, CHUNK])
        ps_qk = m.ps("ps_qk", [P, 2, 2, CHUNK])
        ps_v = m.ps("ps_v", [P, 4, P])
        w_in = m.sem("w_in")
        s_stats, s_var, s_root, s_rstd = m.sem("s_stats"), m.sem("s_var"), m.sem("s_root"), m.sem("s_rstd")
        normed, turned, xT_in = m.sem("normed"), m.sem("turned"), m.sem("xT_in")
        qk_made, v_made, qk_full, v_in = m.sem("qk_made"), m.sem("v_made"), m.sem("qk_full"), m.sem("v_in")
        split_hi, rest1, split_mid, split_lo = m.sem("split_hi"), m.sem("rest1"), m.sem("split_mid"), m.sem("split_lo")
        fixed = m.sem("fixed")
        residual, stored = m.sem("residual"), [m.sem(f"stored{n}") for n in range(2)]
        LOADS = 7
        STORES = 2
        scale = float(HD) ** -0.5

        block = ctx.enter_context(nc.Block())

        @block.sync
        def _(sp):
            for n, src in enumerate((Wq, Wk, Wv)):
                sp.dma_start(w[:, n, :, :], src.rearrange("(k p) n -> p k n", p=P)).then_inc(w_in, 16)
            sp.dma_start(qb_sb[:, :], qb).then_inc(w_in, 16)
            sp.dma_start(kb_sb[:, :], kb).then_inc(w_in, 16)
            sp.dma_start(vb_sb[0:64, :], vb.partition_broadcast(64)).then_inc(w_in, 16)
            sp.dma_start(vb_sb[64:P, :], vb.partition_broadcast(64)).then_inc(w_in, 16)
            for c in range(CHUNKS):
                s, b, at = c % 2, c // 2, (c % 2) * CHUNK
                sp.wait_ge(split_lo, 2 * c + 2)
                for n in range(2):
                    sp.dma_start(qkd[n, :, b * P:(b + 1) * P, at:at + CHUNK].rearrange("a p n -> p a n"),
                                 part[:, s, n, :, :]).then_inc(stored[s], 16)
                if c == CHUNKS // BATCH:
                    sp.wait_ge(fixed, 4)
                    sp.wait_ge(stored[0], 16 * STORES)
                    sp.wait_ge(stored[1], 16 * STORES)
                    B.load(sp, qkd, 0, 0)
            for s in range(2):
                sp.wait_ge(stored[s], 16 * STORES * CHUNKS // 2)

        @block.tensor
        def _(pe):
            pe.wait_ge(w_in, 16 * LOADS)
            for c in range(CHUNKS):
                s = c % 2
                pe.wait_ge(normed, c + 1)
                if c >= 1:
                    pe.wait_ge(xT_in, c)
                for t in range(4):
                    for k in range(KD):
                        mm = pe.transpose(ps_x[:, k, t * P:(t + 1) * P], xn[:, s, t, k * P:(k + 1) * P], ident[:, :])
                mm.then_inc(turned, 1)
                pe.wait_ge(xT_in, c + 1)
                if c >= 2:
                    pe.wait_ge(qk_full, 2 * (c - 1))
                for n in range(2):
                    for k in range(KD):
                        mm = pe.matmul(ps_qk[:, s, n, :], w[:, n, k, :], xT[:, s, k, :], start=k == 0, stop=k == KD - 1)
                mm.then_inc(qk_made, 1)
                if c >= 1:
                    pe.wait_ge(v_in, c)
                for t in range(4):
                    for k in range(KD):
                        mm = pe.matmul(ps_v[:, t, :], xT[:, s, k, t * P:(t + 1) * P], w[:, 2, k, :],
                                       start=k == 0, stop=k == KD - 1)
                mm.then_inc(v_made, 1)

        @block.vector
        def _(dve):
            norm_stats(dve, s_root, X, stats, mv, root, rstd, s_stats, s_var, s_rstd)

            def norm(c):
                if c >= 2:
                    dve.wait_ge(turned, c - 1)
                    dve.wait_ge(residual, c - 1)
                for t in range(4):
                    n = 4 * c + t
                    ins = dve.tensor_scalar(xn[:, c % 2, t, :], X[:, n, :], mv[:, n, 0:1], rstd[:, n:n + 1],
                                            ALU.subtract, ALU.mult)
                ins.then_inc(normed, 1)

            dve.wait_ge(w_in, 16 * LOADS)
            norm(0)
            for c in range(CHUNKS):
                s = c % 2
                if c + 1 < CHUNKS:
                    norm(c + 1)
                dve.wait_ge(qk_made, c + 1)
                if c >= 2:
                    dve.wait_ge(split_lo, 2 * (c - 1))
                dve.tensor_scalar(full[:, s, 0, :], ps_qk[:, s, 0, :], qb_sb[:, :], scale, ALU.add,
                                  ALU.mult).then_inc(qk_full, 1)
                dve.tensor_scalar(full[:, s, 1, :], ps_qk[:, s, 1, :], kb_sb[:, :], None, ALU.add).then_inc(qk_full, 1)
                dve.wait_ge(v_made, c + 1)
                b = c // 2
                for t in range(4):
                    kt = (c % 2) * 4 + t
                    ins = dve.tensor_tensor(V[:, b * GROUP:(b + 1) * GROUP, kt, :],
                                            ps_v[:, t, :].rearrange("p (g n) -> p g n", g=GROUP),
                                            vb_sb[:, :].rearrange("p (g n) -> p g n", g=GROUP), ALU.add)
                ins.then_inc(v_in, 1)
                dve.wait_ge(split_hi, c + 1)
                dve.tensor_tensor(full[:, s, :, :], full[:, s, :, :], part[:, s, :, 0, :], ALU.subtract).then_inc(rest1, 1)
                dve.wait_ge(split_mid, c + 1)
                for n in range(2):
                    dve.tensor_tensor(part[:, s, n, 2, :], full[:, s, n, :], part[:, s, n, 1, :],
                                      ALU.subtract).then_inc(split_lo, 1)

        @block.gpsimd
        def _(pool):
            k_max = B.k[MAXROW:MAXROW + PARTS, :, :, :]
            rows = (B.q[64:MAXROW, :, :, :].bitcast(F32), 0.0), (B.k[64:MAXROW, :, :, :].bitcast(F32), 0.0), (k_max, -1.0)
            columns = (B.v[:, :, :, :, :], 0.0), (B.v[:, :, :, :, HD:HD + 1], 1.0)
            for n, (dst, value) in enumerate(rows + columns):
                if n:
                    pool.wait_ge(fixed, n)
                pool.memset(dst, value).then_inc(fixed, 1)
            pool.wait_ge(fixed, 5)
            pool.tensor_copy(identb[:, :], ident[:, :]).then_inc(fixed, 1)
            for c in range(CHUNKS):
                pool.wait_ge(normed, c + 1)
                for t in range(4):
                    n = 4 * c + t
                    ins = pool.tensor_tensor(X[:, n, :], X[:, n, :], xn[:, c % 2, t, :], ALU.add)
                ins.then_inc(residual, 1)

        @block.scalar
        def _(act):
            act.wait_ge(s_var, 1)
            act.activation(root[:, :], root[:, :], ACT.Sqrt).then_inc(s_root, 1)
            for c in range(CHUNKS):
                s = c % 2
                act.wait_ge(turned, c + 1)
                if c >= 2:
                    act.wait_ge(v_made, c - 1)
                act.activation(xT[:, s, :, :], ps_x[:, :, :], ACT.Copy).then_inc(xT_in, 1)
                act.wait_ge(qk_full, 2 * c + 2)
                if c >= 2:
                    act.wait_ge(stored[s], 16 * STORES * (c // 2))
                act.activation(part[:, s, :, 0, :], full[:, s, :, :], ACT.Copy).then_inc(split_hi, 1)
                act.wait_ge(rest1, c + 1)
                act.activation(part[:, s, :, 1, :], full[:, s, :, :], ACT.Copy).then_inc(split_mid, 1)


STEPS = BATCH * KT * GROUP
UNITS = STEPS // GROUP
EARLY = 4
AHEAD = 12
BANKS = 3


def first_pass(last):
    items = []
    for j in range(GROUP):
        for n in range(EARLY if j == 0 else 0, 2 * KT):
            if j and n == 8:
                items.append(("turn", j - 1, 0, 0))
            items.append(("score", j, n // 2, n % 2))
    if not last:
        items += [("next", 0, n // 2, n % 2) for n in range(EARLY)]
    return items + [("turn", GROUP - 1, 0, 0)]


CYCLE, LAST_CYCLE = first_pass(False), first_pass(True)
NI = len(CYCLE)


def phase_attention(nc, ident, identb, B, qkd, aon, aod):
    with ExitStack() as ctx:
        m = Scope(nc, ctx, "att")
        q, k, v, qk_in = B.q, B.k, B.v, B.qk_in
        e = m.sb("e", [P, 2, GROUP, 512])
        o = m.sb("o", [P, SLOTS, 2, 512])
        mh = m.sb("mh", [P, 2, 2 * KT])
        mf = m.sb("mf", [P, 2, KT])
        mr = m.sb("mr", [P, 2, KT])
        mp = m.sb("mp", [P, 2, PARTS, KT], BF16)
        mT = m.sb("mT", [PARTS * KT, 2, P], BF16)
        ps_s = m.ps("ps_s", [P, BANKS, 512])
        ps_m = m.ps("ps_m", [P, BANKS, 512])
        ps_o = m.ps("ps_o", [P, 2, 512])

        m_in = [m.sem(f"m_in{n}") for n in range(2)]
        v_in = m.sem("v_in")
        item_made, item_read = m.sem("item_made"), m.sem("item_read")
        m_hi, m_mid, m_parts = m.sem("m_hi"), m.sem("m_mid"), m.sem("m_parts")
        step_made, step_exp, summed, sums_out, stored = (m.sem("step_made"), m.sem("step_exp"), m.sem("summed"),
                                                         m.sem("sums_out"), m.sem("stored"))
        QKL = 2 * PARTS
        OST = GROUP + 1

        def groups(eng, run):
            run(0, 0)
            with eng.Fori(0, (GROUPS - 2) // SLOTS) as i:
                for s in range(SLOTS):
                    run(i * SLOTS + s + 1, (s + 1) % SLOTS)
            run(GROUPS - 1, (GROUPS - 1) % SLOTS)

        def first_group(g):
            return isinstance(g, int) and g == 0

        def last_group(g):
            return isinstance(g, int) and g == GROUPS - 1

        def cycle(g):
            return LAST_CYCLE if last_group(g) else CYCLE

        def items_to(g, n):
            return g * NI + n + EARLY

        def bank(slot, n):
            return (slot * NI + n + EARLY) % BANKS

        block = ctx.enter_context(nc.Block())

        @block.sync
        def _(sp):
            def maxima(g, slot):
                for j in range(GROUP):
                    sp.wait_ge(item_read, items_to(g, cycle(g).index(("turn", j, 0, 0)) + 1) + LEAD)
                    sp.dma_start(q[MAXROW:MAXROW + PARTS, slot, j, :], mT[:, j % 2, :]).then_inc(m_in[j % 2], 16)

            def store(g, slot):
                sp.wait_ge(sums_out, 2 * (g + 1) + LEAD)
                sp.dma_start(aod[bass.ds(g * GROUP, GROUP), :], o[HD:P:32, slot, :, :]).then_inc(stored, 16)
                for j in range(GROUP):
                    sp.dma_start(aon[bass.ds(g * GROWS + j * HD, HD), :],
                                 o[32 * j:32 * j + HD, slot, :, :]).then_inc(stored, 16)

            B.load(sp, qkd, 1, 1)
            maxima(0, 0)
            with sp.Fori(0, (GROUPS - 2) // SLOTS) as i:
                for s in range(SLOTS):
                    g = i * SLOTS + s
                    sp.wait_ge(step_exp, g * STEPS + LEAD)
                    B.load(sp, qkd, g + 2, (s + 2) % SLOTS)
                    maxima(g + 1, (s + 1) % SLOTS)
                    store(g, s)
            maxima(GROUPS - 1, (GROUPS - 1) % SLOTS)
            for g in (GROUPS - 2, GROUPS - 1):
                store(g, g % SLOTS)
            sp.wait_ge(stored, 16 * OST * GROUPS + LEAD)

        @block.tensor
        def _(pe):
            pe.sem_inc(summed, LEAD)

            def score_half(slot, j, t, half, count, b):
                pe.wait_ge(item_read, count - 2 + LEAD)
                pe.matmul(ps_m[:, b, :], q[0:MAXROW, slot, j, t * P:(t + 1) * P],
                          k[0:MAXROW, slot, j, half * 512:(half + 1) * 512], start=True, stop=True).then_inc(item_made, 1)

            def first(g, slot, frm, upto):
                for n in range(frm, upto):
                    what, j, t, half = cycle(g)[n]
                    if what != "turn":
                        if (what, t, half) == ("next", 0, 0):
                            load_wait(g + 1, (slot + 1) % SLOTS)
                        score_half((slot + (what == "next")) % SLOTS, j, t, half, items_to(g, n), bank(slot, n))
                    else:
                        pe.wait_ge(item_read, items_to(g, n) - 2 + LEAD)
                        pe.wait_ge(m_parts, g * GROUP + j + 1)
                        pe.transpose(ps_m[0:PARTS * KT, bank(slot, n), 0:P // 2].bitcast(BF16),
                                     mp[:, j % 2, :, :].rearrange("p a t -> p (a t)"), identb[:, :]).then_inc(item_made, 1)

            def load_wait(g, slot):
                pe.wait_ge(qk_in[slot], 16 * QKL * ((g - slot) // SLOTS + 1))

            def sums(g, slot, w, part):
                kt, half = w // 2, w % 2
                at = slice(part * 256, (part + 1) * 256)
                if part == 0:
                    pe.wait_ge(step_exp, g * STEPS + (w + 1) * GROUP + LEAD)
                    if kt == 0:
                        pe.wait_ge(sums_out, 2 * g - 1 + half + LEAD)
                    if w == 0:
                        pe.wait_ge(v_in, g + 1)
                for j in range(GROUP):
                    mm = pe.matmul(ps_o[32 * j:32 * (j + 1), half, at], v[:, slot, kt, j, :], e[:, w % 2, j, at],
                                   start=kt == part == 0, stop=kt == KT - 1 and part == 1)
                if part == 1:
                    mm.then_inc(summed, 1)

            def unit(g, slot, w, between, before):
                kt, half = w // 2, w % 2
                for j in range(GROUP):
                    u = w * GROUP + j
                    pe.wait_ge(step_exp, g * STEPS + u - 2 + LEAD)
                    pe.matmul(ps_s[:, (slot * STEPS + u) % BANKS, :], k[0:MAXROW + PARTS, slot, j, kt * P:(kt + 1) * P],
                              q[0:MAXROW + PARTS, slot, j, half * 512:(half + 1) * 512],
                              start=True, stop=True).then_inc(step_made, 1)
                    between(j)
                    if j % 2 == 1 and before is not None:
                        sums(*before, j // 2)

            def maxima_wait(g):
                for n in range(2):
                    pe.wait_ge(m_in[n], 16 * (GROUP // 2) * (g + 1))

            load_wait(0, 0)
            for n in range(EARLY):
                score_half(0, 0, n // 2, n % 2, n, n % BANKS)
            first(0, 0, 0, NI)
            first(1, 1, 0, AHEAD)
            maxima_wait(0)
            unit(0, 0, 0, lambda j: None, None)

            def run(g, slot, items, more):
                done = [0]

                def between(at):
                    upto = min(items, (at + 1) * NI // STEPS)
                    one = NI - AHEAD
                    for n in range(done[0], upto):
                        if n < one:
                            first(g + 1, (slot + 1) % SLOTS, AHEAD + n, AHEAD + n + 1)
                        else:
                            first(g + 2, (slot + 2) % SLOTS, n - one, n - one + 1)
                    done[0] = max(upto, done[0])

                for w in range(1, UNITS):
                    unit(g, slot, w, lambda j: between((w - 1) * GROUP + j), (g, slot, w - 1))
                if more:
                    maxima_wait(g + 1)
                    unit(g + 1, (slot + 1) % SLOTS, 0, lambda j: between((UNITS - 1) * GROUP + j), (g, slot, UNITS - 1))

            with pe.Fori(0, (GROUPS - 2) // SLOTS) as i:
                for s in range(SLOTS):
                    run(i * SLOTS + s, s, NI, True)
            run(GROUPS - 2, (GROUPS - 2) % SLOTS, len(LAST_CYCLE) - AHEAD, True)
            run(GROUPS - 1, (GROUPS - 1) % SLOTS, 0, False)
            for part in range(2):
                sums(GROUPS - 1, (GROUPS - 1) % SLOTS, UNITS - 1, part)

        @block.vector
        def _(dve):
            dve.sem_inc(item_read, LEAD)

            def maximum(head, s, t, half, count, b):
                dve.wait_ge(item_made, count + 1)
                if t == half == 0 and not (isinstance(head, int) and head < 2):
                    dve.wait_ge(m_parts, head - 1)
                dve.tensor_reduce(mh[:, s, 2 * t + half:2 * t + half + 1], ps_m[:, b, :], AX.X,
                                  ALU.max).then_inc(item_read, 1)
                if (t, half) == (KT - 1, 1):
                    dve.wait_ge(item_read, count + 1 + LEAD)
                    a, c = (mh[:, s, h:2 * KT:2] for h in range(2))
                    for dst in (mp[:, s, 0, :], mf[:, s, :]):
                        dve.tensor_tensor(dst, a, c, ALU.max).then_inc(m_hi, 1)

            def first(g, slot):
                for n, (what, j, t, half) in enumerate(cycle(g)):
                    if what != "turn":
                        head = g * GROUP + j + (GROUP if what == "next" else 0)
                        maximum(head, j % 2, t, half, items_to(g, n), bank(slot, n))
                    else:
                        dve.wait_ge(item_made, items_to(g, n) + 1)
                        if not (first_group(g) and j < 2):
                            dve.wait_ge(m_in[j % 2], 16 * (g * (GROUP // 2) + j // 2))
                        dve.tensor_copy(mT[:, j % 2, :], ps_m[0:PARTS * KT, bank(slot, n), 0:P // 2].bitcast(BF16)
                                        ).then_inc(item_read, 1)

            for n in range(EARLY):
                maximum(0, 0, n // 2, n % 2, n, n % BANKS)
            groups(dve, first)

        @block.gpsimd
        def _(pool):
            def first(g):
                for j in range(GROUP):
                    n = g * GROUP + j
                    s = j % 2
                    pool.wait_ge(m_hi, 2 * n + 2)
                    pool.tensor_tensor(mp[:, s, 1, :], mf[:, s, :], mp[:, s, 0, :], ALU.subtract).then_inc(m_mid, 1)
                    pool.tensor_tensor(mr[:, s, :], mf[:, s, :], mp[:, s, 0, :], ALU.subtract).then_inc(m_mid, 1)
                    pool.wait_ge(m_mid, 2 * n + 2)
                    pool.tensor_tensor(mp[:, s, 2, :], mr[:, s, :], mp[:, s, 1, :], ALU.subtract).then_inc(m_parts, 1)

            def values(g, slot):
                pool.tensor_copy(v[:, slot, :, :, 0:HD], B.V[:, g, :, :].rearrange("p t (j d) -> p t j d", d=HD)
                                 ).then_inc(v_in, 1)

            first(0)

            def run(g, slot):
                values(g, slot)
                if not last_group(g):
                    first(g + 1)

            groups(pool, run)

        @block.scalar
        def _(act):
            for s in (step_exp, sums_out, stored):
                act.sem_inc(s, LEAD)

            def out(g, slot, half):
                act.wait_ge(summed, (g + 1) * UNITS - 1 + half + LEAD)
                act.wait_ge(stored, 16 * OST * g + LEAD)
                act.activation(o[:, slot, half, :], ps_o[:, half, :], ACT.Copy).then_inc(sums_out, 1)

            def run(g, slot):
                for u in range(STEPS):
                    w, j = u // GROUP, u % GROUP
                    act.wait_ge(step_made, g * STEPS + u + 1)
                    if j == 0:
                        act.wait_ge(summed, g * UNITS + w - 1 + LEAD)
                    act.activation(e[:, w % 2, j, :], ps_s[:, (slot * STEPS + u) % BANKS, :], ACT.Exp).then_inc(step_exp, 1)
                    if u in (1, 5) and not first_group(g):
                        out(g - 1, (slot - 1) % SLOTS, u // 4)

            groups(act, run)
            for half in range(2):
                out(GROUPS - 1, (GROUPS - 1) % SLOTS, half)


EXPERTS, FF = 8, 512
FT = FF // P
CT = CHUNK // P


def f32(ap):
    return ap.bitcast(F32)


def phase_moe(nc, X, ident, aon, aod, ow, ob, rw, rb, b2, iota, w1, b1, w2):
    with ExitStack() as ctx:
        m = Scope(nc, ctx, "moe")
        mla_hi, mla_lo = m.sb("mla_hi", [P, KD, BATCH * SEQ], F32R), m.sb("mla_lo", [P, KD, BATCH * SEQ], F32R)
        acc = m.sb("acc", [P, TILES, DIM])
        ow_sb, ob_sb = m.sb("ow", [P, DIM]), m.sb("ob", [P, KD])
        rw_sb, rb_sb = m.sb("rw", [P, KD, EXPERTS]), m.sb("rb", [P, EXPERTS])
        iota_sb = m.sb("iota", [P, EXPERTS])
        b2_sb = m.sb("b2", [P, EXPERTS * DIM])
        logit = m.sb("logit", [P, TILES, EXPERTS])
        top = m.sb("top", [P, TILES, 8])
        index = m.sb("index", [P, TILES, 8], U32)
        indexf = m.sb("indexf", [P, TILES, 2])
        big = m.sb("big", [P, TILES])
        pair = m.sb("pair", [P, TILES, 2])
        first = m.sb("first", [P, TILES, EXPERTS])
        combine = m.sb("combine", [P, TILES, EXPERTS])
        raw1, raw2, rawb = m.sb("raw1", [P, 2, KD, FF]), m.sb("raw2", [P, 2, FT, DIM]), m.sb("rawb", [P, 2, FT])
        w1_hi, w1_lo = m.sb("w1_hi", [P, 2, KD, FF], F32R), m.sb("w1_lo", [P, 2, KD, FF], F32R)
        w2_hi, w2_lo = m.sb("w2_hi", [P, 2, FT, DIM], F32R), m.sb("w2_lo", [P, 2, FT, DIM], F32R)
        b1_sb = m.sb("b1", [P, 2, FT])
        one = m.sb("one", [P, KD])
        g = m.sb("g", [P, 2, FT, CHUNK])
        g_hi, g_lo = m.sb("g_hi", [P, 2, FT, CHUNK], F32R), m.sb("g_lo", [P, 2, FT, CHUNK], F32R)
        full = g[:, 0, :, :].rearrange("p (s k) n -> p s k n", k=KD)
        num, den = g[:, 1, 0:2, :], g[:, 1, 2:4, :]
        ps_h = [m.ps(f"ps_h{n}", [P, CHUNK]) for n in range(FT)]
        ps_o = [m.ps(f"ps_o{n}", [P, 512]) for n in range(CT)]

        w_in, sums_in = m.sem("w_in"), [m.sem(f"sums_in{n}") for n in range(2)]
        inverted, divided, mla_made, mla_full, hi_made, mla_split = (
            m.sem("inverted"), m.sem("divided"), m.sem("mla_made"), m.sem("mla_full"), m.sem("hi_made"), m.sem("mla_split"))
        routed, logits, chain, placed, exped = (m.sem("routed"), m.sem("logits"), m.sem("chain"), m.sem("placed"),
                                                m.sem("exped"))
        raw_in = [m.sem(f"raw_in{n}") for n in range(2)]
        w_ready, hid_made, hid_out, lo_made, out_made, out_added = (m.sem("w_ready"), m.sem("hid_made"), m.sem("hid_out"),
                                                                    m.sem("lo_made"), m.sem("out_made"), m.sem("out_added"))
        b2_added, scaled, set_up = m.sem("b2_added"), m.sem("scaled"), m.sem("set_up")
        LOADS = 10
        CHAIN = 13 + 2 * TILES
        SPLITS = 5
        W_LEAD, HID_LEAD, OUT_LEAD, ADD_LEAD = 2 * SPLITS, 2 * FT, CHUNKS * CT + 1, CT
        EPAIRS = EXPERTS // 2

        block = ctx.enter_context(nc.Block())

        def expert_pairs(eng, run):
            with eng.Fori(0, EPAIRS - 1) as i:
                run(i * 2, True)
            run(EXPERTS - 2, False)

        @block.sync
        def _(sp):
            def sums(c):
                s, b, at = c % 2, c // 2, (c % 2) * CHUNK
                sp.dma_start(den[:, s, :], aod[b * HEADS:(b + 1) * HEADS, at:at + CHUNK].unsqueeze(1)
                             .to_broadcast([HEADS, HD, CHUNK])).then_inc(sums_in[s], 16)
                sp.dma_start(num[:, s, :], aon[b * P:(b + 1) * P, at:at + CHUNK]).then_inc(sums_in[s], 16)

            def weights(e, s):
                sp.dma_start(raw1[:, s, :, :], w1[e].rearrange("(k p) f -> p k f", p=P)).then_inc(raw_in[s], 16)
                sp.dma_start(raw2[:, s, :, :], w2[e].rearrange("(k p) f -> p k f", p=P)).then_inc(raw_in[s], 16)
                sp.dma_start(rawb[:, s, :], b1[e]).then_inc(raw_in[s], 16)

            sums(0)
            for dst, src in ((ow_sb, ow), (ob_sb, ob), (iota_sb, iota)):
                sp.dma_start(dst[:, :], src).then_inc(w_in, 16)
            sp.dma_start(rw_sb[:, :, :], rw.rearrange("(k p) e -> p k e", p=P)).then_inc(w_in, 16)
            for n in range(4):
                sp.dma_start(rb_sb[32 * n:32 * (n + 1), :], rb.partition_broadcast(32)).then_inc(w_in, 16)
            sums(1)
            for n in range(2):
                sp.dma_start(b2_sb[64 * n:64 * (n + 1), :], b2.partition_broadcast(64)).then_inc(w_in, 16)
            for e in range(2):
                weights(e, e)
            for c in range(2, CHUNKS):
                sp.wait_ge(mla_made, c - 1)
                sums(c)
            with sp.Fori(1, EPAIRS) as i:
                for s in range(2):
                    e = i * 2 + s
                    sp.wait_ge(w_ready, W_LEAD + (e - 1) * SPLITS)
                    weights(e, s)

        @block.gpsimd
        def _(pool):
            pool.sem_inc(w_ready, W_LEAD)
            pool.memset(one[:, :], 1.0).then_inc(set_up, 1)
            pool.wait_ge(set_up, 1)
            pool.memset(acc[:, :, :], 0.0).then_inc(set_up, 1)
            pool.wait_ge(set_up, 2)
            with pool.Fori(0, EPAIRS) as i:
                for s in range(2):
                    e = i * 2 + s
                    pool.wait_ge(raw_in[s], 48 * (i + 1))
                    pool.wait_ge(out_made, OUT_LEAD + (e - 1) * CHUNKS * CT)
                    pool.tensor_tensor(w1_hi[:, s, :, :], raw1[:, s, :, :],
                                       one[:, :].unsqueeze(2).to_broadcast([P, KD, FF]), ALU.mult).then_inc(w_ready, 1)
                    pool.tensor_copy(w2_hi[:, s, :, :], raw2[:, s, :, :]).then_inc(w_ready, 1)
                    pool.tensor_copy(b1_sb[:, s, :], rawb[:, s, :]).then_inc(w_ready, 1)
                    pool.wait_ge(w_ready, W_LEAD + e * SPLITS + 2)
                    pool.tensor_tensor(w1_lo[:, s, :, :], raw1[:, s, :, :], f32(w1_hi[:, s, :, :]),
                                       ALU.subtract).then_inc(w_ready, 1)
                    pool.tensor_tensor(w2_lo[:, s, :, :], raw2[:, s, :, :], f32(w2_hi[:, s, :, :]),
                                       ALU.subtract).then_inc(w_ready, 1)

        @block.tensor
        def _(pe):
            pe.sem_inc(out_made, OUT_LEAD)

            def project(c):
                pe.wait_ge(divided, c + 1)
                if c >= 2:
                    pe.wait_ge(mla_full, c - 1)
                for k in range(KD):
                    mm = pe.matmul(ps_h[c % 2 * KD + k][:, :], ow_sb[:, k * P:(k + 1) * P], num[:, c % 2, :],
                                   start=True, stop=True)
                mm.then_inc(mla_made, 1)

            def route(c):
                s = c % 2
                pe.wait_ge(mla_full, c + 1)
                if c >= 2:
                    pe.wait_ge(logits, c - 1)
                for t in range(CT):
                    for k in range(KD):
                        mm = pe.matmul(ps_o[s][:, t * EXPERTS:(t + 1) * EXPERTS], full[:, s, k, t * P:(t + 1) * P],
                                       rw_sb[:, k, :], start=k == 0, stop=k == KD - 1)
                mm.then_inc(routed, 1)

            pe.wait_ge(w_in, 16 * LOADS)
            project(0)
            for c in range(CHUNKS):
                if c + 1 < CHUNKS:
                    project(c + 1)
                route(c)

            def hidden(n, s, c, sg):
                for f in range(FT):
                    pe.wait_ge(hid_out, n * 2 * FT + 2 * (f + 1))
                    at = slice(c * CHUNK, (c + 1) * CHUNK)
                    for i, (w, x) in enumerate(((w1_hi, mla_hi), (w1_lo, mla_hi), (w1_hi, mla_lo))):
                        for k in range(KD):
                            mm = pe.matmul(ps_h[f][:, :], w[:, s, k, f * P:(f + 1) * P], x[:, k, at],
                                           start=i == 0 and k == 0, stop=i == 2 and k == KD - 1)
                    mm.then_inc(hid_made, 1)

            def output(n, s, sg):
                pe.wait_ge(lo_made, (n + 1) * FT)
                for t in range(CT):
                    pe.wait_ge(out_added, n * CT + t + 1)
                    for i, (x, w) in enumerate(((g_hi, w2_hi), (g_lo, w2_hi), (g_hi, w2_lo))):
                        for f in range(FT):
                            mm = pe.matmul(ps_o[t][:, 0:DIM], x[:, sg, f, t * P:(t + 1) * P], w[:, s, f, :],
                                           start=i == 0 and f == 0, stop=i == 2 and f == FT - 1)
                    mm.then_inc(out_made, 1)

            pe.wait_ge(w_ready, W_LEAD + SPLITS)
            pe.wait_ge(mla_split, CHUNKS)
            hidden(0, 0, 0, 0)
            pe.wait_ge(logits, CHUNKS)

            def run(e0, more):
                for j in range(2 * CHUNKS):
                    n = e0 * CHUNKS + j
                    if more or j + 1 < 2 * CHUNKS:
                        if (j + 1) % CHUNKS == 0:
                            pe.wait_ge(w_ready, W_LEAD + (e0 + (j + 1) // CHUNKS + 1) * SPLITS)
                        hidden(n + 1, (j + 1) // CHUNKS % 2, (j + 1) % CHUNKS, (j + 1) % 2)
                    output(n, j // CHUNKS, j % 2)

            expert_pairs(pe, run)

        @block.scalar
        def _(act):
            act.sem_inc(hid_out, HID_LEAD)
            act.wait_ge(w_in, 16 * LOADS)
            for c in range(CHUNKS):
                s = c % 2
                act.wait_ge(mla_made, c + 1)
                if c >= 2:
                    act.wait_ge(mla_split, c - 1)
                    act.wait_ge(routed, c - 1)
                for k in range(KD):
                    ins = act.activation(full[:, s, k, :], ps_h[s * KD + k][:, :], ACT.Identity, bias=ob_sb[:, k:k + 1])
                ins.then_inc(mla_full, 1)
            act.wait_ge(chain, 2)
            act.activation(logit[:, :, :], logit[:, :, :], ACT.Exp).then_inc(exped, 1)
            act.wait_ge(mla_split, CHUNKS)
            act.wait_ge(routed, CHUNKS)
            with act.Fori(0, EPAIRS) as i:
                for j in range(2 * CHUNKS):
                    n, s, sg = i * (2 * CHUNKS) + j, j // CHUNKS, j % 2
                    act.wait_ge(out_made, OUT_LEAD + (n - 1) * CT)
                    for f in range(FT):
                        act.wait_ge(hid_made, n * FT + f + 1)
                        for dst in (g, g_hi):
                            act.activation(dst[:, sg, f, :], ps_h[f][:, :], ACT.Gelu, bias=b1_sb[:, s, f:f + 1]).then_inc(hid_out, 1)

        @block.vector
        def _(dve):
            dve.sem_inc(out_added, ADD_LEAD)

            def divide(c):
                s = c % 2
                dve.wait_ge(sums_in[s], 32 * (c // 2 + 1))
                dve.reciprocal(den[:, s, :], den[:, s, :]).then_inc(inverted, 1)
                dve.wait_ge(inverted, c + 1)
                dve.tensor_tensor(num[:, s, :], num[:, s, :], den[:, s, :], ALU.mult).then_inc(divided, 1)

            divide(0)
            dve.wait_ge(w_in, 16 * LOADS)
            divide(1)
            for c in range(CHUNKS):
                s = c % 2
                at = c * CHUNK
                dve.wait_ge(mla_full, c + 1)
                dve.tensor_copy(mla_hi[:, :, at:at + CHUNK], full[:, s, :, :]).then_inc(hi_made, 1)
                dve.wait_ge(hi_made, c + 1)
                dve.tensor_tensor(mla_lo[:, :, at:at + CHUNK], full[:, s, :, :], f32(mla_hi[:, :, at:at + CHUNK]),
                                  ALU.subtract).then_inc(mla_split, 1)
                if c + 2 < CHUNKS:
                    divide(c + 2)
                dve.wait_ge(routed, c + 1)
                dve.tensor_tensor(logit[:, c * CT:(c + 1) * CT, :],
                                  ps_o[s][:, 0:CT * EXPERTS].rearrange("p (t e) -> p t e", e=EXPERTS),
                                  rb_sb[:, :].unsqueeze(1).to_broadcast([P, CT, EXPERTS]), ALU.add).then_inc(logits, 1)

            made = [0]

            def linked(ins):
                made[0] += 1
                ins.then_inc(chain, 1)
                dve.wait_ge(chain, made[0])

            wide = [P, TILES, EXPERTS]
            dve.wait_ge(logits, CHUNKS)
            linked(dve.tensor_reduce(big[:, :], logit[:, :, :], AX.X, ALU.max))
            linked(dve.tensor_tensor(logit[:, :, :], logit[:, :, :], big[:, :].unsqueeze(2).to_broadcast(wide),
                                     ALU.subtract))
            dve.wait_ge(exped, 1)
            linked(dve.tensor_reduce(big[:, :], logit[:, :, :], AX.X, ALU.add))
            linked(dve.reciprocal(big[:, :], big[:, :]))
            linked(dve.tensor_tensor(logit[:, :, :], logit[:, :, :], big[:, :].unsqueeze(2).to_broadcast(wide), ALU.mult))
            for t in range(TILES):
                dve.max(top[:, t, :], logit[:, t, :]).then_inc(chain, 1)
            made[0] += TILES
            dve.wait_ge(chain, made[0])
            for t in range(TILES):
                dve.max_index(index[:, t, :], top[:, t, :], logit[:, t, :]).then_inc(chain, 1)
            made[0] += TILES
            dve.wait_ge(chain, made[0])
            linked(dve.tensor_copy(indexf[:, :, :], index[:, :, 0:2]))
            linked(dve.tensor_tensor(big[:, :], top[:, :, 0], top[:, :, 1], ALU.add))
            linked(dve.tensor_scalar(big[:, :], big[:, :], 1e-8, None, ALU.add))
            linked(dve.reciprocal(big[:, :], big[:, :]))
            linked(dve.tensor_tensor(pair[:, :, :], top[:, :, 0:2], big[:, :].unsqueeze(2).to_broadcast([P, TILES, 2]),
                                     ALU.mult))
            for n, dst in ((0, first), (1, combine)):
                dve.tensor_tensor(dst[:, :, :], iota_sb[:, :].unsqueeze(1).to_broadcast(wide),
                                  indexf[:, :, n].unsqueeze(2).to_broadcast(wide), ALU.is_equal).then_inc(placed, 1)
                dve.wait_ge(placed, n + 1)
                linked(dve.tensor_tensor(dst[:, :, :], dst[:, :, :], pair[:, :, n].unsqueeze(2).to_broadcast(wide),
                                         ALU.mult))
            linked(dve.tensor_tensor(combine[:, :, :], combine[:, :, :], first[:, :, :], ALU.add))
            assert made[0] == CHAIN, made[0]
            dve.wait_ge(set_up, 2)

            def low(n, sg):
                for f in range(FT):
                    dve.wait_ge(hid_out, HID_LEAD + n * 2 * FT + 2 * (f + 1))
                    dve.tensor_tensor(g_lo[:, sg, f, :], g[:, sg, f, :], f32(g_hi[:, sg, f, :]), ALU.subtract).then_inc(lo_made, 1)

            def add(n, e, c, last):
                weight = [combine[:, c * CT + t, bass.ds(e, 1)] for t in range(CT)]
                for t in range(CT):
                    tile = c * CT + t
                    dve.wait_ge(out_added, n * CT + t + 1)
                    dve.scalar_tensor_tensor(out=acc[:, tile, :], in0=b2_sb[:, bass.ds(e * DIM, DIM)], scalar=weight[t],
                                             in1=acc[:, tile, :], op0=ALU.mult, op1=ALU.add).then_inc(b2_added, 1)
                for t in range(CT):
                    tile = c * CT + t
                    dve.wait_ge(b2_added, n * CT + t + 1)
                    dve.wait_ge(out_made, OUT_LEAD + n * CT + t + 1)
                    dve.scalar_tensor_tensor(out=acc[:, tile, :], in0=ps_o[t][:, 0:DIM], scalar=weight[t],
                                             in1=acc[:, tile, :], op0=ALU.mult, op1=ALU.add).then_inc(out_added, 1)
                if last:
                    for t in range(CT):
                        tile = c * CT + t
                        dve.wait_ge(out_added, ADD_LEAD + n * CT + t + 1)
                        dve.scalar_tensor_tensor(out=X[:, tile, :], in0=acc[:, tile, :], scalar=0.3, in1=X[:, tile, :],
                                                 op0=ALU.mult, op1=ALU.add).then_inc(scaled, 1)

            low(0, 0)

            def run(e0, more):
                for j in range(2 * CHUNKS):
                    n = e0 * CHUNKS + j
                    if more or j + 1 < 2 * CHUNKS:
                        low(n + 1, (j + 1) % 2)
                    add(n, e0 + j // CHUNKS, j % CHUNKS, not more and j >= CHUNKS)

            expert_pairs(dve, run)


GROUPS1 = 2


def phase_xattn1(nc, X, ident, ctxT, Wq, Wk, Wv, Wo, bq, bk, bv, bo, mask8):
    with ExitStack() as ctx:
        m = Scope(nc, ctx, "xa1")
        ctx_sb = m.sb("ctx", [P, 2, BATCH * CTX])
        wq, wk, wv, wo = (m.sb(n, [P, 2, DIM]) for n in ("wq", "wk", "wv", "wo"))
        bq_sb, bk_sb, bv_sb = (m.sb(n, [P, GROUPS1]) for n in ("bq", "bk", "bv"))
        bo_sb = m.sb("bo", [P, DIM])
        mask = m.sb("mask", [P, GH])
        kblk = m.sb("kblk", [P, BATCH, GROUPS1, HJ])
        vT = m.sb("vT", [P, BATCH, GROUPS1, HJ])
        vblk = m.sb("vblk", [P, BATCH, GROUPS1, HJT, P])
        stats, mv = m.sb("stats", [P, TILES, 6]), m.sb("mv", [P, TILES, 2])
        root, rstd = m.sb("root", [P, TILES]), m.sb("rstd", [P, TILES])
        xn = m.sb("xn", [P, 2, DIM])
        xT = m.sb("xT", [P, 2, KD, P])
        qT = m.sb("qT", [P, 2, GROUPS1, P])
        mx, sm, rc = (m.sb(n, [P, 2, GROUPS1, GH]) for n in ("mx", "sm", "rc"))
        pr = m.sb("pr", [P, 2, GROUPS1, HJ])
        pT = m.sb("pT", [P, 2, GROUPS1, HJT, P])
        aT = m.sb("aT", [P, 2, GROUPS1, P])
        ps_x = m.ps("ps_x", [P, 512])
        ps_s = m.ps("ps_s", [P, GROUPS1, 2, 512])
        ps_p = m.ps("ps_p", [P, 2, 512])
        ps_o = m.ps("ps_o", [P, 512])

        w_in = m.sem("w_in")
        prep_pe, prep_dve, prep_act = m.sem("prep_pe"), m.sem("prep_dve"), m.sem("prep_act")
        s_stats, s_var, s_root, s_rstd = m.sem("s_stats"), m.sem("s_var"), m.sem("s_root"), m.sem("s_rstd")
        normed, turned, xT_in, queried, qT_in = (m.sem("normed"), m.sem("turned"), m.sem("xT_in"), m.sem("queried"),
                                                 m.sem("qT_in"))
        pairs = ("scored", "maxed", "shifted", "exped", "summed", "inverted", "weighted", "pturned", "pT_in")
        scored, maxed, shifted, exped, summed, inverted, weighted, pturned, pT_in = (
            [m.sem(f"{n}{g}") for g in range(GROUPS1)] for n in pairs)
        attended, aT_in, projected, biased, added = (m.sem("attended"), m.sem("aT_in"), m.sem("projected"),
                                                     m.sem("biased"), m.sem("added"))
        LOADS = 14
        LAG = 5

        def rows_of(i):
            return P if i < HJT - 1 else HJR

        block = ctx.enter_context(nc.Block())

        @block.sync
        def _(sp):
            sp.dma_start(mask[:, :], mask8).then_inc(w_in, 16)
            for k, (at, rows) in enumerate(((0, P), (P, C2))):
                sp.dma_start(ctx_sb[0:rows, k, :], ctxT[at:at + rows, :]).then_inc(w_in, 16)
                sp.dma_start(wk[0:rows, k, :], Wk[at:at + rows, :]).then_inc(w_in, 16)
                sp.dma_start(wv[0:rows, k, :], Wv[at:at + rows, :]).then_inc(w_in, 16)
            for dst, src in ((bq_sb, bq), (bk_sb, bk), (bv_sb, bv)):
                sp.dma_start(dst[:, :], src).then_inc(w_in, 16)
            for dst, src in ((wq, Wq), (wo, Wo)):
                sp.dma_start(dst[:, :, :], src.rearrange("(k p) n -> p k n", p=P)).then_inc(w_in, 16)
            for n in range(2):
                sp.dma_start(bo_sb[64 * n:64 * (n + 1), :], bo.partition_broadcast(64)).then_inc(w_in, 16)

        @block.tensor
        def _(pe):
            pe.wait_ge(w_in, 16 * LOADS)
            for n, w in enumerate((wk, wv)):
                for g in range(GROUPS1):
                    for k, rows in enumerate((P, C2)):
                        mm = pe.matmul(ps_s[:, n, g, 0:BATCH * CTX], w[0:rows, k, g * P:(g + 1) * P],
                                       ctx_sb[0:rows, k, :], start=k == 0, stop=k == 1)
                    mm.then_inc(prep_pe, 1)
            pe.wait_ge(prep_dve, 2 * BATCH * GROUPS1)
            n = 0
            for b in range(BATCH):
                for g in range(GROUPS1):
                    if n:
                        pe.wait_ge(prep_act, n)
                    for i in range(HJT):
                        rows = rows_of(i)
                        mm = pe.transpose(ps_p[0:rows, i // 4, (i % 4) * P:(i % 4 + 1) * P],
                                          vT[:, b, g, i * P:i * P + rows], ident[:, :])
                    mm.then_inc(prep_pe, 1)
                    n += 1
            pe.wait_ge(prep_act, n)
            for s in (turned, queried, *scored, *pturned, attended, projected):
                pe.sem_inc(s, LEAD)

            def turn_p(t, s, g):
                pe.wait_ge(weighted[g], has(t))
                pe.wait_ge(pT_in[1 - g], one_ago(t) if g == 0 else has(t))
                for j in range(HJT):
                    rows = rows_of(j)
                    mm = pe.transpose(ps_p[0:rows, j // 4, (j % 4) * P:(j % 4 + 1) * P],
                                      pr[:, s, g, j * P:j * P + rows], ident[:, :])
                mm.then_inc(pturned[g], 1)

            def turn(i, par):
                if live(i - 3):
                    turn_p(i - 3, 1 - par, 0)
                if live(i - 1):
                    t, s = i - 1, 1 - par
                    pe.wait_ge(qT_in, has(t))
                    for g in range(GROUPS1):
                        pe.wait_ge(shifted[g], one_ago(t))
                        for half in range(2):
                            mm = pe.matmul(ps_s[:, g, half, 0:HALF], qT[:, s, g, :],
                                           kblk[:, s, g, half * HALF:(half + 1) * HALF], start=True, stop=True)
                        mm.then_inc(scored[g], 1)
                if live(i - 3):
                    turn_p(i - 3, 1 - par, 1)
                if live(i):
                    t = i
                    pe.wait_ge(normed, has(t))
                    pe.wait_ge(qT_in, one_ago(t))
                    for k in range(KD):
                        mm = pe.transpose(ps_x[:, k * P:(k + 1) * P], xn[:, par, k * P:(k + 1) * P], ident[:, :])
                    mm.then_inc(turned, 1)
                if live(i - 5):
                    t, s = i - 5, 1 - par
                    pe.wait_ge(aT_in, has(t))
                    for g in range(GROUPS1):
                        mm = pe.matmul(ps_o[:, DIM:2 * DIM], aT[:, s, g, :], wo[:, g, :], start=g == 0,
                                       stop=g == GROUPS1 - 1)
                    mm.then_inc(projected, 1)
                if live(i):
                    t = i
                    pe.wait_ge(xT_in, has(t))
                    for g in range(GROUPS1):
                        for k in range(KD):
                            mm = pe.matmul(ps_x[:, g * P:(g + 1) * P], wq[:, k, g * P:(g + 1) * P], xT[:, par, k, :],
                                           start=k == 0, stop=k == KD - 1)
                    mm.then_inc(queried, 1)
                if live(i - 4):
                    t, s = i - 4, par
                    pe.wait_ge(pT_in[1], has(t))
                    pe.wait_ge(added, one_ago(t))
                    for g in range(GROUPS1):
                        for j in range(HJT):
                            rows = rows_of(j)
                            mm = pe.matmul(ps_o[:, g * P:(g + 1) * P], vblk[0:rows, s, g, j, :],
                                           pT[0:rows, s, g, j, :], start=j == 0, stop=j == HJT - 1)
                    mm.then_inc(attended, 1)

            turns(pe, LAG, turn)

        @block.vector
        def _(dve):
            norm_stats(dve, s_root, X, stats, mv, root, rstd, s_stats, s_var, s_rstd)
            dve.wait_ge(w_in, 16 * LOADS)
            for n, (dst, bias) in enumerate(((kblk, bk_sb), (vT, bv_sb))):
                dve.wait_ge(prep_pe, 2 * (n + 1))
                for b in range(BATCH):
                    for g in range(GROUPS1):
                        dve.scalar_tensor_tensor(
                            out=dst[:, b, g, :].rearrange("p (h j) -> p h j", h=GH),
                            in0=ps_s[:, n, g, b * CTX:(b + 1) * CTX].unsqueeze(1).to_broadcast([P, GH, CTX]),
                            scalar=bias[:, g:g + 1], in1=mask[:, :].unsqueeze(2).to_broadcast([P, GH, CTX]),
                            op0=ALU.add, op1=ALU.mult).then_inc(prep_dve, 1)
            for s in (normed, *maxed, *shifted, *summed, *inverted, added):
                dve.sem_inc(s, LEAD)

            def turn(i, par):
                if live(i):
                    t = i
                    dve.wait_ge(turned, two_ago(t))
                    x = tile_of(t, par)
                    dve.tensor_scalar(xn[:, par, :], X[:, x, :], mv[:, x, 0:1], rstd[:, bass.ds(x, 1)],
                                      ALU.subtract, ALU.mult).then_inc(normed, 1)
                if live(i - 2):
                    t, s = i - 2, par
                    for g in range(GROUPS1):
                        dve.wait_ge(exped[g], has(t))
                        dve.wait_ge(weighted[g], two_ago(t))
                        dve.tensor_reduce(sm[:, s, g, :], pr[:, s, g, :].rearrange("p (h j) -> p h j", j=CTX), AX.X,
                                          ALU.add).then_inc(summed[g], 1)
                        dve.wait_ge(summed[g], has(t))
                        dve.reciprocal(rc[:, s, g, :], sm[:, s, g, :]).then_inc(inverted[g], 1)
                for g in range(GROUPS1):
                    if live(i - 1):
                        t, s = i - 1, 1 - par
                        dve.wait_ge(scored[g], has(t))
                        src = ps_s[:, g, :, 0:HALF].rearrange("p a (h j) -> p a h j", j=CTX)
                        dve.tensor_reduce(mx[:, s, g, :].rearrange("p (a h) -> p a h", a=2), src, AX.X,
                                          ALU.max).then_inc(maxed[g], 1)
                        dve.wait_ge(maxed[g], has(t))
                        dve.wait_ge(pturned[g], two_ago(t))
                        dve.tensor_tensor(pr[:, s, g, :].rearrange("p (a h j) -> p a h j", a=2, j=CTX), src,
                                          mx[:, s, g, :].rearrange("p (a h) -> p a h", a=2).unsqueeze(3)
                                          .to_broadcast([P, 2, GH // 2, CTX]), ALU.subtract).then_inc(shifted[g], 1)
                    if g == 0 and live(i - 5):
                        t = i - 5
                        dve.wait_ge(projected, has(t))
                        dve.wait_ge(biased, has(t))
                        x = tile_of(t, 1 - par)
                        dve.tensor_tensor(X[:, x, :], ps_o[:, DIM:2 * DIM], X[:, x, :], ALU.add).then_inc(added, 1)

            turns(dve, LAG, turn)

        @block.gpsimd
        def _(pool):
            for s in (*weighted, biased):
                pool.sem_inc(s, LEAD)
            pool.wait_ge(w_in, 16 * LOADS)

            def turn(i, par):
                if live(i - 2):
                    t, s = i - 2, par
                    for g in range(GROUPS1):
                        pool.wait_ge(inverted[g], has(t))
                        v = pr[:, s, g, :].rearrange("p (h j) -> p h j", j=CTX)
                        pool.tensor_tensor(v, v, rc[:, s, g, :].unsqueeze(2).to_broadcast([P, GH, CTX]),
                                           ALU.mult).then_inc(weighted[g], 1)
                if live(i - 1):
                    t = i - 1
                    pool.wait_ge(normed, has(t))
                    x = tile_of(t, 1 - par)
                    pool.tensor_tensor(X[:, x, :], X[:, x, :], bo_sb[:, :], ALU.add).then_inc(biased, 1)

            turns(pool, LAG, turn)

        @block.scalar
        def _(act):
            act.wait_ge(s_var, 1)
            act.activation(root[:, :], root[:, :], ACT.Sqrt).then_inc(s_root, 1)
            n = 0
            for b in range(BATCH):
                for g in range(GROUPS1):
                    act.wait_ge(prep_pe, 5 + n)
                    act.activation(vblk[:, b, g, 0:4, :].rearrange("p k n -> p (k n)"), ps_p[:, 0, :], ACT.Copy)
                    act.activation(vblk[0:HJR, b, g, 4, :], ps_p[0:HJR, 1, 0:P], ACT.Copy).then_inc(prep_act, 1)
                    n += 1
            for s in (xT_in, qT_in, *exped, *pT_in, aT_in):
                act.sem_inc(s, LEAD)

            def copy_p(t, s, g):
                act.wait_ge(pturned[g], has(t))
                act.wait_ge(attended, two_ago(t))
                act.activation(pT[:, s, g, 0:4, :].rearrange("p k n -> p (k n)"), ps_p[:, 0, :], ACT.Copy)
                act.activation(pT[0:HJR, s, g, 4, :], ps_p[0:HJR, 1, 0:P], ACT.Copy).then_inc(pT_in[g], 1)

            def exps(t, s, g):
                act.wait_ge(shifted[g], has(t))
                act.activation(pr[:, s, g, :], pr[:, s, g, :], ACT.Exp, scale=0.25).then_inc(exped[g], 1)

            def turn(i, par):
                if live(i - 5):
                    t, s = i - 5, 1 - par
                    act.wait_ge(attended, has(t))
                    act.wait_ge(projected, two_ago(t))
                    act.activation(aT[:, s, :, :].rearrange("p k n -> p (k n)"), ps_o[:, 0:DIM], ACT.Copy).then_inc(aT_in, 1)
                if live(i - 3):
                    copy_p(i - 3, 1 - par, 0)
                if live(i - 3):
                    copy_p(i - 3, 1 - par, 1)
                if live(i):
                    t = i
                    act.wait_ge(turned, has(t))
                    act.wait_ge(queried, two_ago(t))
                    act.activation(xT[:, par, :, :].rearrange("p k n -> p (k n)"), ps_x[:, 0:DIM],
                                   ACT.Copy).then_inc(xT_in, 1)
                if live(i - 1):
                    exps(i - 1, 1 - par, 0)
                if live(i - 1):
                    exps(i - 1, 1 - par, 1)
                if live(i):
                    t = i
                    act.wait_ge(queried, has(t))
                    act.wait_ge(scored[1], two_ago(t))
                    act.activation(qT[:, par, 0, :], ps_x[:, 0:P], ACT.Identity, bias=bq_sb[:, 0:1])
                    act.activation(qT[:, par, 1, :], ps_x[:, P:2 * P], ACT.Identity, bias=bq_sb[:, 1:2]).then_inc(qT_in, 1)

            turns(act, LAG, turn)


HID = 1024
KH = HID // P
ROUND = 12582912.0


def phase_ffn(nc, X, ident, identb, out, w1T, w2T, b1, b2, g1, n1, g2, n2):
    with ExitStack() as ctx:
        m = Scope(nc, ctx, "ffn")
        raw = m.sb("raw", [P, 2, 2048])
        wq = m.sb("wq", [P, 2, 2048], BF16)
        w1q = wq[:, 0, :].rearrange("p (k n) -> p k n", k=KD)
        w2q = wq[:, 1, :].rearrange("p (k n) -> p k n", k=KH)
        ones = m.sb("ones", [P, P])
        wsum, wmean, winv, wfac = m.sb("wsum", [P, 2]), m.sb("wmean", [P, 2]), m.sb("winv", [P, 2]), m.sb("wfac", [P, 2])
        b1_sb, g2_sb, n2_sb = m.sb("b1", [P, HID]), m.sb("g2", [P, HID]), m.sb("n2", [P, HID])
        b2_sb, g1_sb, n1_sb = m.sb("b2", [P, DIM]), m.sb("g1", [P, DIM]), m.sb("n1", [P, DIM])
        stats, mv = m.sb("stats", [P, TILES, 6]), m.sb("mv", [P, TILES, 2])
        root, rstd = m.sb("root", [P, TILES]), m.sb("rstd", [P, TILES])
        stats2, mv2 = m.sb("stats2", [P, TILES, 12]), m.sb("mv2", [P, TILES, 2])
        root2, rstd2 = m.sb("root2", [P, TILES]), m.sb("rstd2", [P, TILES])
        G = m.sb("G", [P, TILES, HID])
        nmr, nmr2 = m.sb("nmr", [P, TILES]), m.sb("nmr2", [P, TILES])
        z = m.sb("z", [P, 2, HID])
        h = m.sb("h", [P, 2, HID])
        q = m.sb("q", [P, 2, HID], BF16)
        qT = m.sb("qT", [P, 2, HID], BF16)
        y = m.sb("y", [P, 2, HID])
        amax, ainv, fac = m.sb("amax", [P, TILES]), m.sb("ainv", [P, TILES]), m.sb("fac", [P, TILES])
        ps_t = m.ps("ps_t", [P, 2, 1024], BF16)
        ps_y = m.ps("ps_y", [P, 2, HID])
        ps_w = m.ps("ps_w", [P, 512])

        w_in, v_in = m.sem("w_in"), m.sem("v_in")
        w_abs, w_sum, w_chain, w_rounded = m.sem("w_abs"), m.sem("w_sum"), m.sem("w_chain"), m.sem("w_rounded")
        s_stats, s_var, s_root, s_rstd = m.sem("s_stats"), m.sem("s_var"), m.sem("s_root"), m.sem("s_rstd")
        s_stats2, s_var2, s_root2, s_rstd2 = m.sem("s_stats2"), m.sem("s_var2"), m.sem("s_root2"), m.sem("s_rstd2")
        s_nmr = m.sem("s_nmr")
        names = ("centred", "gained", "quant", "scaled", "rounded", "turned", "qT_in", "made", "used")
        first = {n: m.sem(f"first_{n}") for n in names + ("gelued", "y_full")}
        second = {n: m.sem(f"second_{n}") for n in names}
        biased, stored = m.sem("biased"), m.sem("stored")
        LAG = 4
        VLOADS = 12

        block = ctx.enter_context(nc.Block())

        @block.sync
        def _(sp):
            sp.dma_start(raw[:, 0, :].rearrange("p (k n) -> p k n", k=KD), w1T.rearrange("(k p) n -> p k n", p=P)).then_inc(w_in, 16)
            sp.dma_start(raw[:, 1, :].rearrange("p (k n) -> p k n", k=KH), w2T.rearrange("(k p) n -> p k n", p=P)).then_inc(w_in, 16)
            for dst, src in ((g1_sb, g1), (n1_sb, n1), (b1_sb, b1), (g2_sb, g2), (n2_sb, n2), (b2_sb, b2)):
                for n in range(2):
                    sp.dma_start(dst[64 * n:64 * (n + 1), :], src.partition_broadcast(64)).then_inc(v_in, 16)
            for t in range(0, TILES, 4):
                sp.wait_ge(second["used"], LEAD + t + 4)
                sp.dma_start(out[t * P:(t + 4) * P, :].rearrange("(t p) d -> p t d", p=P), X[:, t:t + 4, :]).then_inc(stored, 16)
            sp.wait_ge(stored, 16 * TILES // 4)

        @block.gpsimd
        def _(pool):
            pool.memset(ones[:, :], 1.0).then_inc(w_abs, 1)
            for sems in (first, second):
                for n in ("gained", "quant"):
                    pool.sem_inc(sems[n], LEAD)
            pool.sem_inc(first["y_full"], LEAD)
            pool.wait_ge(v_in, 16 * VLOADS)

            def layer(sems, width, gain, shift, bias):
                def turn(i, par):
                    if live(i):
                        t, zs = i, z[:, par, 0:width]
                        pool.wait_ge(sems["centred"], has(t))
                        pool.tensor_tensor(zs, zs, gain[:, :], ALU.mult).then_inc(sems["gained"], 1)
                        pool.wait_ge(sems["gained"], has(t))
                        pool.wait_ge(sems["rounded"], two_ago(t))
                        pool.tensor_tensor(h[:, par, 0:width], zs, shift[:, :], ALU.add).then_inc(sems["quant"], 1)
                    if bias and live(i - 4):
                        t = i - 4
                        pool.wait_ge(first["used"], has(t))
                        pool.tensor_tensor(y[:, par, :], y[:, par, :], b1_sb[:, :], ALU.add).then_inc(first["y_full"], 1)

                turns(pool, 4 if bias else 0, turn)

            layer(first, DIM, g1_sb, n1_sb, True)
            layer(second, HID, g2_sb, n2_sb, False)

        @block.tensor
        def _(pe):
            pe.wait_ge(w_abs, 3)
            pe.matmul(ps_w[:, 0:2], ones[:, :], wsum[:, :], start=True, stop=True).then_inc(w_sum, 1)
            for sems in (first, second):
                for n in ("turned", "made"):
                    pe.sem_inc(sems[n], LEAD)
            pe.wait_ge(w_rounded, 1)

            def layer(sems, kin, width, w):
                def turn(i, par):
                    if live(i - 3):
                        t, s = i - 3, 1 - par
                        pe.wait_ge(sems["rounded"], has(t))
                        pe.wait_ge(sems["qT_in"], two_ago(t))
                        for k in range(kin):
                            mm = pe.transpose(ps_t[:, s, k * P:(k + 1) * P], q[:, s, k * P:(k + 1) * P], identb[:, :])
                        mm.then_inc(sems["turned"], 1)
                    if live(i - 4):
                        t, s = i - 4, par
                        pe.wait_ge(sems["qT_in"], has(t))
                        pe.wait_ge(sems["used"], two_ago(t))
                        for half in range((width + 511) // 512):
                            n = min(512, width)
                            for k in range(kin):
                                mm = pe.matmul(ps_y[:, s, half * n:(half + 1) * n], qT[:, s, k * P:(k + 1) * P],
                                               w[:, k, half * n:(half + 1) * n], start=k == 0, stop=k == kin - 1)
                        mm.then_inc(sems["made"], 1)

                turns(pe, LAG, turn)

            layer(first, KD, HID, w1q)
            pe.wait_ge(w_rounded, 2)
            layer(second, KH, DIM, w2q)

        @block.vector
        def _(dve):
            def less_mean(neg, mean, rst):
                dve.scalar_tensor_tensor(out=neg[:, :], in0=mean[:, :, 0], scalar=-1.0, in1=rst[:, :], op0=ALU.mult,
                                         op1=ALU.mult).then_inc(s_nmr, 1)

            def round_weight(n):
                dve.tensor_scalar(raw[:, n, :], raw[:, n, :], winv[:, n:n + 1], ROUND, ALU.mult, ALU.add).then_inc(w_chain, 1)
                dve.wait_ge(w_chain, 4 + 2 * n)
                dve.tensor_scalar(raw[:, n, :], raw[:, n, :], ROUND, 1.0, ALU.subtract, ALU.min).then_inc(w_chain, 1)
                dve.wait_ge(w_chain, 5 + 2 * n)
                dve.tensor_scalar(wq[:, n, :], raw[:, n, :], -1.0, None, ALU.max).then_inc(w_rounded, 1)

            norm_stats(dve, s_root, X, stats, mv, root, rstd, s_stats, s_var, s_rstd)
            less_mean(nmr, mv, rstd)
            dve.wait_ge(w_sum, 1)
            dve.tensor_scalar(wmean[:, :], ps_w[:, 0:2], 1.0 / (DIM * HID), 1e-5, ALU.mult, ALU.max).then_inc(w_chain, 1)
            dve.wait_ge(w_chain, 1)
            dve.reciprocal(winv[:, :], wmean[:, :]).then_inc(w_chain, 1)
            dve.tensor_scalar(wfac[:, :], wmean[:, :], 1.0 / 127.0, None, ALU.mult).then_inc(w_chain, 1)
            dve.wait_ge(w_chain, 3)
            round_weight(0)
            for sems in (first, second):
                dve.sem_inc(sems["scaled"], LEAD)
            dve.sem_inc(second["used"], LEAD)
            dve.wait_ge(v_in, 16 * VLOADS)

            def quantise(sems, t, s, width, wn):
                col = bass.ds(t, 1)
                hs = h[:, s, 0:width]
                dve.wait_ge(sems["quant"], has(t))
                dve.tensor_reduce(amax[:, col], hs, AX.X, ALU.max, apply_absolute_value=True).then_inc(sems["scaled"], 1)
                dve.wait_ge(sems["scaled"], LEAD + 6 * t + 1)
                dve.tensor_scalar(amax[:, col], amax[:, col], 1e-5, None, ALU.max).then_inc(sems["scaled"], 1)
                dve.wait_ge(sems["scaled"], LEAD + 6 * t + 2)
                dve.reciprocal(ainv[:, col], amax[:, col]).then_inc(sems["scaled"], 1)
                dve.tensor_scalar(fac[:, col], amax[:, col], wfac[:, wn:wn + 1], None, ALU.mult).then_inc(sems["scaled"], 1)
                dve.wait_ge(sems["scaled"], LEAD + 6 * t + 4)
                dve.tensor_scalar(hs, hs, ainv[:, col], 127.0, ALU.mult, ALU.mult).then_inc(sems["scaled"], 1)
                dve.wait_ge(sems["scaled"], LEAD + 6 * t + 5)
                dve.tensor_scalar(hs, hs, 127.0, ROUND, ALU.min, ALU.add).then_inc(sems["scaled"], 1)

            def turn1(i, par):
                if live(i - 1):
                    t = i - 1
                    quantise(first, t, 1 - par, DIM, 0)
                    dve.tensor_tensor(X[:, t, :], X[:, t, :], b2_sb[:, :], ALU.add).then_inc(biased, 1)
                if live(i - 6):
                    t = i - 6
                    dve.wait_ge(first["gelued"], has(t))
                    for n in range(2):
                        dve.bn_stats(stats2[:, t, 6 * n:6 * n + 6], G[:, t, n * 512:(n + 1) * 512]).then_inc(s_stats2, 1)

            turns(dve, 6, turn1)
            dve.wait_ge(s_stats2, 2 * TILES)
            for t in range(TILES):
                dve.bn_aggr(mv2[:, t, :], stats2[:, t, :]).then_inc(s_stats2, 1)
            dve.wait_ge(s_stats2, 3 * TILES)
            dve.tensor_scalar(root2[:, :], mv2[:, :, 1], EPS, None, ALU.add).then_inc(s_var2, 1)
            dve.wait_ge(s_root2, 1)
            dve.reciprocal(rstd2[:, :], root2[:, :]).then_inc(s_rstd2, 1)
            dve.wait_ge(s_rstd2, 1)
            less_mean(nmr2, mv2, rstd2)
            round_weight(1)

            def turn2(i, par):
                if live(i - 1):
                    quantise(second, i - 1, 1 - par, HID, 1)
                if live(i - 5):
                    t, s = i - 5, 1 - par
                    dve.wait_ge(second["made"], has(t))
                    dve.wait_ge(biased, TILES)
                    dve.scalar_tensor_tensor(out=X[:, t, :], in0=ps_y[:, s, 0:DIM], scalar=fac[:, bass.ds(t, 1)],
                                             in1=X[:, t, :], op0=ALU.mult, op1=ALU.add).then_inc(second["used"], 1)

            turns(dve, 5, turn2)

        @block.scalar
        def _(act):
            act.wait_ge(w_in, 32)
            for n in range(2):
                act.activation(G[:, 2 * n:2 * n + 2, :].rearrange("p t n -> p (t n)"), raw[:, n, :], ACT.Abs, accum_out=wsum[:, n:n + 1]).then_inc(w_abs, 1)
            act.wait_ge(s_var, 1)
            act.activation(root[:, :], root[:, :], ACT.Sqrt).then_inc(s_root, 1)
            for sems in (first, second):
                for n in ("centred", "rounded", "qT_in"):
                    act.sem_inc(sems[n], LEAD)
            for n in ("used", "gelued"):
                act.sem_inc(first[n], LEAD)

            def layer(sems, width, x, rst, neg, gelu):
                def turn(i, par):
                    if live(i - 2):
                        t, s = i - 2, par
                        act.wait_ge(sems["scaled"], LEAD + 6 * t + 6)
                        act.wait_ge(sems["turned"], two_ago(t))
                        act.activation(q[:, s, 0:width], h[:, s, 0:width], ACT.Copy, bias=-ROUND).then_inc(sems["rounded"], 1)
                    if live(i):
                        t, s = i, par
                        act.wait_ge(sems["quant"], two_ago(t))
                        act.activation(z[:, s, 0:width], x[:, t, :], ACT.Identity, bias=neg[:, bass.ds(t, 1)],
                                       scale=rst[:, bass.ds(t, 1)]).then_inc(sems["centred"], 1)
                    if live(i - 3):
                        t, s = i - 3, 1 - par
                        act.wait_ge(sems["turned"], has(t))
                        act.wait_ge(sems["made"], two_ago(t))
                        act.activation(qT[:, s, 0:width], ps_t[:, s, 0:width], ACT.Copy).then_inc(sems["qT_in"], 1)
                    if gelu and live(i - 4):
                        t, s = i - 4, par
                        act.wait_ge(sems["made"], has(t))
                        act.wait_ge(sems["gelued"], two_ago(t))
                        act.activation(y[:, s, :], ps_y[:, s, :], ACT.Identity, scale=fac[:, bass.ds(t, 1)]).then_inc(sems["used"], 1)
                    if gelu and live(i - 5):
                        t, s = i - 5, 1 - par
                        act.wait_ge(sems["y_full"], has(t))
                        act.activation(G[:, t, :], y[:, s, :], ACT.Gelu).then_inc(sems["gelued"], 1)

                turns(act, 5 if gelu else 3, turn)

            act.wait_ge(s_nmr, 1)
            layer(first, DIM, X, rstd, nmr, True)
            act.wait_ge(s_var2, 1)
            act.activation(root2[:, :], root2[:, :], ACT.Sqrt).then_inc(s_root2, 1)
            act.wait_ge(s_nmr, 2)
            layer(second, HID, G, rstd2, nmr2, False)


def program(nc, a, out):
    with ExitStack() as ctx:
        X = ctx.enter_context(nc.sbuf_tensor("X", [P, TILES, DIM], F32))
        ident = ctx.enter_context(nc.sbuf_tensor("ident", [P, P], F32))
        identb = ctx.enter_context(nc.sbuf_tensor("identb", [P, P], BF16))
        x_loaded = ctx.enter_context(nc.semaphore("x_loaded"))
        phase_xattn0(nc, X, ident, x_loaded, a["x"], a["ctxT"], a["WqT0"], a["Wk0"], a["Wv0"], a["Wo0"], a["bo0"],
                     a["mask2"], a["ident"])
        qkd = nc.dram_tensor("qk_parts", (2, PARTS, BATCH * P, SEQ), BF16).ap()
        aon = nc.dram_tensor("attn_sums", (BATCH * P, SEQ), F32).ap()
        aod = nc.dram_tensor("attn_weights", (BATCH * HEADS, SEQ), F32).ap()
        with ExitStack() as attn:
            B = AttentionBuffers(Scope(nc, attn, "attn"))
            phase_qkv(nc, X, ident, identb, B, qkd, a["Wq"], a["Wk"], a["Wv"], a["qb"], a["kb"], a["vb"])
            phase_attention(nc, ident, identb, B, qkd, aon, aod)
        phase_moe(nc, X, ident, aon, aod, a["ow"], a["ob"], a["rw"], a["rb"], a["b2"], a["iota"], a["w1"], a["b1"],
                  a["w2"])
        phase_xattn1(nc, X, ident, a["ctxT"], a["Wq1"], a["Wk1"], a["Wv1"], a["Wo1"], a["bq1"], a["bk1"], a["bv1"],
                     a["bo1"], a["mask8"])
        phase_ffn(nc, X, ident, identb, out, a["f1T"], a["f2T"], a["fb1"], a["fb2"], a["g1"], a["n1"], a["g2"], a["n2"])


def layout(inputs):
    import numpy as np

    g = {k: np.asarray(v) for k, v in inputs.items()}
    c = np.ascontiguousarray
    kv1 = g["L1_xattn_Wkv"].reshape(16, 2, 16, CDIM)
    bkv1 = g["L1_xattn_bkv"].reshape(16, 2, 16)

    def by_dimension(w):
        return w.reshape(-1, HEADS // GROUP, GROUP, HD).transpose(0, 1, 3, 2).reshape(-1, P)

    a = {
        "x": c(g["x"].reshape(-1, DIM)),
        "ctxT": c(g["ctx_768"].reshape(-1, CDIM).T),
        "WqT0": c(g["L0_xattn_Wq"].T), "Wk0": g["L0_xattn_Wk"], "Wv0": g["L0_xattn_Wv"],
        "Wo0": g["L0_xattn_Wo"], "bo0": g["L0_xattn_bo"],
        "ident": np.eye(P, dtype=np.float32),
        "Wq": by_dimension(g["L0_ffn_q_w"].reshape(DIM, HEADS, 2 * HD)[:, :, :HD]),
        "qb": by_dimension(g["L0_ffn_q_b"].reshape(1, HEADS, 2 * HD)[:, :, :HD]).T,
        "Wk": by_dimension(g["L0_ffn_k_w"]), "kb": by_dimension(g["L0_ffn_k_b"]).T,
        "Wv": g["L0_ffn_v_w"], "vb": g["L0_ffn_v_b"],
        "ow": g["L0_ffn_o_w"][:P], "ob": g["L0_ffn_o_b"].reshape(KD, P).T,
        "rw": g["L0_ffn_router_w"], "rb": g["L0_ffn_router_b"], "b2": g["L0_ffn_b2"].reshape(-1),
        "iota": np.tile(np.arange(EXPERTS, dtype=np.float32), (P, 1)),
        "w1": g["L0_ffn_w1"], "w2": g["L0_ffn_w2"], "b1": g["L0_ffn_b1"].reshape(EXPERTS, FT, P).transpose(0, 2, 1),
        "Wq1": g["L1_xattn_Wq"].T, "Wo1": g["L1_xattn_Wo"].T,
        "Wk1": kv1[:, 0].reshape(DIM, CDIM).T, "Wv1": kv1[:, 1].reshape(DIM, CDIM).T,
        "bq1": g["L1_xattn_bq"].reshape(GROUPS1, P).T, "bo1": g["L1_xattn_bo"],
        "bk1": bkv1[:, 0].reshape(GROUPS1, P).T, "bv1": bkv1[:, 1].reshape(GROUPS1, P).T,
        "f1T": g["L1_ffn_w1"].T, "f2T": g["L1_ffn_w2"].T, "fb1": g["L1_ffn_b1"], "fb2": g["L1_ffn_b2"],
        "g1": g["L1_ffn_ln1_g"], "n1": g["L1_ffn_ln1_b"], "g2": g["L1_ffn_ln2_g"], "n2": g["L1_ffn_ln2_b"],
        "mask8": np.repeat(np.eye(GH, dtype=np.float32), P // GH, axis=0),
        "mask2": np.repeat(np.eye(2, dtype=np.float32), 64, axis=0),
    }
    return {k: c(v) for k, v in a.items()}


def kernel(**inputs):
    import concourse.bacc as bacc
    from concourse.bass_utils import run_bass_kernel_spmd

    nc = bacc.Bacc("TRN2", target_bir_lowering=False, num_devices=1)
    arrays = layout(inputs)
    a = {k: nc.dram_tensor(k + "_dram", v.shape, mybir.dt.from_np(v.dtype), kind="ExternalInput").ap()
         for k, v in arrays.items()}
    out = nc.dram_tensor("out_dram", (BATCH * SEQ, DIM), F32, kind="ExternalOutput").ap()
    program(nc, a, out)
    r = run_bass_kernel_spmd(nc, [{k + "_dram": v for k, v in arrays.items()}], core_ids=[0])
    return r.results[0]["out_dram"].reshape(BATCH, SEQ, DIM)
```

```python
from contextlib import ExitStack

import concourse.bass as bass
import numpy as np
from concourse import mybir

F32 = mybir.dt.float32
F32R = mybir.dt.float32r
BF16 = mybir.dt.bfloat16
U32 = mybir.dt.uint32
ALU = mybir.AluOpType
ACT = mybir.ActivationFunctionType
AX = mybir.AxisListType

P = 128
BATCH, SEQ, DIM = 2, 1024, 256
TILES = BATCH * SEQ // P
PAIRS = TILES // 2
TILES_PER_BATCH = SEQ // P
KD = DIM // P
CTX, CDIM = 77, 192
C2 = CDIM - P
EPS = 1e-5

GH = 8
HJ = GH * CTX
HALF = HJ // 2
HJT = (HJ + P - 1) // P
HJR = HJ - (HJT - 1) * P


class Scope:

    def __init__(self, nc, ctx, tag):
        self.nc, self.ctx, self.tag, self.sems = nc, ctx, tag, []
        ctx.callback(self.clear)

    def sb(self, name, shape, dt=F32):
        return self.ctx.enter_context(self.nc.sbuf_tensor(f"{self.tag}_{name}", shape, dt))

    def ps(self, name, shape, dt=F32):
        return self.ctx.enter_context(self.nc.psum_tensor(f"{self.tag}_{name}", shape, dt))

    def sem(self, name):
        self.sems.append(self.nc.alloc_semaphore(f"{self.tag}_{name}"))
        return self.sems[-1]

    def clear(self):
        self.nc.clear_and_free_semaphores(self.sems)
        self.nc.all_engine_barrier()


LEAD = 3


def has(t):
    return t + 1 + LEAD


def two_ago(t):
    return t - 1 + LEAD


def one_ago(t):
    return t + LEAD


def live(t):
    return not isinstance(t, int) or 0 <= t < TILES


def is_turn(i, n):
    return isinstance(i, int) and i == n


def tile_of(t, parity):
    return parity * TILES_PER_BATCH + t // 2


def turns(eng, lag, turn):
    head = (lag + 1) // 2
    for i in range(2 * head):
        turn(i, i % 2)
    with eng.Fori(head, PAIRS) as pair:
        turn(pair * 2, 0)
        turn(pair * 2 + 1, 1)
    for i in range(TILES, TILES + lag):
        turn(i, i % 2)


def norm_stats(dve, act_done, stats, mv, root, rstd, s_stats, s_var, s_rstd, before):
    for t in range(TILES):
        dve.bn_aggr(mv[:, t, :], stats[:, t, :]).then_inc(s_stats, 1)
    dve.wait_ge(s_stats, before + TILES)
    dve.tensor_scalar(root[:, :], mv[:, :, 1], EPS, None, ALU.add).then_inc(s_var, 1)
    dve.wait_ge(act_done, 1)
    dve.reciprocal(rstd[:, :], root[:, :]).then_inc(s_rstd, 1)
    dve.wait_ge(s_rstd, 1)


def phase_xattn0(nc, X, stats, prefetch, set_up, ident, x_loaded, x, ctxT, WqT, Wk, Wv, Wo, bo, mask2, identd):
    with ExitStack() as ctx:
        m = Scope(nc, ctx, "xa0")
        R = 4
        pair = 2 * CTX
        ctx_sb = m.sb("ctx", [P, 2, BATCH * CTX])
        wqT = m.sb("wqT", [P, R, DIM])
        wk = m.sb("wk", [P, 2, 512])
        wv = m.sb("wv", [P, 2, 512])
        wo = m.sb("wo", [P, R, DIM])
        bo_sb = m.sb("bo", [P, DIM])
        mask = m.sb("mask", [P, 2])
        kblk = m.sb("kblk", [P, BATCH, R, pair])
        vblk = m.sb("vblk", [P, BATCH, R, HJ])
        G = m.sb("G", [P, BATCH, KD, HJ])
        U = m.sb("U", [P, BATCH, HJT, DIM])
        mv = m.sb("mv", [P, TILES, 2])
        root = m.sb("root", [P, TILES])
        rstd = m.sb("rstd", [P, TILES])
        xn = m.sb("xn", [P, 2, DIM])
        xT = m.sb("xT", [P, 2, KD, P])
        mx = m.sb("mx", [P, 2, GH])
        sm = m.sb("sm", [P, 2, GH])
        rc = m.sb("rc", [P, 2, GH])
        pr = m.sb("pr", [P, 2, HJ])
        pT = m.sb("pT", [P, 2, HJT, P])
        ps_x = m.ps("ps_x", [P, 512])
        ps_s = m.ps("ps_s", [P, 2, 2, 512])
        ps_p = m.ps("ps_p", [P, 2, 512])
        ps_o = m.ps("ps_o", [P, 512])

        kv_in, w_in, bo_in, zeroed = m.sem("kv_in"), m.sem("w_in"), m.sem("bo_in"), m.sem("zeroed")
        prep_pe, prep_dve, prep_act = m.sem("prep_pe"), m.sem("prep_dve"), m.sem("prep_act")
        s_stats, s_var, s_root, s_rstd = m.sem("s_stats"), m.sem("s_var"), m.sem("s_root"), m.sem("s_rstd")
        normed, turned, xT_in = m.sem("normed"), m.sem("turned"), m.sem("xT_in")
        scored, maxed, shifted = m.sem("scored"), m.sem("maxed"), m.sem("shifted")
        exped, summed, inverted, weighted = m.sem("exped"), m.sem("summed"), m.sem("inverted"), m.sem("weighted")
        pturned, pT_in, projected = m.sem("pturned"), m.sem("pT_in"), m.sem("projected")
        biased, added, s_next = m.sem("biased"), m.sem("added"), m.sem("s_next")

        KV_LOADS, LOADS, BO_LOADS = 7, 3, 2
        LAG = 4

        def U_rows(i):
            return P if i < HJT - 1 else HJR

        def U_bank(n):
            return ps_o if n % 2 else ps_p[:, 0, :]

        def U_of_turn(i):
            return range(*((2 * HJT * k + 2) // 3 for k in (i, i + 1))) if isinstance(i, int) and i < 3 else ()

        block = ctx.enter_context(nc.Block())

        @block.sync
        def _(sp):
            for k, (at, rows) in enumerate(((0, P), (P, C2))):
                sp.dma_start(ctx_sb[0:rows, k, :], ctxT[at:at + rows, :]).then_inc(kv_in, 16)
                sp.dma_start(wk[0:rows, k, :], Wk[at:at + rows, :]).then_inc(kv_in, 16)
                sp.dma_start(wv[0:rows, k, :], Wv[at:at + rows, :]).then_inc(kv_in, 16)
            sp.dma_start(mask[:, :], mask2).then_inc(kv_in, 16)
            sp.dma_start(wqT[:, :, :], WqT.rearrange("(r p) c -> p r c", p=P)).then_inc(w_in, 16)
            sp.dma_start(wo[:, :, :], Wo.rearrange("(r p) c -> p r c", p=P)).then_inc(w_in, 16)
            sp.dma_start(ident[:, :], identd).then_inc(w_in, 16)
            sp.dma_start(X[:, :, :], x.rearrange("(t p) d -> p t d", p=P)).then_inc(x_loaded, 16)
            sp.dma_start(bo_sb[0:64, :], bo.partition_broadcast(64)).then_inc(bo_in, 16)
            sp.dma_start(bo_sb[64:P, :], bo.partition_broadcast(64)).then_inc(bo_in, 16)
            prefetch(sp)

        @block.tensor
        def _(pe):
            pe.wait_ge(kv_in, 16 * KV_LOADS)
            for w, bank0 in ((wk, 0), (wv, 1)):
                for r in range(R):
                    for k, rows in enumerate((P, C2)):
                        mm = pe.matmul(ps_s[:, bank0, r // 2, (r % 2) * pair:(r % 2 + 1) * pair],
                                       w[0:rows, k, r * P:(r + 1) * P], ctx_sb[0:rows, k, :],
                                       start=k == 0, stop=k == 1)
                mm.then_inc(prep_pe, 1)
            pe.wait_ge(w_in, 16 * LOADS)
            for b in range(BATCH):
                for k in range(KD):
                    n = b * KD + k
                    pe.wait_ge(prep_dve, 1)
                    pe.wait_ge(prep_dve, 2)
                    if n >= 2:
                        pe.wait_ge(prep_act, n - 1)
                    for r in range(R):
                        mm = pe.matmul(ps_s[:, n % 2, r // 2, (r % 2) * pair:(r % 2 + 1) * pair],
                                       wqT[:, r, k * P:(k + 1) * P], kblk[:, b, r, :],
                                       start=True, stop=True)
                    mm.then_inc(prep_pe, 1)

            def make_U(which):
                for n in which:
                    b, i = n // HJT, n % HJT
                    if n >= 2:
                        pe.wait_ge(prep_act, 3 + n)
                    rows = U_rows(i)
                    over = [r for r in range(R) if r * pair < i * P + rows and (r + 1) * pair > i * P]
                    for r in over:
                        mm = pe.matmul(U_bank(n)[0:rows, 0:DIM], vblk[:, b, r, i * P:i * P + rows], wo[:, r, :],
                                       start=r == over[0], stop=r == over[-1])
                    mm.then_inc(prep_pe, 1)

            for s in (turned, scored, pturned, projected):
                pe.sem_inc(s, LEAD)
            pe.wait_ge(prep_act, 4)

            def turn(i, par):
                if is_turn(i, 3):
                    pe.wait_ge(prep_act, 4 + 2 * HJT)
                if live(i - 1):
                    t, s = i - 1, 1 - par
                    pe.wait_ge(xT_in, has(t))
                    pe.wait_ge(shifted, two_ago(t))
                    for half in range(2):
                        for k in range(KD):
                            mm = pe.matmul(ps_s[:, s, half, 0:HALF], xT[:, s, k, :],
                                           G[:, s, k, half * HALF:(half + 1) * HALF],
                                           start=k == 0, stop=k == KD - 1)
                    mm.then_inc(scored, 1)
                if live(i):
                    t = i
                    pe.wait_ge(normed, has(t))
                    pe.wait_ge(xT_in, one_ago(t))
                    for k in range(KD):
                        mm = pe.transpose(ps_x[:, k * P:(k + 1) * P], xn[:, par, k * P:(k + 1) * P], ident[:, :])
                    mm.then_inc(turned, 1)
                make_U(U_of_turn(i))
                if live(i - 3):
                    t, s = i - 3, 1 - par
                    pe.wait_ge(weighted, has(t))
                    pe.wait_ge(pT_in, one_ago(t))
                    for j in range(HJT):
                        rows = U_rows(j)
                        mm = pe.transpose(ps_p[0:rows, j // 4, (j % 4) * P:(j % 4 + 1) * P],
                                          pr[:, s, j * P:j * P + rows], ident[:, :])
                    mm.then_inc(pturned, 1)
                if live(i - 4):
                    t, s = i - 4, par
                    pe.wait_ge(pT_in, has(t))
                    pe.wait_ge(added, one_ago(t))
                    for j in range(HJT):
                        rows = U_rows(j)
                        mm = pe.matmul(ps_o[:, 0:DIM], pT[0:rows, s, j, :], U[0:rows, s, j, :],
                                       start=j == 0, stop=j == HJT - 1)
                    mm.then_inc(projected, 1)

            turns(pe, LAG, turn)

        @block.vector
        def _(dve):
            dve.memset(vblk[:, :, :, :], 0.0).then_inc(zeroed, 1)
            dve.wait_ge(kv_in, 16 * KV_LOADS)
            dve.wait_ge(prep_pe, 1)
            for b in range(BATCH):
                for r in range(R):
                    src = ps_s[:, 0, r // 2, (r % 2) * pair + b * CTX:(r % 2) * pair + (b + 1) * CTX]
                    ins = dve.tensor_tensor(kblk[:, b, r, :].rearrange("p (h j) -> p h j", h=2),
                                            src.unsqueeze(1).to_broadcast([P, 2, CTX]),
                                            mask[:, :].unsqueeze(2).to_broadcast([P, 2, CTX]), ALU.mult)
            ins.then_inc(prep_dve, 1)
            dve.wait_ge(prep_pe, 2)
            dve.wait_ge(zeroed, 1)
            for b in range(BATCH):
                for r in range(R):
                    src = ps_s[:, 1, r // 2, (r % 2) * pair + b * CTX:(r % 2) * pair + (b + 1) * CTX]
                    ins = dve.tensor_tensor(vblk[:, b, r, r * pair:(r + 1) * pair].rearrange("p (h j) -> p h j", h=2),
                                            src.unsqueeze(1).to_broadcast([P, 2, CTX]),
                                            mask[:, :].unsqueeze(2).to_broadcast([P, 2, CTX]), ALU.mult)
            ins.then_inc(prep_dve, 1)

            dve.wait_ge(x_loaded, 16)
            for t in range(TILES):
                dve.bn_stats(stats[:, t, :], X[:, t, :]).then_inc(s_stats, 1)
            dve.wait_ge(s_stats, TILES)
            norm_stats(dve, s_root, stats, mv, root, rstd, s_stats, s_var, s_rstd, TILES)
            for s in (normed, maxed, shifted, summed, inverted, added):
                dve.sem_inc(s, LEAD)

            def turn(i, par):
                if live(i):
                    t = i
                    dve.wait_ge(turned, two_ago(t))
                    x = tile_of(t, par)
                    dve.tensor_scalar(xn[:, par, :], X[:, x, :], mv[:, x, 0:1], rstd[:, bass.ds(x, 1)],
                                      ALU.subtract, ALU.mult).then_inc(normed, 1)
                if live(i - 5):
                    t, x = i - 5, tile_of(i - 5, 1 - par)
                    dve.wait_ge(projected, has(t))
                    dve.wait_ge(biased, has(t))
                    dve.tensor_tensor(X[:, x, :], ps_o[:, 0:DIM], X[:, x, :], ALU.add).then_inc(added, 1)
                if live(i - 1):
                    t, s = i - 1, 1 - par
                    dve.wait_ge(scored, has(t))
                    src = ps_s[:, s, :, 0:HALF].rearrange("p a (h j) -> p a h j", j=CTX)
                    dve.tensor_reduce(mx[:, s, :].rearrange("p (a h) -> p a h", a=2), src, AX.X,
                                      ALU.max).then_inc(maxed, 1)
                    dve.wait_ge(maxed, has(t))
                    dve.wait_ge(pturned, two_ago(t))
                    dve.tensor_tensor(pr[:, s, :].rearrange("p (a h j) -> p a h j", a=2, j=CTX), src,
                                      mx[:, s, :].rearrange("p (a h) -> p a h", a=2).unsqueeze(3)
                                      .to_broadcast([P, 2, GH // 2, CTX]), ALU.subtract).then_inc(shifted, 1)
                if live(i - 2):
                    t, s = i - 2, par
                    dve.wait_ge(exped, has(t))
                    dve.wait_ge(weighted, two_ago(t))
                    dve.tensor_reduce(sm[:, s, :], pr[:, s, :].rearrange("p (h j) -> p h j", j=CTX), AX.X,
                                      ALU.add).then_inc(summed, 1)
                    dve.wait_ge(summed, has(t))
                    dve.reciprocal(rc[:, s, :], sm[:, s, :]).then_inc(inverted, 1)
                if live(i - 6):
                    t, x = i - 6, tile_of(i - 6, par)
                    dve.wait_ge(added, has(t))
                    dve.bn_stats(stats[:, x, :], X[:, x, :]).then_inc(s_next, 1)

            turns(dve, LAG + 2, turn)

        @block.gpsimd
        def _(pool):
            for s in (weighted, biased):
                pool.sem_inc(s, LEAD)
            set_up(pool)
            pool.wait_ge(bo_in, 16 * BO_LOADS)

            def turn(i, par):
                if live(i - 1):
                    t, x = i - 1, tile_of(i - 1, 1 - par)
                    pool.wait_ge(normed, has(t))
                    pool.tensor_tensor(X[:, x, :], X[:, x, :], bo_sb[:, :], ALU.add).then_inc(biased, 1)
                if live(i - 2):
                    t, s = i - 2, par
                    pool.wait_ge(inverted, has(t))
                    v = pr[:, s, :].rearrange("p (h j) -> p h j", j=CTX)
                    pool.tensor_tensor(v, v, rc[:, s, :].unsqueeze(2).to_broadcast([P, GH, CTX]),
                                       ALU.mult).then_inc(weighted, 1)

            turns(pool, LAG, turn)

        @block.scalar
        def _(act):
            for n in range(BATCH * KD):
                act.wait_ge(prep_pe, 3 + n)
                act.activation(G[:, n // KD, n % KD, :].rearrange("p (a c) -> p a c", a=2),
                               ps_s[:, n % 2, :, 0:HALF], ACT.Copy).then_inc(prep_act, 1)
            act.wait_ge(s_var, 1)
            act.activation(root[:, :], root[:, :], ACT.Sqrt).then_inc(s_root, 1)
            for s in (xT_in, exped, pT_in):
                act.sem_inc(s, LEAD)

            def turn(i, par):
                if live(i):
                    t = i
                    act.wait_ge(turned, has(t))
                    act.wait_ge(scored, two_ago(t))
                    act.activation(xT[:, par, :, :].rearrange("p k n -> p (k n)"), ps_x[:, 0:DIM],
                                   ACT.Copy).then_inc(xT_in, 1)
                for n in U_of_turn(i):
                    act.wait_ge(prep_pe, 3 + BATCH * KD + n)
                    rows = U_rows(n % HJT)
                    act.activation(U[0:rows, n // HJT, n % HJT, :], U_bank(n)[0:rows, 0:DIM],
                                   ACT.Copy).then_inc(prep_act, 1)
                if live(i - 3):
                    t, s = i - 3, 1 - par
                    act.wait_ge(pturned, has(t))
                    act.wait_ge(projected, two_ago(t))
                    act.activation(pT[:, s, 0:4, :].rearrange("p k n -> p (k n)"), ps_p[:, 0, :], ACT.Copy)
                    act.activation(pT[0:HJR, s, 4, :], ps_p[0:HJR, 1, 0:P], ACT.Copy).then_inc(pT_in, 1)
                if live(i - 1):
                    t, s = i - 1, 1 - par
                    act.wait_ge(shifted, has(t))
                    act.activation(pr[:, s, :], pr[:, s, :], ACT.Exp, scale=0.125).then_inc(exped, 1)

            turns(act, LAG, turn)


HEADS, HD = 16, 8
GROUP = 4
GROUPS = BATCH * HEADS // GROUP
GROWS = GROUP * HD
PARTS = 3
TERMS = PARTS * PARTS * HD
MAXROW = 96
KT = SEQ // P
CHUNK = 512
CHUNKS = BATCH * SEQ // CHUNK


SLOTS = 3


class AttentionBuffers:

    def __init__(self, m):
        self.V = m.sb("V", [P, GROUPS, KT, GROWS])
        self.q = m.sb("q", [P, SLOTS, GROUP, SEQ], BF16)
        self.k = m.sb("k", [P, SLOTS, GROUP, SEQ], BF16)
        self.v = m.sb("v", [P, SLOTS, KT, GROUP, 32])
        self.qk_in = [m.sem(f"qk_in{n}") for n in range(SLOTS)]
        self.fixed = m.sem("fixed")
        self.stored = [m.sem(f"stored{n}") for n in range(2)]
        self.all_stored = 16 * CHUNKS

    def set_up(self, pool):
        two_minus_ones = float(np.array([0xBF80BF80], np.uint32).view(np.float32)[0])
        for n, (dst, value) in enumerate(((self.q[64:MAXROW, :, :, :].bitcast(F32), 0.0),
                                          (self.k[64:MAXROW, :, :, :].bitcast(F32), 0.0),
                                          (self.k[MAXROW:MAXROW + PARTS, :, :, :].bitcast(F32), two_minus_ones),
                                          (self.v[:, :, :, :, :], 0.0), (self.v[:, :, :, :, HD:HD + 1], 1.0))):
            if n:
                pool.wait_ge(self.fixed, n)
            pool.memset(dst, value).then_inc(self.fixed, 1)

    def load(self, sp, qkd, g, slot):
        rows = bass.ds(g * GROWS, GROWS)
        for a in range(PARTS):
            at = slice(a * PARTS * HD, (a + 1) * PARTS * HD)
            sp.dma_start(self.q[at, slot, :, :], qkd[0, :, rows, :].rearrange("b (d j) n -> b d (j n)", d=HD)
                         ).then_inc(self.qk_in[slot], 16)
            sp.dma_start(self.k[at, slot, :, :], qkd[1, a, rows, :].rearrange("(d j) n -> d (j n)", d=HD).unsqueeze(0)
                         .to_broadcast([PARTS, HD, GROUP * SEQ])).then_inc(self.qk_in[slot], 16)


class QkvWeights:

    def __init__(self, m):
        self.w = m.sb("w", [P, 3, KD, P])
        self.qb, self.kb = m.sb("qb", [P, 1]), m.sb("kb", [P, 1])
        self.vb = m.sb("vb", [P, P])
        self.w_in = m.sem("w_in")
        self.loads = 7

    def load(self, sp, Wq, Wk, Wv, qb, kb, vb):
        for n, src in enumerate((Wq, Wk, Wv)):
            sp.dma_start(self.w[:, n, :, :], src.rearrange("(k p) n -> p k n", p=P)).then_inc(self.w_in, 16)
        sp.dma_start(self.qb[:, :], qb).then_inc(self.w_in, 16)
        sp.dma_start(self.kb[:, :], kb).then_inc(self.w_in, 16)
        for n in range(2):
            sp.dma_start(self.vb[64 * n:64 * (n + 1), :], vb.partition_broadcast(64)).then_inc(self.w_in, 16)


def phase_qkv(nc, X, stats, W, ident, identb, B, qkd):
    with ExitStack() as ctx:
        m = Scope(nc, ctx, "qkv")
        V = B.V
        w, qb_sb, kb_sb, vb_sb, w_in = W.w, W.qb, W.kb, W.vb, W.w_in
        mv = m.sb("mv", [P, TILES, 2])
        root, rstd = m.sb("root", [P, TILES]), m.sb("rstd", [P, TILES])
        xn = m.sb("xn", [P, 2, 4, DIM])
        xT = m.sb("xT", [P, 2, KD, CHUNK])
        full = m.sb("full", [P, 2, 2, CHUNK])
        part = m.sb("part", [P, 2, 2, PARTS, CHUNK], BF16)
        ps_x = m.ps("ps_x", [P, KD, CHUNK])
        ps_qk = m.ps("ps_qk", [P, 2, 2, CHUNK])
        ps_v = m.ps("ps_v", [P, 4, P])
        s_stats, s_var, s_root, s_rstd = m.sem("s_stats"), m.sem("s_var"), m.sem("s_root"), m.sem("s_rstd")
        normed, turned, xT_in = m.sem("normed"), m.sem("turned"), m.sem("xT_in")
        qk_made, v_made, qk_full, v_in = m.sem("qk_made"), m.sem("v_made"), m.sem("qk_full"), m.sem("v_in")
        split_hi, rest1, split_mid, split_lo = m.sem("split_hi"), m.sem("rest1"), m.sem("split_mid"), m.sem("split_lo")
        residual, stored = m.sem("residual"), B.stored
        LOADS = W.loads
        STORES = 2
        scale = float(HD) ** -0.5

        block = ctx.enter_context(nc.Block())

        @block.sync
        def _(sp):
            for c in range(CHUNKS):
                s, b, at = c % 2, c // 2, (c % 2) * CHUNK
                sp.wait_ge(split_lo, 2 * c + 2)
                for n in range(2):
                    sp.dma_start(qkd[n, :, b * P:(b + 1) * P, at:at + CHUNK].rearrange("a p n -> p a n"),
                                 part[:, s, n, :, :]).then_inc(stored[s], 16)
                if c == CHUNKS // BATCH:
                    sp.wait_ge(stored[0], 16 * STORES)
                    sp.wait_ge(stored[1], 16 * STORES)
                    B.load(sp, qkd, 0, 0)

        @block.tensor
        def _(pe):
            pe.wait_ge(w_in, 16 * LOADS)

            def turn(c):
                s = c % 2
                pe.wait_ge(normed, c + 1)
                if c >= 1:
                    pe.wait_ge(xT_in, c)
                for t in range(4):
                    for k in range(KD):
                        mm = pe.transpose(ps_x[:, k, t * P:(t + 1) * P], xn[:, s, t, k * P:(k + 1) * P], ident[:, :])
                mm.then_inc(turned, 1)

            turn(0)
            for c in range(CHUNKS):
                s = c % 2
                if c + 1 < CHUNKS:
                    turn(c + 1)
                pe.wait_ge(xT_in, c + 1)
                if c >= 2:
                    pe.wait_ge(qk_full, 2 * (c - 1))
                for n in range(2):
                    for k in range(KD):
                        mm = pe.matmul(ps_qk[:, s, n, :], w[:, n, k, :], xT[:, s, k, :], start=k == 0, stop=k == KD - 1)
                mm.then_inc(qk_made, 1)
                if c >= 1:
                    pe.wait_ge(v_in, c)
                for t in range(4):
                    for k in range(KD):
                        mm = pe.matmul(ps_v[:, t, :], xT[:, s, k, t * P:(t + 1) * P], w[:, 2, k, :],
                                       start=k == 0, stop=k == KD - 1)
                mm.then_inc(v_made, 1)

        @block.vector
        def _(dve):
            norm_stats(dve, s_root, stats, mv, root, rstd, s_stats, s_var, s_rstd, 0)

            def norm(c):
                if c >= 2:
                    dve.wait_ge(turned, c - 1)
                    dve.wait_ge(residual, c - 1)
                for t in range(4):
                    n = 4 * c + t
                    ins = dve.tensor_scalar(xn[:, c % 2, t, :], X[:, n, :], mv[:, n, 0:1], rstd[:, n:n + 1],
                                            ALU.subtract, ALU.mult)
                ins.then_inc(normed, 1)

            norm(0)
            norm(1)
            dve.wait_ge(w_in, 16 * LOADS)
            for c in range(CHUNKS):
                s = c % 2
                dve.wait_ge(qk_made, c + 1)
                if c >= 2:
                    dve.wait_ge(split_lo, 2 * (c - 1))
                dve.tensor_scalar(full[:, s, 0, :], ps_qk[:, s, 0, :], qb_sb[:, :], scale, ALU.add,
                                  ALU.mult).then_inc(qk_full, 1)
                dve.tensor_scalar(full[:, s, 1, :], ps_qk[:, s, 1, :], kb_sb[:, :], None, ALU.add).then_inc(qk_full, 1)
                dve.wait_ge(v_made, c + 1)
                b = c // 2
                for t in range(4):
                    kt = (c % 2) * 4 + t
                    ins = dve.tensor_tensor(V[:, b * GROUP:(b + 1) * GROUP, kt, :],
                                            ps_v[:, t, :].rearrange("p (g n) -> p g n", g=GROUP),
                                            vb_sb[:, :].rearrange("p (g n) -> p g n", g=GROUP), ALU.add)
                ins.then_inc(v_in, 1)
                if c + 2 < CHUNKS:
                    norm(c + 2)
                dve.wait_ge(split_hi, c + 1)
                dve.tensor_tensor(full[:, s, :, :], full[:, s, :, :], part[:, s, :, 0, :], ALU.subtract).then_inc(rest1, 1)
                dve.wait_ge(split_mid, c + 1)
                for n in range(2):
                    dve.tensor_tensor(part[:, s, n, 2, :], full[:, s, n, :], part[:, s, n, 1, :],
                                      ALU.subtract).then_inc(split_lo, 1)

        @block.gpsimd
        def _(pool):
            for c in range(CHUNKS):
                pool.wait_ge(normed, c + 1)
                for t in range(4):
                    n = 4 * c + t
                    ins = pool.tensor_tensor(X[:, n, :], X[:, n, :], xn[:, c % 2, t, :], ALU.add)
                ins.then_inc(residual, 1)
            pool.tensor_copy(identb[:, :], ident[:, :]).then_inc(residual, 1)

        @block.scalar
        def _(act):
            act.wait_ge(s_var, 1)
            act.activation(root[:, :], root[:, :], ACT.Sqrt).then_inc(s_root, 1)

            def out(c):
                act.wait_ge(turned, c + 1)
                if c >= 2:
                    act.wait_ge(v_made, c - 1)
                act.activation(xT[:, c % 2, :, :], ps_x[:, :, :], ACT.Copy).then_inc(xT_in, 1)

            out(0)
            for c in range(CHUNKS):
                s = c % 2
                if c + 1 < CHUNKS:
                    out(c + 1)
                act.wait_ge(qk_full, 2 * c + 2)
                if c >= 2:
                    act.wait_ge(stored[s], 16 * STORES * (c // 2))
                act.activation(part[:, s, :, 0, :], full[:, s, :, :], ACT.Copy).then_inc(split_hi, 1)
                act.wait_ge(rest1, c + 1)
                act.activation(part[:, s, :, 1, :], full[:, s, :, :], ACT.Copy).then_inc(split_mid, 1)


STEPS = BATCH * KT * GROUP
UNITS = STEPS // GROUP
EARLY = 4
AHEAD = 10
BANKS = 3


def first_pass(last):
    items = []
    for j in range(GROUP):
        for n in range(EARLY if j == 0 else 0, 2 * KT):
            if j and n == 8:
                items.append(("turn", j - 1, 0, 0))
            items.append(("score", j, n // 2, n % 2))
    if not last:
        items += [("next", 0, n // 2, n % 2) for n in range(EARLY)]
    return items + [("turn", GROUP - 1, 0, 0)]


CYCLE, LAST_CYCLE = first_pass(False), first_pass(True)
NI = len(CYCLE)


def phase_attention(nc, prefetch, ident, identb, B, qkd, aon, aod):
    with ExitStack() as ctx:
        m = Scope(nc, ctx, "att")
        q, k, v, qk_in = B.q, B.k, B.v, B.qk_in
        e = m.sb("e", [P, 2, GROUP, 512])
        o = m.sb("o", [P, SLOTS, 2, 512])
        mh = m.sb("mh", [P, 2, 2 * KT])
        mf = m.sb("mf", [P, 2, KT])
        mr = m.sb("mr", [P, 2, KT])
        mp = m.sb("mp", [P, 2, PARTS, KT], BF16)
        mT = m.sb("mT", [PARTS * KT, 2, P], BF16)
        ps_s = m.ps("ps_s", [P, BANKS, 512])
        ps_m = m.ps("ps_m", [P, BANKS, 512])
        ps_o = m.ps("ps_o", [P, 2, 512])

        m_in = [m.sem(f"m_in{n}") for n in range(2)]
        v_in = m.sem("v_in")
        item_made, item_read = m.sem("item_made"), m.sem("item_read")
        m_hi, m_mid, m_parts = m.sem("m_hi"), m.sem("m_mid"), m.sem("m_parts")
        step_made, step_exp, summed, sums_out, stored = (m.sem("step_made"), m.sem("step_exp"), m.sem("summed"),
                                                         m.sem("sums_out"), m.sem("stored"))
        QKL = 2 * PARTS
        OST = GROUP + 1

        def groups(eng, run):
            run(0, 0)
            with eng.Fori(0, (GROUPS - 2) // SLOTS) as i:
                for s in range(SLOTS):
                    run(i * SLOTS + s + 1, (s + 1) % SLOTS)
            run(GROUPS - 1, (GROUPS - 1) % SLOTS)

        def first_group(g):
            return isinstance(g, int) and g == 0

        def last_group(g):
            return isinstance(g, int) and g == GROUPS - 1

        def cycle(g):
            return LAST_CYCLE if last_group(g) else CYCLE

        def items_to(g, n):
            return g * NI + n + EARLY

        def bank(slot, n):
            return (slot * NI + n + EARLY) % BANKS

        block = ctx.enter_context(nc.Block())

        @block.sync
        def _(sp):
            def maxima(g, slot):
                for j in range(GROUP):
                    sp.wait_ge(item_read, items_to(g, cycle(g).index(("turn", j, 0, 0)) + 1) + LEAD)
                    sp.dma_start(q[MAXROW:MAXROW + PARTS, slot, j, :], mT[:, j % 2, :]).then_inc(m_in[j % 2], 16)

            def store(g, slot):
                sp.wait_ge(sums_out, 2 * (g + 1) + LEAD)
                sp.dma_start(aod[bass.ds(g * GROUP, GROUP), :], o[HD:P:32, slot, :, :]).then_inc(stored, 16)
                for j in range(GROUP):
                    sp.dma_start(aon[bass.ds(g * GROWS + j * HD, HD), :],
                                 o[32 * j:32 * j + HD, slot, :, :]).then_inc(stored, 16)

            for n in range(2):
                sp.wait_ge(B.stored[n], B.all_stored)
            B.load(sp, qkd, 1, 1)
            prefetch(sp)
            maxima(0, 0)
            with sp.Fori(0, (GROUPS - 2) // SLOTS) as i:
                for s in range(SLOTS):
                    g = i * SLOTS + s
                    sp.wait_ge(step_exp, g * STEPS + LEAD)
                    B.load(sp, qkd, g + 2, (s + 2) % SLOTS)
                    maxima(g + 1, (s + 1) % SLOTS)
                    store(g, s)
            maxima(GROUPS - 1, (GROUPS - 1) % SLOTS)
            for g in (GROUPS - 2, GROUPS - 1):
                store(g, g % SLOTS)
            sp.wait_ge(stored, 16 * OST * GROUPS + LEAD)

        @block.tensor
        def _(pe):
            pe.sem_inc(summed, LEAD)

            def score_half(slot, j, t, half, count, b):
                pe.wait_ge(item_read, count - 2 + LEAD)
                pe.matmul(ps_m[:, b, :], q[0:MAXROW, slot, j, t * P:(t + 1) * P],
                          k[0:MAXROW, slot, j, half * 512:(half + 1) * 512], start=True, stop=True).then_inc(item_made, 1)

            def first(g, slot, frm, upto):
                for n in range(frm, upto):
                    what, j, t, half = cycle(g)[n]
                    if what != "turn":
                        if (what, t, half) == ("next", 0, 0):
                            load_wait(g + 1, (slot + 1) % SLOTS)
                        score_half((slot + (what == "next")) % SLOTS, j, t, half, items_to(g, n), bank(slot, n))
                    else:
                        pe.wait_ge(item_read, items_to(g, n) - 2 + LEAD)
                        pe.wait_ge(m_parts, g * GROUP + j + 1)
                        pe.transpose(ps_m[0:PARTS * KT, bank(slot, n), 0:P // 2].bitcast(BF16),
                                     mp[:, j % 2, :, :].rearrange("p a t -> p (a t)"), identb[:, :]).then_inc(item_made, 1)

            def load_wait(g, slot):
                pe.wait_ge(qk_in[slot], 16 * QKL * ((g - slot) // SLOTS + 1))

            def sums(g, slot, w, part):
                kt, half = w // 2, w % 2
                at = slice(part * 256, (part + 1) * 256)
                if part == 0:
                    pe.wait_ge(step_exp, g * STEPS + (w + 1) * GROUP + LEAD)
                    if kt == 0:
                        pe.wait_ge(sums_out, 2 * g - 1 + half + LEAD)
                    if w == 0:
                        pe.wait_ge(v_in, g + 1)
                for j in range(GROUP):
                    mm = pe.matmul(ps_o[32 * j:32 * (j + 1), half, at], v[:, slot, kt, j, :], e[:, w % 2, j, at],
                                   start=kt == part == 0, stop=kt == KT - 1 and part == 1)
                if part == 1:
                    mm.then_inc(summed, 1)

            def unit(g, slot, w, between, before):
                kt, half = w // 2, w % 2
                for j in range(GROUP):
                    u = w * GROUP + j
                    pe.wait_ge(step_exp, g * STEPS + u - 2 + LEAD)
                    pe.matmul(ps_s[:, (slot * STEPS + u) % BANKS, :], k[0:MAXROW + PARTS, slot, j, kt * P:(kt + 1) * P],
                              q[0:MAXROW + PARTS, slot, j, half * 512:(half + 1) * 512],
                              start=True, stop=True).then_inc(step_made, 1)
                    between(j)
                    if j % 2 == 1 and before is not None:
                        sums(*before, j // 2)

            def maxima_wait(g):
                for n in range(2):
                    pe.wait_ge(m_in[n], 16 * (GROUP // 2) * (g + 1))

            for n in range(2):
                pe.wait_ge(B.stored[n], B.all_stored)
            load_wait(0, 0)
            for n in range(EARLY):
                score_half(0, 0, n // 2, n % 2, n, n % BANKS)
            first(0, 0, 0, NI)
            first(1, 1, 0, EARLY)
            maxima_wait(0)
            unit(0, 0, 0, lambda j: first(1, 1, *(EARLY + (AHEAD - EARLY) * n // GROUP for n in (j, j + 1))), None)

            def run(g, slot, items, more):
                done = [0]

                def between(at):
                    upto = min(items, (at + 1) * NI // STEPS)
                    one = NI - AHEAD
                    for n in range(done[0], upto):
                        if n < one:
                            first(g + 1, (slot + 1) % SLOTS, AHEAD + n, AHEAD + n + 1)
                        else:
                            first(g + 2, (slot + 2) % SLOTS, n - one, n - one + 1)
                    done[0] = max(upto, done[0])

                for w in range(1, UNITS):
                    unit(g, slot, w, lambda j: between((w - 1) * GROUP + j), (g, slot, w - 1))
                if more:
                    maxima_wait(g + 1)
                    unit(g + 1, (slot + 1) % SLOTS, 0, lambda j: between((UNITS - 1) * GROUP + j), (g, slot, UNITS - 1))

            with pe.Fori(0, (GROUPS - 2) // SLOTS) as i:
                for s in range(SLOTS):
                    run(i * SLOTS + s, s, NI, True)
            run(GROUPS - 2, (GROUPS - 2) % SLOTS, len(LAST_CYCLE) - AHEAD, True)
            run(GROUPS - 1, (GROUPS - 1) % SLOTS, 0, False)
            for part in range(2):
                sums(GROUPS - 1, (GROUPS - 1) % SLOTS, UNITS - 1, part)

        @block.vector
        def _(dve):
            dve.sem_inc(item_read, LEAD)

            def maximum(head, s, t, half, count, b):
                dve.wait_ge(item_made, count + 1)
                if t == half == 0 and not (isinstance(head, int) and head < 2):
                    dve.wait_ge(m_parts, head - 1)
                dve.tensor_reduce(mh[:, s, 2 * t + half:2 * t + half + 1], ps_m[:, b, :], AX.X,
                                  ALU.max).then_inc(item_read, 1)
                if (t, half) == (KT - 1, 1):
                    dve.wait_ge(item_read, count + 1 + LEAD)
                    a, c = (mh[:, s, h:2 * KT:2] for h in range(2))
                    for dst in (mp[:, s, 0, :], mf[:, s, :]):
                        dve.tensor_tensor(dst, a, c, ALU.max).then_inc(m_hi, 1)

            def first(g, slot):
                for n, (what, j, t, half) in enumerate(cycle(g)):
                    if what != "turn":
                        head = g * GROUP + j + (GROUP if what == "next" else 0)
                        maximum(head, j % 2, t, half, items_to(g, n), bank(slot, n))
                    else:
                        dve.wait_ge(item_made, items_to(g, n) + 1)
                        if not (first_group(g) and j < 2):
                            dve.wait_ge(m_in[j % 2], 16 * (g * (GROUP // 2) + j // 2))
                        dve.tensor_copy(mT[:, j % 2, :], ps_m[0:PARTS * KT, bank(slot, n), 0:P // 2].bitcast(BF16)
                                        ).then_inc(item_read, 1)

            for n in range(EARLY):
                maximum(0, 0, n // 2, n % 2, n, n % BANKS)
            groups(dve, first)

        @block.gpsimd
        def _(pool):
            def first(g):
                for j in range(GROUP):
                    n = g * GROUP + j
                    s = j % 2
                    pool.wait_ge(m_hi, 2 * n + 2)
                    pool.tensor_tensor(mp[:, s, 1, :], mf[:, s, :], mp[:, s, 0, :], ALU.subtract).then_inc(m_mid, 1)
                    pool.tensor_tensor(mr[:, s, :], mf[:, s, :], mp[:, s, 0, :], ALU.subtract).then_inc(m_mid, 1)
                    pool.wait_ge(m_mid, 2 * n + 2)
                    pool.tensor_tensor(mp[:, s, 2, :], mr[:, s, :], mp[:, s, 1, :], ALU.subtract).then_inc(m_parts, 1)

            def values(g, slot):
                pool.tensor_copy(v[:, slot, :, :, 0:HD], B.V[:, g, :, :].rearrange("p t (j d) -> p t j d", d=HD)
                                 ).then_inc(v_in, 1)

            first(0)

            def run(g, slot):
                values(g, slot)
                if not last_group(g):
                    first(g + 1)

            groups(pool, run)

        @block.scalar
        def _(act):
            for s in (step_exp, sums_out, stored):
                act.sem_inc(s, LEAD)

            def out(g, slot, half):
                act.wait_ge(summed, (g + 1) * UNITS - 1 + half + LEAD)
                act.wait_ge(stored, 16 * OST * g + LEAD)
                act.activation(o[:, slot, half, :], ps_o[:, half, :], ACT.Copy).then_inc(sums_out, 1)

            def run(g, slot):
                for u in range(STEPS):
                    w, j = u // GROUP, u % GROUP
                    act.wait_ge(step_made, g * STEPS + u + 1)
                    if j == 0:
                        act.wait_ge(summed, g * UNITS + w - 1 + LEAD)
                    act.activation(e[:, w % 2, j, :], ps_s[:, (slot * STEPS + u) % BANKS, :], ACT.Exp).then_inc(step_exp, 1)
                    if u in (1, 5) and not first_group(g):
                        out(g - 1, (slot - 1) % SLOTS, u // 4)

            groups(act, run)
            for half in range(2):
                out(GROUPS - 1, (GROUPS - 1) % SLOTS, half)


EXPERTS, FF = 8, 512
FT = FF // P
CT = CHUNK // P


def f32(ap):
    return ap.bitcast(F32)


class RouterWeights:

    def __init__(self, m):
        self.ow, self.ob = m.sb("ow", [P, DIM]), m.sb("ob", [P, KD])
        self.rw, self.rb = m.sb("rw", [P, KD, EXPERTS]), m.sb("rb", [EXPERTS, 1])
        self.iota = m.sb("iota", [P, EXPERTS])
        self.b2 = m.sb("b2", [P, EXPERTS * DIM])
        self.w_in = m.sem("w_in")
        self.loads = 7

    def load(self, sp, ow, ob, rw, rb, b2, iota):
        for dst, src in ((self.ow, ow), (self.ob, ob), (self.rb, rb), (self.iota, iota)):
            sp.dma_start(dst[:, :], src).then_inc(self.w_in, 16)
        sp.dma_start(self.rw[:, :, :], rw.rearrange("(k p) e -> p k e", p=P)).then_inc(self.w_in, 16)
        for n in range(2):
            sp.dma_start(self.b2[64 * n:64 * (n + 1), :], b2.partition_broadcast(64)).then_inc(self.w_in, 16)


def phase_moe(nc, X, stats, R, prefetch, ident, aon, aod, w1, b1, w2):
    with ExitStack() as ctx:
        m = Scope(nc, ctx, "moe")
        mla_hi, mla_lo = m.sb("mla_hi", [P, KD, BATCH * SEQ], F32R), m.sb("mla_lo", [P, KD, BATCH * SEQ], F32R)
        acc = m.sb("acc", [P, TILES, DIM])
        ow_sb, ob_sb, rw_sb, rb_sb, iota_sb, b2_sb, w_in = R.ow, R.ob, R.rw, R.rb, R.iota, R.b2, R.w_in
        logit = m.sb("logit", [P, TILES, EXPERTS])
        top = m.sb("top", [P, TILES, 8])
        index = m.sb("index", [P, TILES, 8], U32)
        indexf = m.sb("indexf", [P, TILES, 2])
        big = m.sb("big", [P, TILES])
        pair = m.sb("pair", [P, TILES, 2])
        first = m.sb("first", [P, TILES, EXPERTS])
        combine = m.sb("combine", [P, TILES, EXPERTS])
        raw1, raw2, rawb = m.sb("raw1", [P, 2, KD, FF]), m.sb("raw2", [P, 2, FT, DIM]), m.sb("rawb", [P, 2, FT])
        w1_hi, w1_lo = m.sb("w1_hi", [P, 2, KD, FF], F32R), m.sb("w1_lo", [P, 2, KD, FF], F32R)
        w2_hi, w2_lo = m.sb("w2_hi", [P, 2, FT, DIM], F32R), m.sb("w2_lo", [P, 2, FT, DIM], F32R)
        b1_sb = m.sb("b1", [P, 2, FT])
        one = m.sb("one", [P, KD])
        g = m.sb("g", [P, 2, FT, CHUNK])
        g_hi, g_lo = m.sb("g_hi", [P, 2, FT, CHUNK], F32R), m.sb("g_lo", [P, 2, FT, CHUNK], F32R)
        full = g[:, 0, :, :].rearrange("p (s k) n -> p s k n", k=KD)
        num, den = g[:, 1, 0:2, :], g[:, 1, 2:4, :]
        logitT = acc[0:EXPERTS, 0:TILES // 2, :].rearrange("p t n -> p (t n)").rearrange("p (c n) -> p c n", c=CHUNKS)
        ps_h = [m.ps(f"ps_h{n}", [P, CHUNK]) for n in range(FT)]
        ps_o = [m.ps(f"ps_o{n}", [P, 512]) for n in range(CT)]

        sums_in = [m.sem(f"sums_in{n}") for n in range(2)]
        inverted, divided, mla_made, mla_full, mla_split = (
            m.sem("inverted"), m.sem("divided"), m.sem("mla_made"), m.sem("mla_full"), m.sem("mla_split"))
        routed, logits, chain, placed, exped = (m.sem("routed"), m.sem("logits"), m.sem("chain"), m.sem("placed"),
                                                m.sem("exped"))
        raw_in = [m.sem(f"raw_in{n}") for n in range(2)]
        w_ready, hid_made, hid_out, lo_made, out_made, out_added = (m.sem("w_ready"), m.sem("hid_made"), m.sem("hid_out"),
                                                                    m.sem("lo_made"), m.sem("out_made"), m.sem("out_added"))
        b2_added, scaled, counted = m.sem("b2_added"), m.sem("scaled"), m.sem("counted")
        set_up, cleared = m.sem("set_up"), m.sem("cleared")
        LOADS = R.loads
        CHAIN = 13 + 2 * TILES
        SPLITS = 5
        W_LEAD, HID_LEAD, OUT_LEAD, ADD_LEAD = 2 * SPLITS, 2 * FT, CHUNKS * CT + 1, CT
        EPAIRS = EXPERTS // 2

        block = ctx.enter_context(nc.Block())

        def expert_pairs(eng, run):
            with eng.Fori(0, EPAIRS - 1) as i:
                run(i * 2, True)
            run(EXPERTS - 2, False)

        @block.sync
        def _(sp):
            def sums(c):
                s, b, at = c % 2, c // 2, (c % 2) * CHUNK
                sp.dma_start(den[:, s, :], aod[b * HEADS:(b + 1) * HEADS, at:at + CHUNK].unsqueeze(1)
                             .to_broadcast([HEADS, HD, CHUNK])).then_inc(sums_in[s], 16)
                sp.dma_start(num[:, s, :], aon[b * P:(b + 1) * P, at:at + CHUNK]).then_inc(sums_in[s], 16)

            def weights(e, s):
                sp.dma_start(raw1[:, s, :, :], w1[e].rearrange("(k p) f -> p k f", p=P)).then_inc(raw_in[s], 16)
                sp.dma_start(raw2[:, s, :, :], w2[e].rearrange("(k p) f -> p k f", p=P)).then_inc(raw_in[s], 16)
                sp.dma_start(rawb[:, s, :], b1[e]).then_inc(raw_in[s], 16)

            sums(0)
            sums(1)
            for e in range(2):
                weights(e, e)
            for c in range(2, CHUNKS):
                sp.wait_ge(mla_made, c - 1)
                sums(c)
            prefetch(sp)
            with sp.Fori(1, EPAIRS) as i:
                for s in range(2):
                    e = i * 2 + s
                    sp.wait_ge(w_ready, W_LEAD + (e - 1) * SPLITS)
                    weights(e, s)

        @block.gpsimd
        def _(pool):
            pool.sem_inc(w_ready, W_LEAD)
            pool.memset(one[:, :], 1.0).then_inc(set_up, 1)
            pool.wait_ge(set_up, 1)
            pool.memset(acc[:, :, :], 0.0).then_inc(set_up, 1)
            pool.wait_ge(set_up, 2)
            with pool.Fori(0, EPAIRS) as i:
                for s in range(2):
                    e = i * 2 + s
                    pool.wait_ge(raw_in[s], 48 * (i + 1))
                    pool.wait_ge(out_made, OUT_LEAD + (e - 1) * CHUNKS * CT)
                    pool.tensor_tensor(w1_hi[:, s, :, :], raw1[:, s, :, :],
                                       one[:, :].unsqueeze(2).to_broadcast([P, KD, FF]), ALU.mult).then_inc(w_ready, 1)
                    pool.tensor_copy(w2_hi[:, s, :, :], raw2[:, s, :, :]).then_inc(w_ready, 1)
                    pool.tensor_copy(b1_sb[:, s, :], rawb[:, s, :]).then_inc(w_ready, 1)
                    pool.wait_ge(w_ready, W_LEAD + e * SPLITS + 2)
                    pool.tensor_tensor(w1_lo[:, s, :, :], raw1[:, s, :, :], f32(w1_hi[:, s, :, :]),
                                       ALU.subtract).then_inc(w_ready, 1)
                    pool.tensor_tensor(w2_lo[:, s, :, :], raw2[:, s, :, :], f32(w2_hi[:, s, :, :]),
                                       ALU.subtract).then_inc(w_ready, 1)

        @block.tensor
        def _(pe):
            pe.sem_inc(out_made, OUT_LEAD)

            def project(c):
                pe.wait_ge(divided, c + 1)
                if c >= 2:
                    pe.wait_ge(mla_full, c - 1)
                for k in range(KD):
                    mm = pe.matmul(ps_h[c % 2 * KD + k][:, :], ow_sb[:, k * P:(k + 1) * P], num[:, c % 2, :],
                                   start=True, stop=True)
                mm.then_inc(mla_made, 1)

            def route(c):
                s = c % 2
                pe.wait_ge(mla_full, c + 1)
                if c >= 2:
                    pe.wait_ge(logits, c - 1)
                for k in range(KD):
                    mm = pe.matmul(ps_o[s][0:EXPERTS, :], rw_sb[:, k, :], full[:, s, k, :], start=k == 0, stop=k == KD - 1)
                mm.then_inc(routed, 1)

            pe.wait_ge(w_in, 16 * LOADS)
            project(0)
            for c in range(CHUNKS):
                if c + 1 < CHUNKS:
                    project(c + 1)
                route(c)
            pe.wait_ge(logits, CHUNKS)
            for t in range(TILES):
                mm = pe.transpose(ps_o[2][:, t * EXPERTS:(t + 1) * EXPERTS], logitT[:, t // CT, t % CT * P:(t % CT + 1) * P],
                                  ident[0:EXPERTS, 0:EXPERTS])
            mm.then_inc(routed, 1)

            def hidden(n, s, c, sg):
                for f in range(FT):
                    pe.wait_ge(hid_out, n * 2 * FT + 2 * (f + 1))
                    at = slice(c * CHUNK, (c + 1) * CHUNK)
                    for i, (w, x) in enumerate(((w1_hi, mla_hi), (w1_lo, mla_hi), (w1_hi, mla_lo))):
                        for k in range(KD):
                            mm = pe.matmul(ps_h[f][:, :], w[:, s, k, f * P:(f + 1) * P], x[:, k, at],
                                           start=i == 0 and k == 0, stop=i == 2 and k == KD - 1)
                    mm.then_inc(hid_made, 1)

            def output(n, s, sg):
                pe.wait_ge(lo_made, (n + 1) * FT)
                for t in range(CT):
                    pe.wait_ge(out_added, n * CT + t + 1)
                    for i, (x, w) in enumerate(((g_hi, w2_hi), (g_lo, w2_hi), (g_hi, w2_lo))):
                        for f in range(FT):
                            mm = pe.matmul(ps_o[t][:, 0:DIM], x[:, sg, f, t * P:(t + 1) * P], w[:, s, f, :],
                                           start=i == 0 and f == 0, stop=i == 2 and f == FT - 1)
                    mm.then_inc(out_made, 1)

            pe.wait_ge(w_ready, W_LEAD + SPLITS)
            pe.wait_ge(mla_full, CHUNKS)
            pe.wait_ge(mla_split, 1)
            hidden(0, 0, 0, 0)
            pe.wait_ge(mla_split, CHUNKS)
            pe.wait_ge(chain, 2)

            def run(e0, more):
                for j in range(2 * CHUNKS):
                    n = e0 * CHUNKS + j
                    if more or j + 1 < 2 * CHUNKS:
                        if (j + 1) % CHUNKS == 0:
                            pe.wait_ge(w_ready, W_LEAD + (e0 + (j + 1) // CHUNKS + 1) * SPLITS)
                        hidden(n + 1, (j + 1) // CHUNKS % 2, (j + 1) % CHUNKS, (j + 1) % 2)
                    output(n, j // CHUNKS, j % 2)

            expert_pairs(pe, run)

        @block.scalar
        def _(act):
            act.sem_inc(hid_out, HID_LEAD)
            act.wait_ge(w_in, 16 * LOADS)

            def mla_out(c):
                s = c % 2
                act.wait_ge(mla_made, c + 1)
                if c >= 2:
                    act.wait_ge(mla_split, c - 1)
                    act.wait_ge(routed, c - 1)
                for k in range(KD):
                    for dst in (full[:, s, k, :], mla_hi[:, k, c * CHUNK:(c + 1) * CHUNK]):
                        ins = act.activation(dst, ps_h[s * KD + k][:, :], ACT.Identity, bias=ob_sb[:, k:k + 1])
                ins.then_inc(mla_full, 1)

            mla_out(0)
            act.wait_ge(set_up, 2)
            for c in range(CHUNKS):
                if c + 1 < CHUNKS:
                    mla_out(c + 1)
                act.wait_ge(routed, c + 1)
                act.activation(logitT[:, c, :], ps_o[c % 2][0:EXPERTS, :], ACT.Identity, bias=rb_sb[:, :]).then_inc(logits, 1)
            act.wait_ge(chain, 2)
            act.activation(logit[:, :, :], logit[:, :, :], ACT.Exp).then_inc(exped, 1)
            act.activation(acc[0:EXPERTS, 0:TILES // 2, :], acc[0:EXPERTS, TILES // 2:, :], ACT.Copy).then_inc(cleared, 1)
            act.wait_ge(mla_split, CHUNKS)
            act.wait_ge(routed, CHUNKS)
            with act.Fori(0, EPAIRS) as i:
                for j in range(2 * CHUNKS):
                    n, s, sg = i * (2 * CHUNKS) + j, j // CHUNKS, j % 2
                    act.wait_ge(out_made, OUT_LEAD + (n - 1) * CT)
                    for f in range(FT):
                        act.wait_ge(hid_made, n * FT + f + 1)
                        for dst in (g, g_hi):
                            act.activation(dst[:, sg, f, :], ps_h[f][:, :], ACT.Gelu, bias=b1_sb[:, s, f:f + 1]).then_inc(hid_out, 1)

        @block.vector
        def _(dve):
            dve.sem_inc(out_added, ADD_LEAD)

            def divide(c):
                s = c % 2
                dve.wait_ge(sums_in[s], 32 * (c // 2 + 1))
                dve.reciprocal(den[:, s, :], den[:, s, :]).then_inc(inverted, 1)
                dve.wait_ge(inverted, c + 1)
                dve.tensor_tensor(num[:, s, :], num[:, s, :], den[:, s, :], ALU.mult).then_inc(divided, 1)

            divide(0)
            dve.wait_ge(w_in, 16 * LOADS)
            divide(1)
            for c in range(CHUNKS):
                s = c % 2
                at = c * CHUNK
                dve.wait_ge(mla_full, c + 1)
                dve.tensor_tensor(mla_lo[:, :, at:at + CHUNK], full[:, s, :, :], f32(mla_hi[:, :, at:at + CHUNK]),
                                  ALU.subtract).then_inc(mla_split, 1)
                if c + 2 < CHUNKS:
                    divide(c + 2)

            made = [0]

            def linked(ins):
                made[0] += 1
                ins.then_inc(chain, 1)
                dve.wait_ge(chain, made[0])

            wide = [P, TILES, EXPERTS]
            dve.wait_ge(routed, CHUNKS + 1)
            made_logits = ps_o[2][:, 0:TILES * EXPERTS].rearrange("p (t e) -> p t e", e=EXPERTS)
            linked(dve.tensor_reduce(big[:, :], made_logits, AX.X, ALU.max))
            linked(dve.tensor_tensor(logit[:, :, :], made_logits, big[:, :].unsqueeze(2).to_broadcast(wide),
                                     ALU.subtract))
            dve.wait_ge(exped, 1)
            linked(dve.tensor_reduce(big[:, :], logit[:, :, :], AX.X, ALU.add))
            linked(dve.reciprocal(big[:, :], big[:, :]))
            linked(dve.tensor_tensor(logit[:, :, :], logit[:, :, :], big[:, :].unsqueeze(2).to_broadcast(wide), ALU.mult))
            for t in range(TILES):
                dve.max(top[:, t, :], logit[:, t, :]).then_inc(chain, 1)
            made[0] += TILES
            dve.wait_ge(chain, made[0])
            for t in range(TILES):
                dve.max_index(index[:, t, :], top[:, t, :], logit[:, t, :]).then_inc(chain, 1)
            made[0] += TILES
            dve.wait_ge(chain, made[0])
            linked(dve.tensor_copy(indexf[:, :, :], index[:, :, 0:2]))
            linked(dve.tensor_tensor(big[:, :], top[:, :, 0], top[:, :, 1], ALU.add))
            linked(dve.tensor_scalar(big[:, :], big[:, :], 1e-8, None, ALU.add))
            linked(dve.reciprocal(big[:, :], big[:, :]))
            linked(dve.tensor_tensor(pair[:, :, :], top[:, :, 0:2], big[:, :].unsqueeze(2).to_broadcast([P, TILES, 2]),
                                     ALU.mult))
            for n, dst in ((0, first), (1, combine)):
                dve.tensor_tensor(dst[:, :, :], iota_sb[:, :].unsqueeze(1).to_broadcast(wide),
                                  indexf[:, :, n].unsqueeze(2).to_broadcast(wide), ALU.is_equal).then_inc(placed, 1)
                dve.wait_ge(placed, n + 1)
                linked(dve.tensor_tensor(dst[:, :, :], dst[:, :, :], pair[:, :, n].unsqueeze(2).to_broadcast(wide),
                                         ALU.mult))
            linked(dve.tensor_tensor(combine[:, :, :], combine[:, :, :], first[:, :, :], ALU.add))
            assert made[0] == CHAIN, made[0]
            dve.wait_ge(cleared, 1)

            def low(n, sg):
                for f in range(FT):
                    dve.wait_ge(hid_out, HID_LEAD + n * 2 * FT + 2 * (f + 1))
                    dve.tensor_tensor(g_lo[:, sg, f, :], g[:, sg, f, :], f32(g_hi[:, sg, f, :]), ALU.subtract).then_inc(lo_made, 1)

            def add(n, e, c, last):
                weight = [combine[:, c * CT + t, bass.ds(e, 1)] for t in range(CT)]
                for t in range(CT):
                    tile = c * CT + t
                    dve.wait_ge(out_added, n * CT + t + 1)
                    dve.scalar_tensor_tensor(out=acc[:, tile, :], in0=b2_sb[:, bass.ds(e * DIM, DIM)], scalar=weight[t],
                                             in1=acc[:, tile, :], op0=ALU.mult, op1=ALU.add).then_inc(b2_added, 1)
                for t in range(CT):
                    tile = c * CT + t
                    dve.wait_ge(b2_added, n * CT + t + 1)
                    dve.wait_ge(out_made, OUT_LEAD + n * CT + t + 1)
                    dve.scalar_tensor_tensor(out=acc[:, tile, :], in0=ps_o[t][:, 0:DIM], scalar=weight[t],
                                             in1=acc[:, tile, :], op0=ALU.mult, op1=ALU.add).then_inc(out_added, 1)
                if last:
                    for t in range(CT):
                        tile = c * CT + t
                        dve.wait_ge(out_added, ADD_LEAD + n * CT + t + 1)
                        dve.scalar_tensor_tensor(out=X[:, tile, :], in0=acc[:, tile, :], scalar=0.3, in1=X[:, tile, :],
                                                 op0=ALU.mult, op1=ALU.add).then_inc(scaled, 1)
                    for t in range(CT):
                        tile = c * CT + t
                        dve.wait_ge(scaled, tile + 1)
                        dve.bn_stats(stats[:, tile, :], X[:, tile, :]).then_inc(counted, 1)

            low(0, 0)

            def run(e0, more):
                for j in range(2 * CHUNKS):
                    n = e0 * CHUNKS + j
                    if more or j + 1 < 2 * CHUNKS:
                        low(n + 1, (j + 1) % 2)
                    add(n, e0 + j // CHUNKS, j % CHUNKS, not more and j >= CHUNKS)

            expert_pairs(dve, run)


GROUPS1 = 2


class CrossWeights:

    def __init__(self, m):
        self.ctx = m.sb("ctx", [P, 2, BATCH * CTX])
        self.wq, self.wk, self.wv, self.wo = (m.sb(n, [P, 2, DIM]) for n in ("wq", "wk", "wv", "wo"))
        self.bq, self.bk, self.bv = (m.sb(n, [P, GROUPS1]) for n in ("bq", "bk", "bv"))
        self.bo = m.sb("bo", [P, DIM])
        self.mask = m.sb("mask", [P, GH])
        self.w_in = m.sem("w_in")
        self.loads = 14

    def load(self, sp, ctxT, Wq, Wk, Wv, Wo, bq, bk, bv, bo, mask8):
        for k, (at, rows) in enumerate(((0, P), (P, C2))):
            for dst, src in ((self.ctx, ctxT), (self.wk, Wk), (self.wv, Wv)):
                sp.dma_start(dst[0:rows, k, :], src[at:at + rows, :]).then_inc(self.w_in, 16)
        for dst, src in ((self.bq, bq), (self.bk, bk), (self.bv, bv), (self.mask, mask8)):
            sp.dma_start(dst[:, :], src).then_inc(self.w_in, 16)
        for dst, src in ((self.wq, Wq), (self.wo, Wo)):
            sp.dma_start(dst[:, :, :], src.rearrange("(k p) n -> p k n", p=P)).then_inc(self.w_in, 16)
        for n in range(2):
            sp.dma_start(self.bo[64 * n:64 * (n + 1), :], bo.partition_broadcast(64)).then_inc(self.w_in, 16)


def phase_xattn1(nc, X, stats, W, F, prefetch, ident):
    with ExitStack() as ctx:
        m = Scope(nc, ctx, "xa1")
        ctx_sb, wq, wk, wv, wo, mask, w_in = W.ctx, W.wq, W.wk, W.wv, W.wo, W.mask, W.w_in
        bq_sb, bk_sb, bv_sb, bo_sb = W.bq, W.bk, W.bv, W.bo
        kblk = m.sb("kblk", [P, BATCH, GROUPS1, HJ])
        vT = m.sb("vT", [P, BATCH, GROUPS1, HJ])
        vblk = m.sb("vblk", [P, BATCH, GROUPS1, HJT, P])
        mv = m.sb("mv", [P, TILES, 2])
        root, rstd = m.sb("root", [P, TILES]), m.sb("rstd", [P, TILES])
        xn = m.sb("xn", [P, 2, DIM])
        xT = m.sb("xT", [P, 2, KD, P])
        qT = m.sb("qT", [P, 2, GROUPS1, P])
        mx, sm, rc = (m.sb(n, [P, 2, GROUPS1, GH]) for n in ("mx", "sm", "rc"))
        pr = m.sb("pr", [P, 2, GROUPS1, HJ])
        pT = m.sb("pT", [P, 2, GROUPS1, HJT, P])
        aT = m.sb("aT", [P, 2, GROUPS1, P])
        ps_x = m.ps("ps_x", [P, 512])
        ps_s = m.ps("ps_s", [P, GROUPS1, 2, 512])
        ps_p = m.ps("ps_p", [P, 2, 512])
        ps_o = m.ps("ps_o", [P, 512])

        prep_pe, prep_dve, prep_act = m.sem("prep_pe"), m.sem("prep_dve"), m.sem("prep_act")
        s_stats, s_var, s_root, s_rstd = m.sem("s_stats"), m.sem("s_var"), m.sem("s_root"), m.sem("s_rstd")
        normed, turned, xT_in, queried, qT_in = (m.sem("normed"), m.sem("turned"), m.sem("xT_in"), m.sem("queried"),
                                                 m.sem("qT_in"))
        pairs = ("scored", "maxed", "shifted", "exped", "summed", "inverted", "weighted", "pturned", "pT_in")
        scored, maxed, shifted, exped, summed, inverted, weighted, pturned, pT_in = (
            [m.sem(f"{n}{g}") for g in range(GROUPS1)] for n in pairs)
        s_next = m.sem("s_next")
        attended, aT_in, projected, biased, added = (m.sem("attended"), m.sem("aT_in"), m.sem("projected"),
                                                     m.sem("biased"), m.sem("added"))
        LOADS = W.loads
        LAG = 5

        def rows_of(i):
            return P if i < HJT - 1 else HJR

        block = ctx.enter_context(nc.Block())

        @block.sync
        def _(sp):
            prefetch(sp)

        @block.tensor
        def _(pe):
            pe.wait_ge(w_in, 16 * LOADS)
            for n, w in enumerate((wk, wv)):
                for g in range(GROUPS1):
                    for k, rows in enumerate((P, C2)):
                        mm = pe.matmul(ps_s[:, n, g, 0:BATCH * CTX], w[0:rows, k, g * P:(g + 1) * P],
                                       ctx_sb[0:rows, k, :], start=k == 0, stop=k == 1)
                    mm.then_inc(prep_pe, 1)

            def v_blocks():
                pe.wait_ge(prep_dve, 2 * BATCH * GROUPS1)
                n = 0
                for b in range(BATCH):
                    for g in range(GROUPS1):
                        if n:
                            pe.wait_ge(prep_act, n)
                        for i in range(HJT):
                            rows = rows_of(i)
                            mm = pe.transpose(ps_p[0:rows, i // 4, (i % 4) * P:(i % 4 + 1) * P],
                                              vT[:, b, g, i * P:i * P + rows], ident[:, :])
                        mm.then_inc(prep_pe, 1)
                        n += 1

            for s in (turned, queried, *scored, *pturned, attended, projected):
                pe.sem_inc(s, LEAD)

            def turn_p(t, s, g):
                pe.wait_ge(weighted[g], has(t))
                pe.wait_ge(pT_in[1 - g], one_ago(t) if g == 0 else has(t))
                for j in range(HJT):
                    rows = rows_of(j)
                    mm = pe.transpose(ps_p[0:rows, j // 4, (j % 4) * P:(j % 4 + 1) * P],
                                      pr[:, s, g, j * P:j * P + rows], ident[:, :])
                mm.then_inc(pturned[g], 1)

            def turn(i, par):
                if live(i - 3):
                    turn_p(i - 3, 1 - par, 0)
                if live(i - 1):
                    t, s = i - 1, 1 - par
                    pe.wait_ge(qT_in, has(t))
                    for g in range(GROUPS1):
                        pe.wait_ge(shifted[g], one_ago(t))
                        for half in range(2):
                            mm = pe.matmul(ps_s[:, g, half, 0:HALF], qT[:, s, g, :],
                                           kblk[:, s, g, half * HALF:(half + 1) * HALF], start=True, stop=True)
                        mm.then_inc(scored[g], 1)
                if live(i - 3):
                    turn_p(i - 3, 1 - par, 1)
                if live(i):
                    t = i
                    pe.wait_ge(normed, has(t))
                    pe.wait_ge(qT_in, one_ago(t))
                    for k in range(KD):
                        mm = pe.transpose(ps_x[:, k * P:(k + 1) * P], xn[:, par, k * P:(k + 1) * P], ident[:, :])
                    mm.then_inc(turned, 1)
                if live(i - 5):
                    t, s = i - 5, 1 - par
                    pe.wait_ge(aT_in, has(t))
                    for g in range(GROUPS1):
                        mm = pe.matmul(ps_o[:, DIM:2 * DIM], aT[:, s, g, :], wo[:, g, :], start=g == 0,
                                       stop=g == GROUPS1 - 1)
                    mm.then_inc(projected, 1)
                if live(i):
                    t = i
                    pe.wait_ge(xT_in, has(t))
                    for g in range(GROUPS1):
                        for k in range(KD):
                            mm = pe.matmul(ps_x[:, g * P:(g + 1) * P], wq[:, k, g * P:(g + 1) * P], xT[:, par, k, :],
                                           start=k == 0, stop=k == KD - 1)
                    mm.then_inc(queried, 1)
                if is_turn(i, 0):
                    v_blocks()
                if is_turn(i, 3):
                    pe.wait_ge(prep_act, BATCH * GROUPS1)
                if live(i - 4):
                    t, s = i - 4, par
                    pe.wait_ge(pT_in[1], has(t))
                    pe.wait_ge(added, one_ago(t))
                    for g in range(GROUPS1):
                        for j in range(HJT):
                            rows = rows_of(j)
                            mm = pe.matmul(ps_o[:, g * P:(g + 1) * P], vblk[0:rows, s, g, j, :],
                                           pT[0:rows, s, g, j, :], start=j == 0, stop=j == HJT - 1)
                    mm.then_inc(attended, 1)

            turns(pe, LAG, turn)

        @block.vector
        def _(dve):
            norm_stats(dve, s_root, stats, mv, root, rstd, s_stats, s_var, s_rstd, 0)
            dve.wait_ge(w_in, 16 * LOADS)

            def blocks(n, dst, bias):
                dve.wait_ge(prep_pe, 2 * (n + 1))
                for b in range(BATCH):
                    for g in range(GROUPS1):
                        dve.scalar_tensor_tensor(
                            out=dst[:, b, g, :].rearrange("p (h j) -> p h j", h=GH),
                            in0=ps_s[:, n, g, b * CTX:(b + 1) * CTX].unsqueeze(1).to_broadcast([P, GH, CTX]),
                            scalar=bias[:, g:g + 1], in1=mask[:, :].unsqueeze(2).to_broadcast([P, GH, CTX]),
                            op0=ALU.add, op1=ALU.mult).then_inc(prep_dve, 1)
            blocks(0, kblk, bk_sb)
            for s in (normed, *maxed, *shifted, *summed, *inverted, added):
                dve.sem_inc(s, LEAD)

            def turn(i, par):
                if live(i):
                    t = i
                    dve.wait_ge(turned, two_ago(t))
                    x = tile_of(t, par)
                    dve.tensor_scalar(xn[:, par, :], X[:, x, :], mv[:, x, 0:1], rstd[:, bass.ds(x, 1)],
                                      ALU.subtract, ALU.mult).then_inc(normed, 1)
                if is_turn(i, 0):
                    blocks(1, vT, bv_sb)
                if live(i - 2):
                    t, s = i - 2, par
                    for g in range(GROUPS1):
                        dve.wait_ge(exped[g], has(t))
                        dve.wait_ge(weighted[g], two_ago(t))
                        dve.tensor_reduce(sm[:, s, g, :], pr[:, s, g, :].rearrange("p (h j) -> p h j", j=CTX), AX.X,
                                          ALU.add).then_inc(summed[g], 1)
                        dve.wait_ge(summed[g], has(t))
                        dve.reciprocal(rc[:, s, g, :], sm[:, s, g, :]).then_inc(inverted[g], 1)
                for g in range(GROUPS1):
                    if live(i - 1):
                        t, s = i - 1, 1 - par
                        dve.wait_ge(scored[g], has(t))
                        src = ps_s[:, g, :, 0:HALF].rearrange("p a (h j) -> p a h j", j=CTX)
                        dve.tensor_reduce(mx[:, s, g, :].rearrange("p (a h) -> p a h", a=2), src, AX.X,
                                          ALU.max).then_inc(maxed[g], 1)
                        dve.wait_ge(maxed[g], has(t))
                        dve.wait_ge(pturned[g], two_ago(t))
                        dve.tensor_tensor(pr[:, s, g, :].rearrange("p (a h j) -> p a h j", a=2, j=CTX), src,
                                          mx[:, s, g, :].rearrange("p (a h) -> p a h", a=2).unsqueeze(3)
                                          .to_broadcast([P, 2, GH // 2, CTX]), ALU.subtract).then_inc(shifted[g], 1)
                    if g == 0 and live(i - 5):
                        t = i - 5
                        dve.wait_ge(projected, has(t))
                        dve.wait_ge(biased, has(t))
                        x = tile_of(t, 1 - par)
                        dve.tensor_tensor(X[:, x, :], ps_o[:, DIM:2 * DIM], X[:, x, :], ALU.add).then_inc(added, 1)
                if live(i - 6):
                    t = i - 6
                    dve.wait_ge(added, has(t))
                    x = tile_of(t, par)
                    dve.bn_stats(stats[:, x, :], X[:, x, :]).then_inc(s_next, 1)

            turns(dve, LAG + 1, turn)

        @block.gpsimd
        def _(pool):
            for s in (*weighted, biased):
                pool.sem_inc(s, LEAD)
            pool.wait_ge(w_in, 16 * LOADS)

            def turn(i, par):
                if live(i - 2):
                    t, s = i - 2, par
                    for g in range(GROUPS1):
                        pool.wait_ge(inverted[g], has(t))
                        v = pr[:, s, g, :].rearrange("p (h j) -> p h j", j=CTX)
                        pool.tensor_tensor(v, v, rc[:, s, g, :].unsqueeze(2).to_broadcast([P, GH, CTX]),
                                           ALU.mult).then_inc(weighted[g], 1)
                if live(i - 1):
                    t = i - 1
                    pool.wait_ge(normed, has(t))
                    x = tile_of(t, 1 - par)
                    pool.tensor_tensor(X[:, x, :], X[:, x, :], bo_sb[:, :], ALU.add).then_inc(biased, 1)

            turns(pool, LAG, turn)

        @block.scalar
        def _(act):
            act.wait_ge(s_var, 1)
            act.activation(root[:, :], root[:, :], ACT.Sqrt).then_inc(s_root, 1)

            def v_blocks():
                n = 0
                for b in range(BATCH):
                    for g in range(GROUPS1):
                        act.wait_ge(prep_pe, 5 + n)
                        act.activation(vblk[:, b, g, 0:4, :].rearrange("p k n -> p (k n)"), ps_p[:, 0, :], ACT.Copy)
                        act.activation(vblk[0:HJR, b, g, 4, :], ps_p[0:HJR, 1, 0:P], ACT.Copy).then_inc(prep_act, 1)
                        n += 1

            for s in (xT_in, qT_in, *exped, *pT_in, aT_in):
                act.sem_inc(s, LEAD)

            def copy_p(t, s, g):
                act.wait_ge(pturned[g], has(t))
                act.wait_ge(attended, two_ago(t))
                act.activation(pT[:, s, g, 0:4, :].rearrange("p k n -> p (k n)"), ps_p[:, 0, :], ACT.Copy)
                act.activation(pT[0:HJR, s, g, 4, :], ps_p[0:HJR, 1, 0:P], ACT.Copy).then_inc(pT_in[g], 1)

            def exps(t, s, g):
                act.wait_ge(shifted[g], has(t))
                act.activation(pr[:, s, g, :], pr[:, s, g, :], ACT.Exp, scale=0.25).then_inc(exped[g], 1)

            def turn(i, par):
                for n in range(2):
                    if is_turn(i, TILES + 2 + n):
                        F.add_up(act, n)
                if live(i - 5):
                    t, s = i - 5, 1 - par
                    act.wait_ge(attended, has(t))
                    act.wait_ge(projected, two_ago(t))
                    act.activation(aT[:, s, :, :].rearrange("p k n -> p (k n)"), ps_o[:, 0:DIM], ACT.Copy).then_inc(aT_in, 1)
                if live(i - 3):
                    copy_p(i - 3, 1 - par, 0)
                if live(i - 3):
                    copy_p(i - 3, 1 - par, 1)
                if live(i):
                    t = i
                    act.wait_ge(turned, has(t))
                    act.wait_ge(queried, two_ago(t))
                    act.activation(xT[:, par, :, :].rearrange("p k n -> p (k n)"), ps_x[:, 0:DIM],
                                   ACT.Copy).then_inc(xT_in, 1)
                if live(i - 1):
                    exps(i - 1, 1 - par, 0)
                if live(i - 1):
                    exps(i - 1, 1 - par, 1)
                if live(i):
                    t = i
                    act.wait_ge(queried, has(t))
                    act.wait_ge(scored[1], two_ago(t))
                    act.activation(qT[:, par, 0, :], ps_x[:, 0:P], ACT.Identity, bias=bq_sb[:, 0:1])
                    act.activation(qT[:, par, 1, :], ps_x[:, P:2 * P], ACT.Identity, bias=bq_sb[:, 1:2]).then_inc(qT_in, 1)
                if is_turn(i, 0):
                    v_blocks()

            turns(act, LAG, turn)


HID = 1024
KH = HID // P
POOL_B1 = 640
POOL_LN = 768
ROUND = 12582912.0


class FfnWeights:

    def __init__(self, m):
        self.raw = m.sb("raw", [P, 2, 2048])
        self.b1, self.g2, self.n2 = m.sb("b1", [P, HID]), m.sb("g2", [P, HID]), m.sb("n2", [P, HID])
        self.b2, self.g1, self.n1 = m.sb("b2", [P, DIM]), m.sb("g1", [P, DIM]), m.sb("n1", [P, DIM])
        self.absolute = m.sb("absolute", [P, 2048])
        self.sums = m.sb("sums", [P, 2])
        self.w_in, self.v_in, self.w_abs = m.sem("w_in"), m.sem("v_in"), m.sem("w_abs")
        self.vloads = 12

    def add_up(self, act, n):
        act.wait_ge(self.w_in, 32)
        if n:
            act.wait_ge(self.w_abs, n)
        act.activation(self.absolute[:, :], self.raw[:, n, :], ACT.Abs, accum_out=self.sums[:, n:n + 1]).then_inc(self.w_abs, 1)

    def load(self, sp, w1T, w2T, b1, b2, g1, n1, g2, n2):
        for n, (src, k) in enumerate(((w1T, KD), (w2T, KH))):
            sp.dma_start(self.raw[:, n, :].rearrange("p (k n) -> p k n", k=k),
                         src.rearrange("(k p) n -> p k n", p=P)).then_inc(self.w_in, 16)
        for dst, src in ((self.g1, g1), (self.n1, n1), (self.b1, b1), (self.g2, g2), (self.n2, n2), (self.b2, b2)):
            for n in range(2):
                sp.dma_start(dst[64 * n:64 * (n + 1), :], src.partition_broadcast(64)).then_inc(self.v_in, 16)


def phase_ffn(nc, X, stats, W, ident, identb, out):
    with ExitStack() as ctx:
        m = Scope(nc, ctx, "ffn")
        raw, v_in = W.raw, W.v_in
        b1_sb, g2_sb, n2_sb, b2_sb, g1_sb, n1_sb = W.b1, W.g2, W.n2, W.b2, W.g1, W.n1
        wq = m.sb("wq", [P, 2, 2048], BF16)
        w1q = wq[:, 0, :].rearrange("p (k n) -> p k n", k=KD)
        w2q = wq[:, 1, :].rearrange("p (k n) -> p k n", k=KH)
        ones = m.sb("ones", [P, P])
        wsum, w_abs = W.sums, W.w_abs
        wmean, winv, wfac = m.sb("wmean", [P, 2]), m.sb("winv", [P, 2]), m.sb("wfac", [P, 2])
        mv = m.sb("mv", [P, TILES, 2])
        root, rstd = m.sb("root", [P, TILES]), m.sb("rstd", [P, TILES])
        stats2, mv2 = m.sb("stats2", [P, TILES, 12]), m.sb("mv2", [P, TILES, 2])
        root2, rstd2 = m.sb("root2", [P, TILES]), m.sb("rstd2", [P, TILES])
        G = m.sb("G", [P, TILES, HID])
        nmr, nmr2 = m.sb("nmr", [P, TILES]), m.sb("nmr2", [P, TILES])
        z = m.sb("z", [P, 2, HID])
        h = m.sb("h", [P, 2, HID])
        q = m.sb("q", [P, 2, HID], BF16)
        qT = m.sb("qT", [P, 2, HID], BF16)
        y = m.sb("y", [P, 2, HID])
        amax, ainv, fac = m.sb("amax", [P, TILES]), m.sb("ainv", [P, TILES]), m.sb("fac", [P, TILES])
        ps_t = m.ps("ps_t", [P, 2, 1024], BF16)
        ps_y = m.ps("ps_y", [P, 2, HID])
        ps_w = m.ps("ps_w", [P, 512])

        ones_set, w_sum, w_chain, w_rounded = m.sem("ones_set"), m.sem("w_sum"), m.sem("w_chain"), m.sem("w_rounded")
        s_stats, s_var, s_root, s_rstd = m.sem("s_stats"), m.sem("s_var"), m.sem("s_root"), m.sem("s_rstd")
        s_stats2, s_var2, s_root2, s_rstd2 = m.sem("s_stats2"), m.sem("s_var2"), m.sem("s_root2"), m.sem("s_rstd2")
        s_nmr = m.sem("s_nmr")
        names = ("centred", "gained", "quant", "scaled", "rounded", "turned", "qT_in", "made", "used")
        first = {n: m.sem(f"first_{n}") for n in names + ("gelued", "y_full", "y_rest")}
        second = {n: m.sem(f"second_{n}") for n in names}
        biased, stored, rest_ln = m.sem("biased"), m.sem("stored"), m.sem("rest_ln")
        LAG = 4
        VLOADS = W.vloads

        block = ctx.enter_context(nc.Block())

        @block.sync
        def _(sp):
            for t in range(0, TILES, 4):
                sp.wait_ge(second["used"], LEAD + t + 4)
                sp.dma_start(out[t * P:(t + 4) * P, :].rearrange("(t p) d -> p t d", p=P), X[:, t:t + 4, :]).then_inc(stored, 16)
            sp.wait_ge(stored, 16 * TILES // 4)

        @block.gpsimd
        def _(pool):
            pool.memset(ones[:, :], 1.0).then_inc(ones_set, 1)
            for sems in (first, second):
                for n in ("gained", "quant"):
                    pool.sem_inc(sems[n], LEAD)
            pool.sem_inc(first["y_full"], LEAD)
            pool.wait_ge(v_in, 16 * VLOADS)

            def layer(sems, width, gain, shift, bias):
                def turn(i, par):
                    if live(i):
                        t, zs = i, z[:, par, 0:width]
                        pool.wait_ge(sems["centred"], has(t))
                        pool.tensor_tensor(zs, zs, gain[:, 0:width], ALU.mult).then_inc(sems["gained"], 1)
                        pool.wait_ge(sems["gained"], has(t))
                        pool.wait_ge(sems["rounded"], two_ago(t))
                        pool.tensor_tensor(h[:, par, 0:width], zs, shift[:, 0:width], ALU.add).then_inc(sems["quant"], 1)
                    if bias and live(i - 4):
                        t = i - 4
                        pool.wait_ge(first["used"], has(t))
                        ys = y[:, par, 0:POOL_B1]
                        pool.tensor_tensor(ys, ys, b1_sb[:, 0:POOL_B1], ALU.add).then_inc(first["y_full"], 1)

                turns(pool, 4 if bias else 0, turn)

            layer(first, DIM, g1_sb, n1_sb, True)
            layer(second, POOL_LN, g2_sb, n2_sb, False)

        @block.tensor
        def _(pe):
            pe.wait_ge(ones_set, 1)
            pe.wait_ge(w_abs, 2)
            pe.matmul(ps_w[:, 0:2], ones[:, :], wsum[:, :], start=True, stop=True).then_inc(w_sum, 1)
            for sems in (first, second):
                for n in ("turned", "made"):
                    pe.sem_inc(sems[n], LEAD)
            pe.wait_ge(w_rounded, 1)

            def layer(sems, kin, width, w):
                def turn(i, par):
                    if live(i - 3):
                        t, s = i - 3, 1 - par
                        pe.wait_ge(sems["rounded"], has(t))
                        pe.wait_ge(sems["qT_in"], two_ago(t))
                        for k in range(kin):
                            mm = pe.transpose(ps_t[:, s, k * P:(k + 1) * P], q[:, s, k * P:(k + 1) * P], identb[:, :])
                        mm.then_inc(sems["turned"], 1)
                    if live(i - 4):
                        t, s = i - 4, par
                        pe.wait_ge(sems["qT_in"], has(t))
                        pe.wait_ge(sems["used"], two_ago(t))
                        for half in range((width + 511) // 512):
                            n = min(512, width)
                            for k in range(kin):
                                mm = pe.matmul(ps_y[:, s, half * n:(half + 1) * n], qT[:, s, k * P:(k + 1) * P],
                                               w[:, k, half * n:(half + 1) * n], start=k == 0, stop=k == kin - 1)
                        mm.then_inc(sems["made"], 1)

                turns(pe, LAG, turn)

            layer(first, KD, HID, w1q)
            pe.wait_ge(w_rounded, 2)
            layer(second, KH, DIM, w2q)

        @block.vector
        def _(dve):
            def less_mean(neg, mean, rst):
                dve.scalar_tensor_tensor(out=neg[:, :], in0=mean[:, :, 0], scalar=-1.0, in1=rst[:, :], op0=ALU.mult,
                                         op1=ALU.mult).then_inc(s_nmr, 1)

            def round_weight(n):
                dve.tensor_scalar(raw[:, n, :], raw[:, n, :], winv[:, n:n + 1], ROUND, ALU.mult, ALU.add).then_inc(w_chain, 1)
                dve.wait_ge(w_chain, 4 + 2 * n)
                dve.tensor_scalar(raw[:, n, :], raw[:, n, :], ROUND, 1.0, ALU.subtract, ALU.min).then_inc(w_chain, 1)
                dve.wait_ge(w_chain, 5 + 2 * n)
                dve.tensor_scalar(wq[:, n, :], raw[:, n, :], -1.0, None, ALU.max).then_inc(w_rounded, 1)

            norm_stats(dve, s_root, stats, mv, root, rstd, s_stats, s_var, s_rstd, 0)
            less_mean(nmr, mv, rstd)
            dve.wait_ge(w_sum, 1)
            dve.tensor_scalar(wmean[:, :], ps_w[:, 0:2], 1.0 / (DIM * HID), 1e-5, ALU.mult, ALU.max).then_inc(w_chain, 1)
            dve.wait_ge(w_chain, 1)
            dve.reciprocal(winv[:, :], wmean[:, :]).then_inc(w_chain, 1)
            dve.tensor_scalar(wfac[:, :], wmean[:, :], 1.0 / 127.0, None, ALU.mult).then_inc(w_chain, 1)
            dve.wait_ge(w_chain, 3)
            round_weight(0)
            for sems in (first, second):
                dve.sem_inc(sems["scaled"], LEAD)
            for s in (second["used"], first["y_rest"], rest_ln):
                dve.sem_inc(s, LEAD)
            dve.wait_ge(v_in, 16 * VLOADS)

            def quantise(sems, t, s, width, wn, others):
                go = live(t)
                col = bass.ds(t, 1) if go else None
                hs = h[:, s, 0:width]
                if go:
                    dve.wait_ge(sems["quant"], has(t))
                    dve.tensor_reduce(amax[:, col], hs, AX.X, ALU.max, apply_absolute_value=True).then_inc(sems["scaled"], 1)
                others[0]()
                if go:
                    dve.wait_ge(sems["scaled"], LEAD + 6 * t + 1)
                    dve.tensor_scalar(amax[:, col], amax[:, col], 1e-5, None, ALU.max).then_inc(sems["scaled"], 1)
                others[1]()
                if go:
                    dve.wait_ge(sems["scaled"], LEAD + 6 * t + 2)
                    dve.reciprocal(ainv[:, col], amax[:, col]).then_inc(sems["scaled"], 1)
                    dve.tensor_scalar(fac[:, col], amax[:, col], wfac[:, wn:wn + 1], None, ALU.mult).then_inc(sems["scaled"], 1)
                others[2]()
                if go:
                    dve.wait_ge(sems["scaled"], LEAD + 6 * t + 4)
                    dve.tensor_scalar(hs, hs, ainv[:, col], 127.0, ALU.mult, ALU.mult).then_inc(sems["scaled"], 1)
                others[3]()
                if go:
                    dve.wait_ge(sems["scaled"], LEAD + 6 * t + 5)
                    dve.tensor_scalar(hs, hs, 127.0, ROUND, ALU.min, ALU.add).then_inc(sems["scaled"], 1)

            def turn1(i, par):
                def residual():
                    if live(i - 1):
                        t = i - 1
                        dve.tensor_tensor(X[:, t, :], X[:, t, :], b2_sb[:, :], ALU.add).then_inc(biased, 1)

                def statistics(n):
                    if live(i - 6):
                        t = i - 6
                        dve.wait_ge(first["gelued"], has(t))
                        dve.bn_stats(stats2[:, t, 6 * n:6 * n + 6], G[:, t, n * 512:(n + 1) * 512]).then_inc(s_stats2, 1)

                def bias():
                    if live(i - 4):
                        t, ys = i - 4, y[:, par, POOL_B1:HID]
                        dve.wait_ge(first["used"], has(t))
                        dve.tensor_tensor(ys, ys, b1_sb[:, POOL_B1:HID], ALU.add).then_inc(first["y_rest"], 1)

                quantise(first, i - 1, 1 - par, DIM, 0, (residual, lambda: statistics(0), lambda: statistics(1), bias))

            turns(dve, 6, turn1)
            dve.wait_ge(s_stats2, 2 * TILES)
            for t in range(TILES):
                dve.bn_aggr(mv2[:, t, :], stats2[:, t, :]).then_inc(s_stats2, 1)
            dve.wait_ge(s_stats2, 3 * TILES)
            dve.tensor_scalar(root2[:, :], mv2[:, :, 1], EPS, None, ALU.add).then_inc(s_var2, 1)
            dve.wait_ge(s_root2, 1)
            dve.reciprocal(rstd2[:, :], root2[:, :]).then_inc(s_rstd2, 1)
            dve.wait_ge(s_rstd2, 1)
            less_mean(nmr2, mv2, rstd2)
            round_weight(1)
            dve.wait_ge(biased, TILES)

            def turn2(i, par):
                zs = z[:, par, POOL_LN:HID]

                def gain():
                    if live(i):
                        dve.wait_ge(second["centred"], has(i))
                        dve.tensor_tensor(zs, zs, g2_sb[:, POOL_LN:HID], ALU.mult).then_inc(rest_ln, 1)

                def shift():
                    if live(i):
                        dve.wait_ge(rest_ln, LEAD + 2 * i + 1)
                        dve.wait_ge(second["rounded"], two_ago(i))
                        dve.tensor_tensor(h[:, par, POOL_LN:HID], zs, n2_sb[:, POOL_LN:HID], ALU.add).then_inc(rest_ln, 1)

                def result():
                    if live(i - 5):
                        t, s = i - 5, 1 - par
                        dve.wait_ge(second["made"], has(t))
                        dve.scalar_tensor_tensor(out=X[:, t, :], in0=ps_y[:, s, 0:DIM], scalar=fac[:, bass.ds(t, 1)],
                                                 in1=X[:, t, :], op0=ALU.mult, op1=ALU.add).then_inc(second["used"], 1)

                if live(i - 1):
                    dve.wait_ge(rest_ln, LEAD + 2 * (i - 1) + 2)
                quantise(second, i - 1, 1 - par, HID, 1, (gain, result, shift, lambda: None))

            turns(dve, 5, turn2)

        @block.scalar
        def _(act):
            act.wait_ge(s_var, 1)
            act.activation(root[:, :], root[:, :], ACT.Sqrt).then_inc(s_root, 1)
            for sems in (first, second):
                for n in ("centred", "rounded", "qT_in"):
                    act.sem_inc(sems[n], LEAD)
            for n in ("used", "gelued"):
                act.sem_inc(first[n], LEAD)

            def layer(sems, width, x, rst, neg, gelu):
                def turn(i, par):
                    if live(i):
                        t, s = i, par
                        act.wait_ge(sems["quant"], two_ago(t))
                        if width > POOL_LN:
                            act.wait_ge(rest_ln, LEAD + 2 * (t - 2) + 2)
                        act.activation(z[:, s, 0:width], x[:, t, :], ACT.Identity, bias=neg[:, bass.ds(t, 1)],
                                       scale=rst[:, bass.ds(t, 1)]).then_inc(sems["centred"], 1)
                    if live(i - 2):
                        t, s = i - 2, par
                        act.wait_ge(sems["scaled"], LEAD + 6 * t + 6)
                        act.wait_ge(sems["turned"], two_ago(t))
                        act.activation(q[:, s, 0:width], h[:, s, 0:width], ACT.Copy, bias=-ROUND).then_inc(sems["rounded"], 1)
                    if live(i - 3):
                        t, s = i - 3, 1 - par
                        act.wait_ge(sems["turned"], has(t))
                        act.wait_ge(sems["made"], two_ago(t))
                        act.activation(qT[:, s, 0:width], ps_t[:, s, 0:width], ACT.Copy).then_inc(sems["qT_in"], 1)
                    if gelu and live(i - 4):
                        t, s = i - 4, par
                        act.wait_ge(sems["made"], has(t))
                        act.wait_ge(sems["gelued"], two_ago(t))
                        act.activation(y[:, s, :], ps_y[:, s, :], ACT.Identity, scale=fac[:, bass.ds(t, 1)]).then_inc(sems["used"], 1)
                    if gelu and live(i - 5):
                        t, s = i - 5, 1 - par
                        act.wait_ge(sems["y_full"], has(t))
                        act.wait_ge(sems["y_rest"], has(t))
                        act.activation(G[:, t, :], y[:, s, :], ACT.Gelu).then_inc(sems["gelued"], 1)

                turns(act, 5 if gelu else 3, turn)

            act.wait_ge(s_nmr, 1)
            layer(first, DIM, X, rstd, nmr, True)
            act.wait_ge(s_var2, 1)
            act.activation(root2[:, :], root2[:, :], ACT.Sqrt).then_inc(s_root2, 1)
            act.wait_ge(s_nmr, 2)
            layer(second, HID, G, rstd2, nmr2, False)


def program(nc, a, out):
    with ExitStack() as ctx:
        X = ctx.enter_context(nc.sbuf_tensor("X", [P, TILES, DIM], F32))
        stats = ctx.enter_context(nc.sbuf_tensor("stats", [P, TILES, 6], F32))
        ident = ctx.enter_context(nc.sbuf_tensor("ident", [P, P], F32))
        identb = ctx.enter_context(nc.sbuf_tensor("identb", [P, P], BF16))
        x_loaded = ctx.enter_context(nc.semaphore("x_loaded"))
        qkd = nc.dram_tensor("qk_parts", (2, PARTS, BATCH * P, SEQ), BF16).ap()
        aon = nc.dram_tensor("attn_sums", (BATCH * P, SEQ), F32).ap()
        aod = nc.dram_tensor("attn_weights", (BATCH * HEADS, SEQ), F32).ap()
        with ExitStack() as last:
            R, C = RouterWeights(Scope(nc, last, "rw")), CrossWeights(Scope(nc, last, "xaw"))
            with ExitStack() as attn:
                W, B = QkvWeights(Scope(nc, attn, "qkvw")), AttentionBuffers(Scope(nc, attn, "attn"))
                phase_xattn0(nc, X, stats,
                             lambda sp: W.load(sp, a["Wq"], a["Wk"], a["Wv"], a["qb"], a["kb"], a["vb"]),
                             B.set_up, ident, x_loaded, a["x"], a["ctxT"], a["WqT0"], a["Wk0"], a["Wv0"], a["Wo0"],
                             a["bo0"], a["mask2"], a["ident"])
                phase_qkv(nc, X, stats, W, ident, identb, B, qkd)
                phase_attention(nc, lambda sp: R.load(sp, a["ow"], a["ob"], a["rw"], a["rb"], a["b2"], a["iota"]),
                                ident, identb, B, qkd, aon, aod)
            phase_moe(nc, X, stats, R,
                      lambda sp: C.load(sp, a["ctxT"], a["Wq1"], a["Wk1"], a["Wv1"], a["Wo1"], a["bq1"], a["bk1"],
                                        a["bv1"], a["bo1"], a["mask8"]),
                      ident, aon, aod, a["w1"], a["b1"], a["w2"])
            F = FfnWeights(Scope(nc, last, "ffnw"))
            phase_xattn1(nc, X, stats, C, F,
                         lambda sp: F.load(sp, a["f1T"], a["f2T"], a["fb1"], a["fb2"], a["g1"], a["n1"], a["g2"], a["n2"]),
                         ident)
            phase_ffn(nc, X, stats, F, ident, identb, out)


def layout(inputs):
    g = {k: np.asarray(v) for k, v in inputs.items()}
    c = np.ascontiguousarray
    kv1 = g["L1_xattn_Wkv"].reshape(16, 2, 16, CDIM)
    bkv1 = g["L1_xattn_bkv"].reshape(16, 2, 16)

    def by_dimension(w):
        return w.reshape(-1, HEADS // GROUP, GROUP, HD).transpose(0, 1, 3, 2).reshape(-1, P)

    a = {
        "x": c(g["x"].reshape(-1, DIM)),
        "ctxT": c(g["ctx_768"].reshape(-1, CDIM).T),
        "WqT0": c(g["L0_xattn_Wq"].T), "Wk0": g["L0_xattn_Wk"], "Wv0": g["L0_xattn_Wv"],
        "Wo0": g["L0_xattn_Wo"], "bo0": g["L0_xattn_bo"],
        "ident": np.eye(P, dtype=np.float32),
        "Wq": by_dimension(g["L0_ffn_q_w"].reshape(DIM, HEADS, 2 * HD)[:, :, :HD]),
        "qb": by_dimension(g["L0_ffn_q_b"].reshape(1, HEADS, 2 * HD)[:, :, :HD]).T,
        "Wk": by_dimension(g["L0_ffn_k_w"]), "kb": by_dimension(g["L0_ffn_k_b"]).T,
        "Wv": g["L0_ffn_v_w"], "vb": g["L0_ffn_v_b"],
        "ow": g["L0_ffn_o_w"][:P], "ob": g["L0_ffn_o_b"].reshape(KD, P).T,
        "rw": g["L0_ffn_router_w"], "rb": g["L0_ffn_router_b"].reshape(EXPERTS, 1), "b2": g["L0_ffn_b2"].reshape(-1),
        "iota": np.tile(np.arange(EXPERTS, dtype=np.float32), (P, 1)),
        "w1": g["L0_ffn_w1"], "w2": g["L0_ffn_w2"], "b1": g["L0_ffn_b1"].reshape(EXPERTS, FT, P).transpose(0, 2, 1),
        "Wq1": g["L1_xattn_Wq"].T, "Wo1": g["L1_xattn_Wo"].T,
        "Wk1": kv1[:, 0].reshape(DIM, CDIM).T, "Wv1": kv1[:, 1].reshape(DIM, CDIM).T,
        "bq1": g["L1_xattn_bq"].reshape(GROUPS1, P).T, "bo1": g["L1_xattn_bo"],
        "bk1": bkv1[:, 0].reshape(GROUPS1, P).T, "bv1": bkv1[:, 1].reshape(GROUPS1, P).T,
        "f1T": g["L1_ffn_w1"].T, "f2T": g["L1_ffn_w2"].T, "fb1": g["L1_ffn_b1"], "fb2": g["L1_ffn_b2"],
        "g1": g["L1_ffn_ln1_g"], "n1": g["L1_ffn_ln1_b"], "g2": g["L1_ffn_ln2_g"], "n2": g["L1_ffn_ln2_b"],
        "mask8": np.repeat(np.eye(GH, dtype=np.float32), P // GH, axis=0),
        "mask2": np.repeat(np.eye(2, dtype=np.float32), 64, axis=0),
    }
    return {k: c(v) for k, v in a.items()}


def kernel(**inputs):
    import concourse.bacc as bacc
    from concourse.bass_utils import run_bass_kernel_spmd

    nc = bacc.Bacc("TRN2", target_bir_lowering=False, num_devices=1)
    arrays = layout(inputs)
    a = {k: nc.dram_tensor(k + "_dram", v.shape, mybir.dt.from_np(v.dtype), kind="ExternalInput").ap()
         for k, v in arrays.items()}
    out = nc.dram_tensor("out_dram", (BATCH * SEQ, DIM), F32, kind="ExternalOutput").ap()
    program(nc, a, out)
    r = run_bass_kernel_spmd(nc, [{k + "_dram": v for k, v in arrays.items()}], core_ids=[0])
    return r.results[0]["out_dram"].reshape(BATCH, SEQ, DIM)
```
